# Optimizing a Trainium2 kernel written in Bass

```python
import numpy as np
import jax
import jax.numpy as jnp

def _softmax(x, axis=-1):
    return jax.nn.softmax(x, axis=axis)

def _gelu(x):
    return jax.nn.gelu(x, approximate=True)

def _silu(x):
    return jax.nn.silu(x)

def _sigmoid(x):
    return jax.nn.sigmoid(x)

def _layernorm(x, axis=-1, eps=1e-05):
    m = jnp.mean(x, axis=axis, keepdims=True)
    v = jnp.var(x, axis=axis, keepdims=True)
    return (x - m) / jnp.sqrt(v + eps)

def _scatter_add(tgt, idx, src, axis=0):
    return tgt.at[idx].add(src)

def _segment_sum(src, seg, n):
    return jax.ops.segment_sum(src, seg, n)
kernel_name = 'mk_decoder_preln_d1_seqx_r8_a7ff29'

def setup_inputs(seed: int=0):
    np.random.seed(seed)
    _w = jnp.asarray

    def _rec_inputs():
        import jax
        import jax.numpy as jnp
        _rk = jax.random.key(seed)
        x = -9.806e-05 + 1 * jax.random.normal(jax.random.fold_in(_rk, 1), (2, 512, 128), jnp.float32)
        _lenS = 512 - jax.random.randint(jax.random.fold_in(_rk, 7), (2,), 0, max(1, 512 // 4) + 1, jnp.int32)
        _lenS2 = 32 - jax.random.randint(jax.random.fold_in(_rk, 8), (2,), 0, max(1, 32 // 4) + 1, jnp.int32)
        _ctx_1024P = jax.random.normal(jax.random.fold_in(_rk, 11), (2, 16, 128), jnp.float32)
        _ctx_1024c = jax.random.dirichlet(jax.random.fold_in(_rk, 511), 0.3 * jnp.ones((16,), jnp.float32), (2, 32))
        _ctx_1024t = jnp.einsum('bsk,bkd->bsd', _ctx_1024c, _ctx_1024P)
        _ctx_1024t = _ctx_1024t * jax.lax.rsqrt(jnp.mean(jnp.square(_ctx_1024t)) + 1e-12) * 0.953939
        ctx_1024 = -1.52775e-05 + 0.999936 * (_ctx_1024t + 0.3 * jax.random.normal(jax.random.fold_in(_rk, 611), (2, 32, 128), jnp.float32))
        return (x, ctx_1024)
    x, ctx_1024 = _rec_inputs()

    def _L0_attn_setup():
        import jax, jax.numpy as jnp
        import numpy as np
        H = 16
        TOPK_RATIO = 0.05
        LN_EPS = 1e-05

        def _layernorm(t, gamma, beta):
            mu = t.mean(-1, keepdims=True)
            var = t.var(-1, keepdims=True)
            return (t - mu) * jax.lax.rsqrt(var + LN_EPS) * gamma + beta
        key = jax.random.key(seed)
        ks = jax.random.split(key, 4)
        B, N, C = (2, 256, 128)
        x = jax.random.normal(ks[0], (B, N, C), dtype=jnp.float32)
        Wqkv = jax.random.normal(ks[1], (3 * C, C), dtype=jnp.float32) * (1.0 / np.sqrt(C))
        Wproj = jax.random.normal(ks[2], (C, C), dtype=jnp.float32) * (1.0 / np.sqrt(C))
        return {'x': x, 'Wqkv': Wqkv, 'bqkv': jnp.zeros((3 * C,), jnp.float32), 'q_gamma': jnp.ones((C // H,), jnp.float32), 'q_beta': jnp.zeros((C // H,), jnp.float32), 'k_gamma': jnp.ones((C // H,), jnp.float32), 'k_beta': jnp.zeros((C // H,), jnp.float32), 'alpha': jnp.full((H,), 0.5, jnp.float32), 'Wproj': Wproj, 'bproj': jnp.zeros((C,), jnp.float32)}
    _L0_attn_all = _L0_attn_setup()
    _L0_attn_in = {k: v for k, v in _L0_attn_all.items() if k in ('Wqkv', 'bqkv', 'q_gamma', 'q_beta', 'k_gamma', 'k_beta', 'alpha', 'Wproj', 'bproj')}
    del _L0_attn_all

    def _L0_xattn_setup():
        import jax, jax.numpy as jnp
        import numpy as np
        D = 128
        NUM_ITERS = 3
        EPS = 1e-06
        SCALE = D ** (-0.5)

        def rmsnorm(x, w, eps=EPS):
            return x * jax.lax.rsqrt(jnp.mean(x * x, axis=-1, keepdims=True) + eps) * w

        def gru_cell(x, h, wih, whh, bih, bhh):
            gx = x @ wih.T + bih
            gh = h @ whh.T + bhh
            xr, xz, xn = jnp.split(gx, 3, axis=-1)
            hr, hz, hn = jnp.split(gh, 3, axis=-1)
            r = jax.nn.sigmoid(xr + hr)
            z = jax.nn.sigmoid(xz + hz)
            n = jnp.tanh(xn + r * hn)
            return (1.0 - z) * n + z * h
        key = jax.random.key(seed)
        ks = jax.random.split(key, 8)
        B, K, M, d = (8, 64, 512, D)
        w_std = d ** (-0.5)
        return {'slots': jax.random.normal(ks[0], (B, K, d), jnp.float32), 'P': jax.random.normal(ks[1], (B, M, d), jnp.float32), 'Wq': jax.random.normal(ks[2], (d, d), jnp.float32) * w_std, 'Wk': jax.random.normal(ks[3], (d, d), jnp.float32) * w_std, 'Wv': jax.random.normal(ks[4], (d, d), jnp.float32) * w_std, 'gru_wih': jax.random.normal(ks[5], (3 * d, d), jnp.float32) * w_std, 'gru_whh': jax.random.normal(ks[6], (3 * d, d), jnp.float32) * w_std, 'gru_bih': jnp.zeros((3 * d,), jnp.float32), 'gru_bhh': jnp.zeros((3 * d,), jnp.float32), 'slot_norm_w': jnp.ones((d,), jnp.float32), 'input_norm_w': jnp.ones((d,), jnp.float32)}
    _L0_xattn_all = _L0_xattn_setup()
    _L0_xattn_in = {k: v for k, v in _L0_xattn_all.items() if k in ('Wq', 'Wk', 'Wv', 'gru_wih', 'gru_whh', 'gru_bih', 'gru_bhh', 'slot_norm_w', 'input_norm_w')}
    del _L0_xattn_all

    def _L0_ffn_setup():
        import jax, jax.numpy as jnp
        import numpy as np
        E, K, H, F, R = (8, 2, 128, 256, 64)
        B, S = (2, 256)
        key = jax.random.key(seed)
        k0, k1, k2, k3, k4 = jax.random.split(key, 5)
        return {'hidden_states': jax.random.normal(k0, (B, S, H), dtype=jnp.float32), 'W_A': jax.random.normal(k1, (E, R, H), dtype=jnp.float32) * 0.02, 'W_B': jax.random.normal(k2, (E, F, R), dtype=jnp.float32) * 0.02, 'W_up': jax.random.normal(k3, (E, F, H), dtype=jnp.float32) * 0.02, 'W_down': jax.random.normal(k4, (E, H, F), dtype=jnp.float32) * 0.02}
    _L0_ffn_all = _L0_ffn_setup()
    _L0_ffn_in = {k: v for k, v in _L0_ffn_all.items() if k in ('W_A', 'W_B', 'W_up', 'W_down')}
    del _L0_ffn_all
    return {'x': x, 'ctx_1024': ctx_1024, 'L0_attn_Wqkv': _L0_attn_in['Wqkv'], 'L0_attn_bqkv': _L0_attn_in['bqkv'], 'L0_attn_q_gamma': _L0_attn_in['q_gamma'], 'L0_attn_q_beta': _L0_attn_in['q_beta'], 'L0_attn_k_gamma': _L0_attn_in['k_gamma'], 'L0_attn_k_beta': _L0_attn_in['k_beta'], 'L0_attn_alpha': _L0_attn_in['alpha'], 'L0_attn_Wproj': _L0_attn_in['Wproj'], 'L0_attn_bproj': _L0_attn_in['bproj'], 'L0_xattn_Wq': _L0_xattn_in['Wq'], 'L0_xattn_Wk': _L0_xattn_in['Wk'], 'L0_xattn_Wv': _L0_xattn_in['Wv'], 'L0_xattn_gru_wih': _L0_xattn_in['gru_wih'], 'L0_xattn_gru_whh': _L0_xattn_in['gru_whh'], 'L0_xattn_gru_bih': _L0_xattn_in['gru_bih'], 'L0_xattn_gru_bhh': _L0_xattn_in['gru_bhh'], 'L0_xattn_slot_norm_w': _L0_xattn_in['slot_norm_w'], 'L0_xattn_input_norm_w': _L0_xattn_in['input_norm_w'], 'L0_ffn_W_A': _L0_ffn_in['W_A'], 'L0_ffn_W_B': _L0_ffn_in['W_B'], 'L0_ffn_W_up': _L0_ffn_in['W_up'], 'L0_ffn_W_down': _L0_ffn_in['W_down']}

def reference(x, ctx_1024, L0_attn_Wqkv, L0_attn_bqkv, L0_attn_q_gamma, L0_attn_q_beta, L0_attn_k_gamma, L0_attn_k_beta, L0_attn_alpha, L0_attn_Wproj, L0_attn_bproj, L0_xattn_Wq, L0_xattn_Wk, L0_xattn_Wv, L0_xattn_gru_wih, L0_xattn_gru_whh, L0_xattn_gru_bih, L0_xattn_gru_bhh, L0_xattn_slot_norm_w, L0_xattn_input_norm_w, L0_ffn_W_A, L0_ffn_W_B, L0_ffn_W_up, L0_ffn_W_down):
    import jax
    import jax.numpy as jnp

    def _L0_attn_ref(x, Wqkv, bqkv, q_gamma, q_beta, k_gamma, k_beta, alpha, Wproj, bproj):
        import jax, jax.numpy as jnp
        import numpy as np
        H = 16
        TOPK_RATIO = 0.05
        LN_EPS = 1e-05

        def _layernorm(t, gamma, beta):
            mu = t.mean(-1, keepdims=True)
            var = t.var(-1, keepdims=True)
            return (t - mu) * jax.lax.rsqrt(var + LN_EPS) * gamma + beta
        B, N, C = x.shape
        D = C // H
        qkv = (x @ Wqkv.T + bqkv).reshape(B, N, 3, H, D).transpose(2, 0, 3, 1, 4)
        q, k, v = (qkv[0], qkv[1], qkv[2])
        q = _layernorm(q, q_gamma, q_beta)
        k = _layernorm(k, k_gamma, k_beta)
        scores = jnp.einsum('bhnd,bhmd->bhnm', q, k) / jnp.sqrt(jnp.float32(D))
        aw = jax.nn.softmax(scores, axis=-1)
        topk = max(1, int(N * TOPK_RATIO))
        kth = jax.lax.top_k(aw, topk)[0][..., -1:]
        mask = (aw >= kth).astype(aw.dtype)
        aws = aw * mask
        aws = aws / (aws.sum(-1, keepdims=True) + 1e-08)
        o_s = jnp.einsum('bhnm,bhmd->bhnd', aws, v)
        qf = jax.nn.softmax(q, axis=-1)
        kf = jax.nn.softmax(k, axis=-1)
        kv = jnp.einsum('bhnd,bhne->bhde', kf, v)
        z = jnp.einsum('bhnd,bhd->bhn', qf, kf.sum(axis=2))
        o_l = jnp.einsum('bhnd,bhde->bhne', qf, kv) / (z[..., None] + 1e-06)
        a = jax.nn.sigmoid(alpha).reshape(1, H, 1, 1)
        o = (a * o_s + (1.0 - a) * o_l).transpose(0, 2, 1, 3).reshape(B, N, C)
        return o @ Wproj.T + bproj

    def _L0_xattn_ref(slots, P, Wq, Wk, Wv, gru_wih, gru_whh, gru_bih, gru_bhh, slot_norm_w, input_norm_w):
        import jax, jax.numpy as jnp
        import numpy as np
        D = 128
        NUM_ITERS = 3
        EPS = 1e-06
        SCALE = D ** (-0.5)

        def rmsnorm(x, w, eps=EPS):
            return x * jax.lax.rsqrt(jnp.mean(x * x, axis=-1, keepdims=True) + eps) * w

        def gru_cell(x, h, wih, whh, bih, bhh):
            gx = x @ wih.T + bih
            gh = h @ whh.T + bhh
            xr, xz, xn = jnp.split(gx, 3, axis=-1)
            hr, hz, hn = jnp.split(gh, 3, axis=-1)
            r = jax.nn.sigmoid(xr + hr)
            z = jax.nn.sigmoid(xz + hz)
            n = jnp.tanh(xn + r * hn)
            return (1.0 - z) * n + z * h
        Pn = rmsnorm(P, input_norm_w)
        k_proj = Pn @ Wk.T
        v_proj = Pn @ Wv.T
        for _ in range(NUM_ITERS):
            sn = rmsnorm(slots, slot_norm_w)
            q_proj = sn @ Wq.T
            scores = jnp.einsum('bkd,bmd->bkm', q_proj, k_proj) * SCALE
            attn = jax.nn.softmax(scores, axis=-2)
            attn = attn / (jnp.sum(attn, axis=-1, keepdims=True) + EPS)
            updates = jnp.einsum('bkm,bmd->bkd', attn, v_proj)
            slots = gru_cell(updates, slots, gru_wih, gru_whh, gru_bih, gru_bhh)
        return slots

    def _L0_ffn_ref(hidden_states, W_A, W_B, W_up, W_down):
        import jax, jax.numpy as jnp
        import numpy as np
        E, K, H, F, R = (8, 2, 128, 256, 64)
        B, S = (2, 256)
        orig_shape = hidden_states.shape
        x = hidden_states.reshape(-1, orig_shape[-1])
        num_experts = W_A.shape[0]
        gate_hidden = jnp.einsum('nh,erh->ner', x, W_A)
        scores = jnp.sqrt(jnp.sum(gate_hidden * gate_hidden, axis=-1))
        topk_scores, topk_idx = jax.lax.top_k(scores, K)
        topk_w = jax.nn.softmax(topk_scores, axis=-1)
        w_full = jnp.sum(jax.nn.one_hot(topk_idx, num_experts, dtype=topk_w.dtype) * topk_w[..., None], axis=1)
        g = jnp.einsum('ner,efr->nef', gate_hidden, W_B)
        up = jnp.einsum('nh,efh->nef', x, W_up)
        y = jnp.einsum('nef,ehf->neh', jax.nn.silu(g) * up, W_down)
        out = jnp.einsum('neh,ne->nh', y, w_full)
        return out.reshape(orig_shape)
    x = x + _L0_attn_ref(_layernorm(x, axis=-1), L0_attn_Wqkv, L0_attn_bqkv, L0_attn_q_gamma, L0_attn_q_beta, L0_attn_k_gamma, L0_attn_k_beta, L0_attn_alpha, L0_attn_Wproj, L0_attn_bproj)
    x = x + _L0_xattn_ref(_layernorm(x, axis=-1), ctx_1024, L0_xattn_Wq, L0_xattn_Wk, L0_xattn_Wv, L0_xattn_gru_wih, L0_xattn_gru_whh, L0_xattn_gru_bih, L0_xattn_gru_bhh, L0_xattn_slot_norm_w, L0_xattn_input_norm_w)
    x = x + _L0_ffn_ref(_layernorm(x, axis=-1), L0_ffn_W_A, L0_ffn_W_B, L0_ffn_W_up, L0_ffn_W_down)
    return x

_drawn_inputs = setup_inputs


def setup_inputs(seed=0):
    import zlib

    import numpy as np

    out = dict(_drawn_inputs(seed))
    spreads = {'L0_attn_bqkv': (0.0, 0.1),
     'L0_attn_q_gamma': (1.0, 0.2),
     'L0_attn_q_beta': (0.0, 0.1),
     'L0_attn_k_gamma': (1.0, 0.2),
     'L0_attn_k_beta': (0.0, 2.0),
     'L0_attn_alpha': (0.5, 0.6),
     'L0_attn_bproj': (0.0, 0.1),
     'L0_xattn_gru_bih': (0.0, 0.1),
     'L0_xattn_gru_bhh': (0.0, 0.1),
     'L0_xattn_slot_norm_w': (1.0, 0.6),
     'L0_xattn_input_norm_w': (1.0, 0.2)}
    factors = {'L0_ffn_W_A': 8.0, 'L0_ffn_W_B': 8.0, 'L0_ffn_W_up': 8.0, 'L0_ffn_W_down': 8.0}
    for name, (base, spread) in spreads.items():
        noise = np.random.default_rng([zlib.crc32(name.encode()), seed]).standard_normal(out[name].shape)
        drawn = base * np.exp(spread * noise) if base else spread * noise
        out[name] = jnp.asarray(drawn.astype(out[name].dtype))
    for name, factor in factors.items():
        out[name] = (out[name] * factor).astype(out[name].dtype)
    return out
```

```python
import concourse.bass as bass
from concourse import mybir
from contextlib import ExitStack

F32 = mybir.dt.float32
U32 = mybir.dt.uint32
ALU = mybir.AluOpType
ACT = mybir.ActivationFunctionType
AX = mybir.AxisListType

B, N, C = 2, 512, 128
H = 16
D = C // H
DV = D + 1
M = 32
EXPERTS, RANK, FF = 8, 64, 256
ITERS = 3
P = 128
TPB = N // P
T = B * TPB
TOPK = max(1, int(N * 0.05))
BH = B * H
LN_EPS, RMS_EPS, ATT_EPS, LIN_EPS = 1e-5, 1e-6, 1e-8, 1e-6
SCALE = C ** -0.5
REMOVED = -3.0e38

GROUPS = (["wqkv", "rows", "cols", "xn0", "xn1", "x0", "x1", "qT0", "kT0", "proj", "wk_wv", "wih", "whh"]
          + [f"wa{i}" for i in range(1)] + [f"wb{i}" for i in range(2)] + [f"wup{i}" for i in range(4)]
          + [f"wdn{i}" for i in range(4)] + ["ctx", "kproj", "qk_fold", "vproj", "qT1", "kT1", "qf0", "qf1"])


def upto(name):
    return GROUPS.index(name) + 1


def build(nc, x, ctx_in, Wqkv, bqkv, q_gamma, q_beta, k_gamma, k_beta, alpha, Wproj, bproj, Wq, Wk, Wv,
          wih, whh, bih, bhh, slot_w, input_w, W_A, W_B, W_up, W_down, out):
    ctx = ExitStack()
    with ctx:
        def sb(name, shape, dt=F32):
            return ctx.enter_context(nc.sbuf_tensor(name, shape, dt))

        def sem(name):
            return ctx.enter_context(nc.semaphore(name))

        x_sb = sb("x_sb", [P, T, C])
        ctx_sb = sb("ctx_sb", [B * M, C])
        wqkv = sb("wqkv", [P, 3, C])
        wproj, wq, wk, wv = (sb(n, [C, C]) for n in ("wproj", "wq", "wk", "wv"))
        wih_sb, whh_sb = sb("wih_sb", [P, 3, C]), sb("whh_sb", [P, 3, C])
        wa_sb = sb("wa_sb", [P, 4, C])
        wb_sb = sb("wb_sb", [P, 4, 2, P])
        wup_sb = sb("wup_sb", [P, 16, C])
        wdn_sb = sb("wdn_sb", [P, EXPERTS, FF])
        ROW = 3 * C + 4 * D + H
        row = sb("row", [1, ROW])
        cols_in = sb("cols_in", [9, C])

        ident = sb("ident", [P, P])
        headmask = sb("headmask", [P, H])
        blockmask = sb("blockmask", [P, H, DV])
        halves = sb("halves", [P, 2])
        blk = sb("blk", [P, 4, EXPERTS])
        ones_row = sb("ones_row", [1, P])
        mean_mat = sb("mean_mat", [P, P])
        ones_m = sb("ones_m", [M, P])
        minus_half = sb("minus_half", [P, 1])
        plus_half = sb("plus_half", [P, 1])
        iota8 = sb("iota8", [P, EXPERTS])

        wqkvT = sb("wqkvT", [C, 3 * C])
        rowb = sb("rowb", [P, ROW])
        cols = sb("cols", [C, 9])
        wprojT = sb("wprojT", [C, C])
        wkvT = sb("wkvT", [C, 2, C])
        wihT, whhT = sb("wihT", [C, 3, C]), sb("whhT", [C, 3, C])
        waT = sb("waT", [C, 4, P])
        wbT = sb("wbT", [P, 4, 2, P])
        wupT = sb("wupT", [C, 16, P])
        wdnT = sb("wdnT", [P, EXPERTS, 2, C])
        half_rz = sb("half_rz", [C, 2])
        half_hn = sb("half_hn", [C, 1])
        brz = sb("brz", [C, 2])
        gammab, betab = sb("gammab", [P, 2, H, D]), sb("betab", [P, 2, H, D])
        alpha_t = sb("alpha_t", [P, H])
        mix = sb("mix", [P, 2, H])

        stats = sb("stats", [P, T, 6])
        mv = sb("mv", [P, T, 2])
        veps1 = sb("veps1", [P, T])
        rstd1 = sb("rstd1", [P, T])
        xn = sb("xn", [P, T, C])
        xnT, xT = sb("xnT", [C, B * N]), sb("xT", [C, B * N])
        qk = sb("qk", [P, T, 2 * C])
        vaug = sb("vaug", [P, T, H, DV])
        GR = TPB * 2 * H
        gsum, gmean, gvar, gveps, grstd = (sb(n, [P, B, GR]) for n in ("gsum", "gmean", "gvar", "gveps", "grstd"))
        gmax, gden, grec = (sb(n, [P, B, GR]) for n in ("gmax", "gden", "grec"))
        diff = sb("diff", [P, B, TPB * 2 * C])
        sqd = sb("sqd", [P, B, TPB * 2 * C])
        feat = sb("feat", [P, T, 2 * C])
        qT, kT, qfT = sb("qT", [C, B * N]), sb("kT", [C, B * N]), sb("qfT", [C, B * N])

        qm = [sb(f"qm{i}", [C, 2 * P]) for i in range(2)]
        S_all, E_all = sb("S_all", [P, TPB, N]), sb("E_all", [P, TPB, N])
        S = [S_all[:, i, :] for i in range(TPB)]
        W_all, PT_all = sb("W_all", [P, 2, N]), sb("PT_all", [P, 2, N])
        W = [W_all[:, i, :] for i in range(2)]
        E = [E_all[:, i, :] for i in range(TPB)]
        PT = [PT_all[:, i, :] for i in range(2)]
        top = [sb(f"top{i}", [P, 32]) for i in range(TPB)]
        negmax = [sb(f"negmax{i}", [P, 1]) for i in range(TPB)]
        zb = sb("zb", [P, TPB])
        zall = sb("zall", [P, BH, TPB])

        kvb = sb("kvb", [P, B, H * DV])
        den = sb("den", [P, B, 2, TPB, H])
        rden = sb("rden", [P, B, 2, TPB, H])
        wden = sb("wden", [P, B, 2, TPB, H])
        o_tok = sb("o_tok", [P, B, TPB, C])
        o_s, o_l = (a[:, :, :].rearrange("p (b j) c -> p b j c", b=B) for a in (x_sb, xn))
        oT = sb("oT", [C, B, N])
        x1T, x2T = sb("x1T", [C, B, N]), sb("x2T", [C, B, N])
        dT, vT, sqT, rT = diff[:, :, 0:N], diff[:, :, N:2 * N], sqd[:, :, 0:N], sqd[:, :, N:2 * N]
        slots = sb("slots", [C, B, N])
        hT = S_all[:, 0:2, :]
        csq, css, cms, crs = sb("csq", [B * M, C]), sb("css", [B * M, 1]), sb("cms", [B * M, 1]), sb("crs", [B * M, 1])
        pn = sb("pn", [B * M, C])
        pnT = sb("pnT", [C, B * M])
        pnTw = sb("pnTw", [C, B * M])
        kpT = sb("kpT", [C, B * M])
        fold = sb("fold", [C, B * M])
        foldw = sb("foldw", [C, B * M])
        vp = sb("vp", [M, B, C])
        mse, rn = W_all[0:M], PT_all[0:M]
        ex, at = (wup_sb[0:M, 8 * i:8 * i + 8, :].rearrange("p (b j) c -> p b (j c)", b=B) for i in range(2))
        sc = wdn_sb[0:M, 0:4, :].rearrange("p (b j) c -> p b (j c)", b=B)
        smax, snm, ssum, srec = (sb(n, [M, B]) for n in ("smax", "snm", "ssum", "srec"))
        dde, drc = (a[:, :, :].rearrange("p (b j) c -> p b (j c)", b=B) for a in (x_sb, xn))
        upd = xnT[:, :].rearrange("p (b n) -> p b n", b=B)
        zt, ee = (a[:, :].rearrange("p (b n) -> p b n", b=B) for a in (qT, kT))
        rt, dd = sb("rt", [C, B, N]), sb("dd", [C, B, N])
        hw, t1, t2, nn = S_all[:, 0:2, :], S_all[:, 2:4, :], E_all[:, 0:2, :], E_all[:, 2:4, :]
        gh = [a[:, :, :].rearrange("p (k i) c -> p k (i c)", i=2) for a in (qk, feat)]
        sqg = [wup_sb[:, :, :].rearrange("p (k i) c -> p k (i c)", i=4), wdn_sb[:, :, :].rearrange("p (k i) c -> p k (i c)", i=2)]
        s2, sr = sb("s2", [P, B, TPB, EXPERTS]), sb("sr", [P, B, TPB, EXPERTS])
        m8 = sb("m8", [P, B, TPB, EXPERTS])
        ix = sb("ix", [P, B, TPB, EXPERTS], U32)
        ixf = sb("ixf", [P, B, TPB, 2])
        sdif, sexp, spl, srecp = (sb(n, [P, B, TPB]) for n in ("sdif", "sexp", "spl", "srecp"))
        w12 = sb("w12", [P, B, 2, TPB])
        eq = sb("eq", [P, B, 2, TPB, EXPERTS])
        ew = sb("ew", [P, B, 2, TPB, EXPERTS])
        wfull = sb("wfull", [P, B, TPB, EXPERTS])
        th, a1, a2 = PT, W, E
        acc = o_tok

        bank = [ctx.enter_context(nc.psum_tensor(f"bank{i}", [P, 512], F32)) for i in range(4)]
        obank = ctx.enter_context(nc.psum_tensor("obank", [P, 4 * 512], F32))

        def ob(i):
            return obank[:, i * 512:(i + 1) * 512]

        def work(b, i):
            return bank[2 * b + i][:, :] if i < 2 else ob(2 * b + i - 2)

        names = """x0_in x1_in wqkv_in rows_in cols_in_s ctx_in_s att_in xw_in ffa_in ffb_in ffu_in ffd_in consts small
            fence stat_s mv_s veps_s rstd_s xn_s group_ps moved qkv_ps qk_sb v_sb
            lnq dsub dsq dvar dpow qk_ready fmax_s fexp fready scal_c act_c csum_s cpow_s pn_s pnw_s kp_w
            qm_ready scores_ps scores_sb negmax_s exp_done masked pt_ps pt_sb av_done z_saved topk_step
            kv_ps kv_sb ol_ps o_ready ot_ps ot_sb pr_ps x1_s ln_m ln_d ln_q ln_v ln_e ln_r ln_h
            sl_sq ms_ps ms_sb rn_s sc_s snm_s ex_s at_s du_ps u_s g_ps gate_s hw_s t2_s n_s slot_s
            ga_ps gh_s sc_ps s2_s sr_s sd_s se_s wf_s gu_ps th_s a2_s y_ps acc_s x2_ps x2_tok out_s
            dchain pchain achain""".split()
        s = {n: sem(n) for n in names}

        block = ctx.enter_context(nc.Block())

        @block.sync
        def _(sp):
            for b in range(B):
                sp.dma_start(x_sb[:, TPB * b:TPB * (b + 1), :],
                             x[b].rearrange("(j p) c -> p j c", p=P)).then_inc(s[f"x{b}_in"], 16)
            sp.dma_start(ctx_sb[:, :], ctx_in.rearrange("b m c -> (b m) c")).then_inc(s["ctx_in_s"], 16)
            for dst, src in ((wproj, Wproj), (wq, Wq), (wk, Wk), (wv, Wv)):
                sp.dma_start(dst[:, :], src).then_inc(s["xw_in"], 16)
            for dst, src in ((wih_sb, wih), (whh_sb, whh)):
                sp.dma_start(dst[:, :, :], src.rearrange("(g p) c -> p g c", p=P)).then_inc(s["xw_in"], 16)
            sp.dma_start(wup_sb[:, :, :], W_up.rearrange("e (f p) c -> p (e f) c", p=P)).then_inc(s["ffu_in"], 16)
            sp.dma_start(wdn_sb[:, :, :], W_down.rearrange("e h f -> h e f")).then_inc(s["ffd_in"], 16)
            for b in range(B):
                sp.wait_ge(s["acc_s"], (b + 1) * EXPERTS)
                sp.dma_start(out[b].rearrange("(j p) c -> p j c", p=P), acc[:, b]).then_inc(s["out_s"], 16)
            sp.wait_ge(s["out_s"], 16 * B)

        @block.gpsimd
        def _(pool):
            n = [0]

            def link(ins):
                n[0] += 1
                ins.then_inc(s["pchain"], 1)
                pool.wait_ge(s["pchain"], n[0])

            link(nc.gpsimd.memset(ident[:, :], 0.0))
            link(nc.gpsimd.affine_select(out=ident[:, :], in_=ident[:, :], compare_op=ALU.not_equal, fill=1.0,
                                         base=0, pattern=[[-1, P]], channel_multiplier=1))
            link(nc.gpsimd.memset(headmask[:, :], 1.0))
            link(nc.gpsimd.affine_select(out=headmask[:, :], in_=headmask[:, :], compare_op=ALU.is_ge, fill=0.0,
                                         base=0, pattern=[[-D, H]], channel_multiplier=1))
            link(nc.gpsimd.affine_select(out=headmask[:, :], in_=headmask[:, :], compare_op=ALU.is_ge, fill=0.0,
                                         base=D - 1, pattern=[[D, H]], channel_multiplier=-1))
            link(nc.gpsimd.memset(halves[:, :], 1.0))
            link(nc.gpsimd.affine_select(out=halves[:, 0:1], in_=halves[:, 0:1], compare_op=ALU.is_ge, fill=0.0,
                                         base=RANK - 1, pattern=[[0, 1]], channel_multiplier=-1))
            link(nc.gpsimd.affine_select(out=halves[:, 1:2], in_=halves[:, 1:2], compare_op=ALU.is_ge, fill=0.0,
                                         base=-RANK, pattern=[[0, 1]], channel_multiplier=1))
            pool.sem_inc(s["consts"], 1)

            def power(dst, src, width, what):
                const = (minus_half if what < 0 else plus_half)[0:src.shape[0], 0:1]
                return nc.gpsimd.tensor_tensor(dst, src, const.to_broadcast([src.shape[0], width]), ALU.pow)

            pool.wait_ge(s["small"], 1)
            for b in range(B):
                pool.wait_ge(s["veps_s"], b + 1)
                t0 = b * TPB
                power(rstd1[:, t0:t0 + TPB], veps1[:, t0:t0 + TPB], TPB, -1).then_inc(s["rstd_s"], 1)
            pool.wait_ge(s["csum_s"], 1)
            power(crs[:, :], cms[:, :], 1, -1).then_inc(s["cpow_s"], 1)
            for b in range(B):
                pool.wait_ge(s["dvar"], b + 1)
                power(grstd[:, b], gveps[:, b], GR, -1).then_inc(s["dpow"], 1)

            def q_masks(h, p, after=None):
                if after is not None:
                    pool.wait_ge(s["scores_ps"], after)
                pool.sem_inc(s["fence"], 1)
                b = h // H if isinstance(h, int) else (h >> 4) & 1
                hh = h % H if isinstance(h, int) else h & (H - 1)
                nc.gpsimd.tensor_tensor(qm[p][:, :], qT[:, bass.ds(b * N + p * 2 * P, 2 * P)],
                                        headmask[:, bass.ds(hh, 1)].to_broadcast([P, 2 * P]),
                                        ALU.mult).then_inc(s["qm_ready"], 1)

            def save_z(h):
                pool.wait_ge(s["exp_done"], h * TPB + TPB)
                pool.sem_inc(s["fence"], 1)
                nc.gpsimd.tensor_copy(zall[:, bass.ds(h, 1), :], zb[:, :].rearrange("p (o j) -> p o j", o=1)).then_inc(s["z_saved"], 1)

            pool.wait_ge(s["moved"], upto("qT1"))
            q_masks(0, 0)
            q_masks(0, 1)
            with pool.Fori(1, BH) as h:
                q_masks(h, 0, after=h * TPB - TPB + 2)
                q_masks(h, 1, after=h * TPB)
                save_z(h - 1)
            save_z(BH - 1)

            def lns(k):
                for b in range(B):
                    pool.wait_ge(s["ln_e"], 2 * k + b + 1)
                    power(rT[:, b], vT[:, b], N, -1).then_inc(s["ln_r"], 1)

            lns(0)
            for it in range(ITERS):
                for b in range(B):
                    pool.wait_ge(s["ms_sb"], 2 * it + b + 1)
                    power(rn[:, b], mse[:, b], N, -1).then_inc(s["rn_s"], 1)
            lns(1)
            for b in range(B):
                pool.wait_ge(s["s2_s"], b + 1)
                power(sr[:, b].rearrange("p j e -> p (j e)"), s2[:, b].rearrange("p j e -> p (j e)"),
                      TPB * EXPERTS, 1).then_inc(s["sr_s"], 1)

        @block.tensor
        def _(pe):
            g = [0]

            def group():
                if g[0] >= 2:
                    pe.wait_ge(s["moved"], g[0] - 1)
                g[0] += 1
                return bank[2 + (g[0] - 1) % 2]

            def transposes(srcs, rows=P):
                bk = group()
                for i, src in enumerate(srcs):
                    last = nc.tensor.transpose(bk[0:src.shape[1], i * rows:(i + 1) * rows], src, ident[0:rows, 0:rows])
                last.then_inc(s["group_ps"], 1)

            pe.wait_ge(s["consts"], 1)
            pe.wait_ge(s["wqkv_in"], 16)
            transposes([wqkv[:, i, :] for i in range(3)])
            pe.wait_ge(s["rows_in"], 16 * 6)
            pe.wait_ge(s["small"], 1)
            nc.tensor.matmul(group()[:, 0:ROW], ones_row[:, :], row[:, :], start=True, stop=True).then_inc(s["group_ps"], 1)
            pe.wait_ge(s["cols_in_s"], 16 * 5)
            bk = group()
            nc.tensor.transpose(bk[:, 0:9], cols_in[:, :], ident[0:9, 0:9]).then_inc(s["group_ps"], 1)
            for b in range(B):
                pe.wait_ge(s["xn_s"], TPB * (b + 1))
                transposes([xn[:, TPB * b + j, :] for j in range(TPB)])

            def qkv(b):
                pe.wait_ge(s["moved"], upto(f"xn{b}"))
                for j in range(TPB):
                    t = b * TPB + j
                    if t >= 2:
                        pe.wait_ge(s["qk_sb"], t - 1)
                        pe.wait_ge(s["v_sb"], t - 1)
                    nc.tensor.matmul(bank[t % 2][:, 0:3 * C], xnT[:, t * P:(t + 1) * P], wqkvT[:, :],
                                     start=True, stop=False)
                    nc.tensor.matmul(bank[t % 2][:, 0:3 * C], ones_row[:, :], row[:, 0:3 * C],
                                     start=False, stop=True).then_inc(s["qkv_ps"], 1)

            qkv(0)
            qkv(1)
            for b in range(B):
                transposes([x_sb[:, TPB * b + j, :] for j in range(TPB)])
            for b in range(1):
                pe.wait_ge(s["qk_ready"], b + 1)
                for i in range(2):
                    transposes([qk[:, TPB * b + j, i * C:(i + 1) * C] for j in range(TPB)])
            pe.wait_ge(s["xw_in"], 16 * 6)
            transposes([wproj[:, :]])
            transposes([wk[:, :], wv[:, :]])
            transposes([wih_sb[:, i, :] for i in range(3)])
            transposes([whh_sb[:, i, :] for i in range(3)])
            pe.wait_ge(s["ffa_in"], 16)
            transposes([wa_sb[:, i, :] for i in range(4)])
            pe.wait_ge(s["ffb_in"], 16 * 16)
            for k in range(2):
                transposes([wb_sb[:, 2 * k + i // 2, i % 2, :] for i in range(4)])
            pe.wait_ge(s["ffu_in"], 16)
            for k in range(4):
                transposes([wup_sb[:, 4 * k + i, :] for i in range(4)])
            pe.wait_ge(s["ffd_in"], 16)
            for k in range(4):
                transposes([wdn_sb[:, 2 * k + i // 2, (i % 2) * P:(i % 2 + 1) * P] for i in range(4)])
            pe.wait_ge(s["pn_s"], 1)
            transposes([pn[:, :]], rows=B * M)
            pe.wait_ge(s["pnw_s"], 1)
            nc.tensor.matmul(group()[:, 0:B * M], wkvT[:, 0, :], pnTw[:, :], start=True, stop=True).then_inc(s["group_ps"], 1)
            pe.wait_ge(s["moved"], upto("kproj"))
            nc.tensor.matmul(group()[:, 0:B * M], wq[:, :], kpT[:, :], start=True, stop=True).then_inc(s["group_ps"], 1)
            bk = group()
            for b in range(B):
                last = nc.tensor.matmul(bk[0:M, b * C:(b + 1) * C], pnTw[:, b * M:(b + 1) * M], wkvT[:, 1, :],
                                        start=True, stop=True)
            last.then_inc(s["group_ps"], 1)
            pe.wait_ge(s["qk_ready"], 2)
            for i in range(2):
                transposes([qk[:, TPB + j, i * C:(i + 1) * C] for j in range(TPB)])
            for b in range(B):
                pe.wait_ge(s["fready"], b + 1)
                transposes([feat[:, TPB * b + j, 0:C] for j in range(TPB)])
            assert g[0] == len(GROUPS)

            def batch_of(h):
                return h // H if isinstance(h, int) else (h >> 4) & 1

            def head_of(h):
                return h % H if isinstance(h, int) else h & (H - 1)

            def scores(h, p, first=False):
                pe.wait_ge(s["qm_ready"], h * 2 + p + 1)
                for w in range(2):
                    j = 2 * p + w
                    if not (first and p == 0):
                        pe.wait_ge(s["scores_sb"], h * TPB + j - 1)
                    nc.tensor.matmul(bank[w][:, :], qm[p][:, w * P:(w + 1) * P],
                                     kT[:, bass.ds(batch_of(h) * N, N)], start=True, stop=True
                                     ).then_inc(s["scores_ps"], 1)

            def weigh(h, p):
                for w in range(2):
                    j = 2 * p + w
                    pe.wait_ge(s["masked"], h * TPB + j + 1)
                    pe.wait_ge(s["pt_sb"], h * TPB + j + 1)
                    for c in range(TPB):
                        last = nc.tensor.transpose(bank[2 + w][:, c * P:(c + 1) * P], E[j][:, c * P:(c + 1) * P], ident[:, :])
                    last.then_inc(s["pt_ps"], 1)
                for w in range(2):
                    j = 2 * p + w
                    pe.wait_ge(s["pt_sb"], h * TPB + j + 3)
                    at_col = batch_of(h) * 1024 + head_of(h) * DV + (p * 512 + w * H * DV)
                    for c in range(TPB):
                        last = nc.tensor.matmul(
                            obank[:, bass.ds(at_col, DV)], PT[w][:, c * P:(c + 1) * P],
                            vaug[:, :, :, :].rearrange("p t h e -> p (t h e)")[
                                :, bass.ds(batch_of(h) * (TPB * H * DV) + head_of(h) * DV + c * H * DV, DV)],
                            start=(c == 0), stop=(c == TPB - 1))
                    last.then_inc(s["av_done"], 1)

            pe.wait_ge(s["moved"], len(GROUPS))
            pe.wait_ge(s["qk_sb"], T)
            pe.wait_ge(s["v_sb"], T)
            scores(0, 0, first=True)
            scores(0, 1, first=True)
            with pe.Fori(1, BH) as h:
                for p in range(2):
                    scores(h, p)
                    weigh(h - 1, p)
            for p in range(2):
                weigh(BH - 1, p)

            for b in range(B):
                if b == 0:
                    pe.wait_ge(s["scores_sb"], BH * TPB)
                    pe.wait_ge(s["pt_sb"], BH * TPB + 2)
                for j in range(TPB):
                    last = nc.tensor.matmul(work(b, 0)[:, 0:H * DV], feat[:, TPB * b + j, C:2 * C],
                                            vaug[:, TPB * b + j].rearrange("p h e -> p (h e)"),
                                            start=(j == 0), stop=(j == TPB - 1))
                last.then_inc(s["kv_ps"], 1)
            for b in range(B):
                pe.wait_ge(s["kv_sb"], b + 1)
                for j in range(TPB):
                    last = nc.tensor.matmul(work(b, j // 2)[:, (j % 2) * H * DV:(j % 2 + 1) * H * DV],
                                            qfT[:, (TPB * b + j) * P:(TPB * b + j + 1) * P], kvb[:, b, :],
                                            start=True, stop=True)
                last.then_inc(s["ol_ps"], 1)
            for b in range(B):
                pe.wait_ge(s["o_ready"], b + 1)
                for j in range(TPB):
                    last = nc.tensor.transpose(work(b, 0)[:, j * P:(j + 1) * P], o_tok[:, b, j, :], ident[:, :])
                last.then_inc(s["ot_ps"], 1)
            for b in range(B):
                pe.wait_ge(s["ot_sb"], b + 1)
                nc.tensor.matmul(work(b, 1), wprojT[:, :], oT[:, b, :], start=True, stop=True).then_inc(s["pr_ps"], 1)

            def layer_norm(k, src, ready, value):
                for b in range(B):
                    pe.wait_ge(s[ready], value + b)
                    nc.tensor.matmul(work(b, 0), mean_mat[:, :], src[:, b, :], start=True, stop=True).then_inc(s["ln_m"], 1)
                for b in range(B):
                    pe.wait_ge(s["ln_q"], 2 * k + b + 1)
                    nc.tensor.matmul(work(b, 2), mean_mat[:, :], sqT[:, b, :], start=True, stop=True).then_inc(s["ln_v"], 1)

            layer_norm(0, x1T, "x1_s", 1)
            for it in range(ITERS):
                for b in range(B):
                    if it == 0:
                        pe.wait_ge(s["ln_h"], b + 1)
                    else:
                        pe.wait_ge(s["slot_s"], 2 * (it - 1) + b + 1)
                    nc.tensor.matmul(work(b, 1)[0:M, :], foldw[:, b * M:(b + 1) * M], slots[:, b, :], start=True, stop=True)
                    for i in range(2):
                        nc.tensor.matmul(work(b, 2 + i), whhT[:, i, :], slots[:, b, :], start=True, stop=False)
                    pe.wait_ge(s["sl_sq"], 2 * it + b + 1)
                    nc.tensor.matmul(work(b, 0)[0:M, :], mean_mat[:, 0:M], sqT[:, b, :], start=True, stop=True
                                     ).then_inc(s["ms_ps"], 1)
                for b in range(B):
                    pe.wait_ge(s["at_s"], 2 * it + b + 1)
                    nc.tensor.matmul(work(b, 0), ones_m[:, :], at[:, b, :], start=True, stop=True)
                    nc.tensor.matmul(work(b, 1), vp[:, b, :], at[:, b, :], start=True, stop=True).then_inc(s["du_ps"], 1)
                for b in range(B):
                    pe.wait_ge(s["u_s"], 2 * it + b + 1)
                    for i in range(2):
                        nc.tensor.matmul(work(b, 2 + i), wihT[:, i, :], upd[:, b, :], start=False, stop=True)
                    nc.tensor.matmul(work(b, 0), whhT[:, 2, :], slots[:, b, :], start=True, stop=True)
                    nc.tensor.matmul(work(b, 1), wihT[:, 2, :], upd[:, b, :], start=True, stop=True).then_inc(s["g_ps"], 1)
            layer_norm(1, x2T, "slot_s", 2 * ITERS + 1)

            for b in range(B):
                pe.wait_ge(s["ln_h"], 2 + b + 1)
                for c in range(4):
                    if c >= 2 or b:
                        pe.wait_ge(s["gh_s"], 2 * (4 * b + c - 1))
                    nc.tensor.matmul(bank[c % 2][:, :], waT[:, c, :], hT[:, b, :], start=True, stop=True).then_inc(s["ga_ps"], 1)
                if b:
                    pe.wait_ge(s["acc_s"], b * EXPERTS)
                for j in range(TPB):
                    for c in range(4):
                        pe.wait_ge(s["gh_s"], 2 * (4 * b + c) + 2)
                        last = nc.tensor.matmul(bank[2][:, (b * TPB + j) * EXPERTS:(b * TPB + j + 1) * EXPERTS],
                                                sqg[b][:, c, j * P:(j + 1) * P], blk[:, c, :], start=(c == 0), stop=(c == 3))
                last.then_inc(s["sc_ps"], 1)
                for j in range(TPB):
                    last = nc.tensor.transpose(bank[3][:, j * P:(j + 1) * P], x2T[:, b, j * P:(j + 1) * P], ident[:, :])
                last.then_inc(s["x2_ps"], 1)

                def down(e):
                    pe.wait_ge(s["a2_s"], 2 * (b * EXPERTS + e) + 2)
                    if b * EXPERTS + e:
                        pe.wait_ge(s["acc_s"], b * EXPERTS + e)
                    for j in range(TPB):
                        for f in range(2):
                            last = nc.tensor.matmul(bank[2][:, j * P:(j + 1) * P], a2[2 * (e % 2) + f][:, j * P:(j + 1) * P],
                                                    wdnT[:, e, f, :], start=(f == 0), stop=(f == 1))
                    last.then_inc(s["y_ps"], 1)

                pe.wait_ge(s["s2_s"], b + 1)
                for e in range(EXPERTS):
                    for f in range(2):
                        k = 2 * (b * EXPERTS + e) + f
                        if k >= 2:
                            pe.wait_ge(s["a2_s"], k - 1)
                        o = (e % 2) * RANK
                        nc.tensor.matmul(ob(f), wbT[o:o + RANK, e // 2, f, :], gh[b][o:o + RANK, e // 2, :], start=True, stop=True)
                        nc.tensor.matmul(ob(2 + f), wupT[:, 2 * e + f, :], hT[:, b, :], start=True, stop=True
                                         ).then_inc(s["gu_ps"], 1)
                    if e:
                        down(e - 1)
                down(EXPERTS - 1)

        @block.scalar
        def _(act):
            act.dma_start(wqkv[:, :, :], Wqkv.rearrange("(g p) c -> p g c", p=P)).then_inc(s["wqkv_in"], 16)
            at_ = 0
            for src, k in ((bqkv, 3 * C), (q_gamma, D), (k_gamma, D), (q_beta, D), (k_beta, D), (alpha, H)):
                act.dma_start(row[:, at_:at_ + k], src.rearrange("(o n) -> o n", o=1)).then_inc(s["rows_in"], 16)
                at_ += k
            for r, src in enumerate((bproj, slot_w, input_w)):
                act.dma_start(cols_in[r:r + 1, :], src.rearrange("(o n) -> o n", o=1)).then_inc(s["cols_in_s"], 16)
            for r, src in ((3, bih), (6, bhh)):
                act.dma_start(cols_in[r:r + 3, :], src.rearrange("(o n) -> o n", o=3)).then_inc(s["cols_in_s"], 16)
            act.dma_start(wa_sb[:, :, :], W_A.rearrange("(k e) r c -> (e r) k c", e=2)).then_inc(s["ffa_in"], 16)
            for e in range(EXPERTS):
                for f in range(2):
                    act.dma_start(wb_sb[:, e // 2, f, (e % 2) * RANK:(e % 2 + 1) * RANK],
                                  W_B[e, f * P:(f + 1) * P, :]).then_inc(s["ffb_in"], 16)

            g = [0]

            def copy(dst, src):
                return nc.scalar.activation(dst, src, ACT.Copy)

            def move(name, dst, rows, width):
                assert GROUPS[g[0]] == name
                act.wait_ge(s["group_ps"], g[0] + 1)
                copy(dst, bank[2 + g[0] % 2][0:rows, 0:width]).then_inc(s["moved"], 1)
                g[0] += 1

            def flat(ap, pattern):
                return ap.rearrange(pattern)

            act.wait_ge(s["ctx_in_s"], 16)
            nc.scalar.activation(csq[:, :], ctx_sb[:, :], ACT.Square, accum_out=css[:, :]).then_inc(s["achain"], 1)
            move("wqkv", wqkvT[:, :], P, 3 * C)
            move("rows", rowb[:, :], P, ROW)
            move("cols", cols[:, :], P, 9)
            act.wait_ge(s["moved"], upto("rows"))
            nc.scalar.activation(alpha_t[:, :], rowb[:, ROW - H:ROW], ACT.Tanh, scale=0.5).then_inc(s["act_c"], 1)
            for b in range(B):
                move(f"xn{b}", xnT[:, b * N:(b + 1) * N], P, N)
            for t in range(T):
                act.wait_ge(s["qkv_ps"], t + 1)
                copy(qk[:, t, :], bank[t % 2][:, 0:2 * C]).then_inc(s["qk_sb"], 1)
                copy(vaug[:, t, :, 0:D], bank[t % 2][:, 2 * C:3 * C].rearrange("p (h d) -> p h d", d=D)).then_inc(s["v_sb"], 1)
            for b in range(B):
                move(f"x{b}", xT[:, b * N:(b + 1) * N], P, N)

            def squares(b):
                act.wait_ge(s["dsub"], b + 1)
                nc.scalar.activation(sqd[:, b], diff[:, b], ACT.Square).then_inc(s["dsq"], 1)

            def exps(b):
                act.wait_ge(s["fmax_s"], b + 1)
                nc.scalar.activation(sqd[:, b], diff[:, b], ACT.Exp).then_inc(s["fexp"], 1)

            squares(0)
            squares(1)
            move("qT0", qT[:, 0:N], P, N)
            move("kT0", kT[:, 0:N], P, N)
            move("proj", wprojT[:, :], P, C)
            move("wk_wv", wkvT[:, :, :].rearrange("p a b -> p (a b)"), P, 2 * C)
            move("wih", wihT[:, :, :].rearrange("p a b -> p (a b)"), P, 3 * C)
            move("whh", whhT[:, :, :].rearrange("p a b -> p (a b)"), P, 3 * C)
            move("wa0", waT[:, :, :].rearrange("p a b -> p (a b)"), P, N)
            for k in range(2):
                move(f"wb{k}", wbT[:, 2 * k:2 * k + 2].rearrange("p a f b -> p (a f b)"), P, N)
            for k in range(4):
                move(f"wup{k}", wupT[:, 4 * k:4 * k + 4, :].rearrange("p a b -> p (a b)"), P, N)
            for k in range(4):
                move(f"wdn{k}", wdnT[:, 2 * k:2 * k + 2].rearrange("p a f b -> p (a f b)"), P, N)
            move("ctx", pnT[:, :], P, B * M)
            move("kproj", kpT[:, :], P, B * M)
            move("qk_fold", fold[:, :], P, B * M)
            move("vproj", vp[:, :, :].rearrange("p a b -> p (a b)"), M, B * C)
            move("qT1", qT[:, N:2 * N], P, N)
            move("kT1", kT[:, N:2 * N], P, N)
            exps(0)
            exps(1)
            move("qf0", qfT[:, 0:N], P, N)
            move("qf1", qfT[:, N:2 * N], P, N)

            def scores_out(h, p, first=False):
                for w in range(2):
                    j = 2 * p + w
                    act.wait_ge(s["scores_ps"], h * TPB + j + 1)
                    if not first:
                        act.wait_ge(s["masked"], h * TPB + j - TPB + 1)
                        act.wait_ge(s["exp_done"], h * TPB + j - TPB + 1)
                    nc.scalar.activation(S[j], bank[w][:, :], ACT.Copy, scale=float(D) ** -0.5
                                         ).then_inc(s["scores_sb"], 1)

            def turned_out(h, p):
                for w in range(2):
                    j = 2 * p + w
                    act.wait_ge(s["pt_ps"], h * TPB + j + 1)
                    act.wait_ge(s["av_done"], h * TPB + j + 1)
                    copy(PT[w][:, :], bank[2 + w][:, :]).then_inc(s["pt_sb"], 1)

            def exponentials(h, p, first=False):
                act.wait_ge(s["negmax_s"], h * 2 + p + 1)
                if not first:
                    act.wait_ge(s["pt_ps"], h * TPB + 2 * p - TPB + 2)
                    act.wait_ge(s["z_saved"], h)
                for w in range(2):
                    j = 2 * p + w
                    act.wait_ge(s["scores_sb"], h * TPB + j + 1)
                    nc.scalar.activation(E[j], S[j], ACT.Exp, bias=negmax[j][:, :],
                                         accum_out=zb[:, j:j + 1]).then_inc(s["exp_done"], 1)

            act.sem_inc(s["pt_sb"], 2)
            act.sem_inc(s["av_done"], 2)
            for p in range(2):
                scores_out(0, p, first=True)
                exponentials(0, p, first=True)
            with act.Fori(1, BH) as h:
                for p in range(2):
                    scores_out(h, p)
                    turned_out(h - 1, p)
                    exponentials(h, p)
            for p in range(2):
                turned_out(BH - 1, p)

            for b in range(B):
                act.wait_ge(s["ot_ps"], b + 1)
                copy(oT[:, b, :], work(b, 0)).then_inc(s["ot_sb"], 1)

            def layer_norm(k):
                for b in range(B):
                    act.wait_ge(s["ln_d"], 2 * k + b + 1)
                    nc.scalar.activation(sqT[:, b, :], dT[:, b, :], ACT.Square).then_inc(s["ln_q"], 1)
                for b in range(B):
                    act.wait_ge(s["ln_v"], 2 * k + b + 1)
                    nc.scalar.activation(vT[:, b, :], work(b, 2), ACT.Copy, bias=LN_EPS).then_inc(s["ln_e"], 1)

            layer_norm(0)
            for it in range(ITERS):
                for b in range(B):
                    if it == 0:
                        act.wait_ge(s["ln_h"], b + 1)
                        act.wait_ge(s["ln_v"], b + 1)
                    else:
                        act.wait_ge(s["slot_s"], 2 * (it - 1) + b + 1)
                        act.wait_ge(s["ms_ps"], 2 * (it - 1) + b + 1)
                    nc.scalar.activation(sqT[:, b, :], slots[:, b, :], ACT.Square).then_inc(s["sl_sq"], 1)
                for b in range(B):
                    act.wait_ge(s["ms_ps"], 2 * it + b + 1)
                    if it:
                        act.wait_ge(s["rn_s"], 2 * (it - 1) + b + 1)
                    nc.scalar.activation(mse[:, b, :], work(b, 0)[0:M, :], ACT.Copy, bias=RMS_EPS).then_inc(s["ms_sb"], 1)
                for b in range(B):
                    act.wait_ge(s["snm_s"], 2 * it + b + 1)
                    if it:
                        act.wait_ge(s["at_s"], 2 * (it - 1) + b + 1)
                    nc.scalar.activation(ex[:, b, :], sc[:, b, :], ACT.Exp, bias=snm[:, b:b + 1], scale=SCALE,
                                         accum_out=ssum[:, b:b + 1]).then_inc(s["ex_s"], 1)
                for b in range(B):
                    act.wait_ge(s["g_ps"], 2 * it + b + 1)
                    if it:
                        act.wait_ge(s["slot_s"], 2 * (it - 1) + b + 1)
                    nc.scalar.activation(rt[:, b, :], work(b, 2), ACT.Tanh, bias=half_rz[:, 0:1], scale=0.5).then_inc(s["gate_s"], 1)
                    nc.scalar.activation(hw[:, b, :], work(b, 0), ACT.Identity, bias=half_hn[:, :], scale=0.5).then_inc(s["gate_s"], 1)
                    nc.scalar.activation(zt[:, b, :], work(b, 3), ACT.Tanh, bias=half_rz[:, 1:2], scale=0.5).then_inc(s["gate_s"], 1)
                for b in range(B):
                    act.wait_ge(s["t2_s"], 2 * it + b + 1)
                    nc.scalar.activation(nn[:, b, :], t2[:, b, :], ACT.Tanh, bias=cols[:, 5:6]).then_inc(s["n_s"], 1)
            layer_norm(1)

            for b in range(B):
                for c in range(4):
                    act.wait_ge(s["ga_ps"], 4 * b + c + 1)
                    copy(gh[b][:, c, :], bank[c % 2][:, :]).then_inc(s["gh_s"], 1)
                    nc.scalar.activation(sqg[b][:, c, :], bank[c % 2][:, :], ACT.Square).then_inc(s["gh_s"], 1)
                act.wait_ge(s["x2_ps"], b + 1)
                copy(acc[:, b].rearrange("p j c -> p (j c)"), bank[3][:, :]).then_inc(s["x2_tok"], 1)
                for k in range(2 * EXPERTS):
                    kk = 2 * EXPERTS * b + k
                    act.wait_ge(s["gu_ps"], kk + 1)
                    if kk >= 2:
                        act.wait_ge(s["a2_s"], kk - 1)
                    nc.scalar.activation(th[k % 2][:, :], ob(k % 2), ACT.Tanh, scale=0.5).then_inc(s["th_s"], 1)
                    if k == 0:
                        act.wait_ge(s["sd_s"], b + 1)
                        nc.scalar.activation(sexp[:, b, :], sdif[:, b, :], ACT.Exp).then_inc(s["se_s"], 1)

        @block.vector
        def _(dve):
            v = nc.vector
            n = [0]

            def link(ins):
                n[0] += 1
                ins.then_inc(s["dchain"], 1)
                dve.wait_ge(s["dchain"], n[0])

            v.memset(minus_half[:, :], -0.5)
            v.memset(plus_half[:, :], 0.5)
            v.memset(mean_mat[:, :], 1.0 / C)
            v.memset(ones_m[:, :], 1.0)
            v.memset(vaug[:, :, :, D:DV], 1.0)
            for e in range(EXPERTS):
                v.memset(iota8[:, e:e + 1], float(e))
            v.memset(blk[:, :, :], 0.0)
            v.memset(blockmask[:, :, :], 1.0)
            link(v.memset(ones_row[:, :], 1.0))
            dve.sem_inc(s["small"], 1)

            for b in range(B):
                dve.wait_ge(s[f"x{b}_in"], 16)
                for j in range(TPB):
                    t = b * TPB + j
                    v.bn_stats(stats[:, t, :], x_sb[:, t, :]).then_inc(s["stat_s"], 1)
                for j in range(TPB):
                    t = b * TPB + j
                    dve.wait_ge(s["stat_s"], t + 1)
                    v.bn_aggr(mv[:, t, :], stats[:, t, :]).then_inc(s["mv_s"], 1)
                dve.wait_ge(s["mv_s"], TPB * (b + 1))
                v.tensor_scalar(veps1[:, b * TPB:(b + 1) * TPB], mv[:, b * TPB:(b + 1) * TPB, 1], LN_EPS, None,
                                ALU.add).then_inc(s["veps_s"], 1)
            for b in range(B):
                dve.wait_ge(s["rstd_s"], b + 1)
                for j in range(TPB):
                    t = b * TPB + j
                    v.tensor_scalar(xn[:, t, :], x_sb[:, t, :], mv[:, t, 0:1], rstd1[:, t:t + 1],
                                    ALU.subtract, ALU.mult).then_inc(s["xn_s"], 1)
            dve.wait_ge(s["consts"], 1)
            for c in range(4):
                v.tensor_copy(blk[:, c, 2 * c:2 * c + 2], halves[:, :])
            for h in range(0, H):
                v.tensor_scalar(blockmask[:, h, :], blockmask[:, h, :], headmask[:, h:h + 1], None, ALU.mult)
            dve.wait_ge(s["moved"], upto("cols"))
            for i in range(2):
                for dst, o in ((gammab, 3 * C), (betab, 3 * C + 2 * D)):
                    v.tensor_copy(dst[:, i], rowb[:, o + i * D:o + (i + 1) * D].rearrange("p (o d) -> p o d", o=1)
                                  .to_broadcast([P, H, D]))
            link(v.tensor_tensor(brz[:, :], cols[:, 3:5], cols[:, 6:8], ALU.add))
            v.tensor_scalar(half_rz[:, :], brz[:, :], 0.5, None, ALU.mult)
            v.tensor_scalar(half_hn[:, :], cols[:, 8:9], 0.5, None, ALU.mult)
            dve.wait_ge(s["act_c"], 1)
            v.tensor_scalar(mix[:, 0, :], alpha_t[:, :], 0.5, 0.5, ALU.mult, ALU.add)
            link(v.tensor_scalar(mix[:, 1, :], alpha_t[:, :], -0.5, 0.5, ALU.mult, ALU.add))
            dve.wait_ge(s["achain"], 1)
            v.tensor_scalar(cms[:, :], css[:, :], 1.0 / C, RMS_EPS, ALU.mult, ALU.add).then_inc(s["csum_s"], 1)
            dve.wait_ge(s["cpow_s"], 1)
            v.tensor_scalar(pn[:, :], ctx_sb[:, :], crs[:, :], None, ALU.mult).then_inc(s["pn_s"], 1)

            def groups(ap):
                return ap.rearrange("p (g d) -> p g d", d=D)

            def each(ap):
                return ap.rearrange("p (g o) -> p g o", o=1).to_broadcast([P, GR, D])

            def qk_flat(b):
                return qk[:, TPB * b:TPB * (b + 1), :].rearrange("p t c -> p (t c)")

            for b in range(B):
                dve.wait_ge(s["qk_sb"], TPB * (b + 1))
                link(v.tensor_reduce(gsum[:, b], groups(qk_flat(b)), op=ALU.add, axis=AX.X))
                link(v.tensor_scalar(gmean[:, b], gsum[:, b], 1.0 / D, None, ALU.mult))
                v.tensor_tensor(groups(diff[:, b]), groups(qk_flat(b)), each(gmean[:, b]), ALU.subtract).then_inc(s["dsub"], 1)
            for b in range(B):
                dve.wait_ge(s["dsq"], b + 1)
                link(v.tensor_reduce(gvar[:, b], groups(sqd[:, b]), op=ALU.add, axis=AX.X))
                v.tensor_scalar(gveps[:, b], gvar[:, b], 1.0 / D, LN_EPS, ALU.mult, ALU.add).then_inc(s["dvar"], 1)
            for b in range(B):
                dve.wait_ge(s["dpow"], b + 1)
                dve.wait_ge(s["dsub"], b + 1)
                link(v.tensor_tensor(groups(qk_flat(b)), groups(diff[:, b]), each(grstd[:, b]), ALU.mult))
                x3 = qk[:, TPB * b:TPB * (b + 1), :]
                for last, table, op in ((False, gammab, ALU.mult), (True, betab, ALU.add)):
                    tb = table[:, :, :, :].rearrange("p (o a) h d -> p o (a h d)", o=1).to_broadcast([P, TPB, 2 * C])
                    ins = v.tensor_tensor(x3, x3, tb, op)
                    if last:
                        ins.then_inc(s["qk_ready"], 1)
                    else:
                        link(ins)
            for b in range(B):
                dve.wait_ge(s["qk_ready"], b + 1)
                link(v.tensor_reduce(gmax[:, b], groups(qk_flat(b)), op=ALU.max, axis=AX.X))
                v.tensor_tensor(groups(diff[:, b]), groups(qk_flat(b)), each(gmax[:, b]), ALU.subtract).then_inc(s["fmax_s"], 1)
            dve.wait_ge(s["moved"], upto("ctx"))
            v.tensor_scalar(pnTw[:, :], pnT[:, :], cols[:, 2:3], None, ALU.mult).then_inc(s["pnw_s"], 1)
            for b in range(B):
                dve.wait_ge(s["fexp"], b + 1)
                link(v.tensor_reduce(gden[:, b], groups(sqd[:, b]), op=ALU.add, axis=AX.X))
                link(v.reciprocal(grec[:, b], gden[:, b]))
                v.tensor_tensor(groups(feat[:, TPB * b:TPB * (b + 1), :].rearrange("p t c -> p (t c)")), groups(sqd[:, b]),
                                each(grec[:, b]), ALU.mult).then_inc(s["fready"], 1)
            dve.wait_ge(s["moved"], upto("qk_fold"))
            link(v.tensor_scalar(foldw[:, :], fold[:, :], cols[:, 1:2], None, ALU.mult))

            OPS = 4 + 3 + 1
            PAIR = 2 * 7 + 2

            def search(h, p, mask_between):
                base = p * PAIR
                done = [0]

                def step(ins):
                    ins.then_inc(s["topk_step"], 1)
                    done[0] += 1

                def after(k):
                    dve.wait_ge(s["topk_step"], base + k)

                for w in range(2):
                    dve.wait_ge(s["scores_sb"], h * TPB + 2 * p + w + 1)
                    dve.sem_inc(s["fence"], 1)
                    step(v.max(top[2 * p + w][:, 0:8], S[2 * p + w]))
                for w in range(2):
                    after(w + 1)
                    step(v.match_replace(W[w][:, :], top[2 * p + w][:, 0:8], S[2 * p + w], REMOVED))
                for w in range(2):
                    j = 2 * p + w
                    ins = v.tensor_scalar(negmax[j][:, :], top[j][:, 0:1], -1.0, None, ALU.mult)
                    if w == 0:
                        step(ins)
                    else:
                        ins.then_inc(s["negmax_s"], 1)
                mask_between()
                for r in range(1, 4):
                    for w in range(2):
                        after(3 + w if r == 1 else 6 + 4 * (r - 2) + 2 + w)
                        step(v.max(top[2 * p + w][:, 8 * r:8 * r + 8], W[w][:, :]))
                    if r < 3:
                        for w in range(2):
                            after(6 + 4 * (r - 1) + w)
                            step(v.match_replace(W[w][:, :], top[2 * p + w][:, 8 * r:8 * r + 8], W[w][:, :], REMOVED))
                assert done[0] == PAIR - 1

            def mask(h, p):
                for w in range(2):
                    j = 2 * p + w
                    dve.wait_ge(s["exp_done"], h * TPB + j + 1)
                    v.scalar_tensor_tensor(out=E[j], in0=S[j], scalar=top[j][:, TOPK - 1:TOPK], in1=E[j],
                                           op0=ALU.is_ge, op1=ALU.mult).then_inc(s["masked"], 1)

            def head(h, first=False):
                search(h, 0, (lambda: None) if first else (lambda: mask(h - 1, 1)))
                search(h, 1, lambda: mask(h, 0))
                dve.wait_ge(s["topk_step"], 2 * (PAIR - 1))
                dve.sem_clear(s["topk_step"])

            head(0, first=True)
            with dve.Fori(1, BH) as h:
                head(h)
            mask(BH - 1, 1)

            for b in range(B):
                dve.wait_ge(s["kv_ps"], b + 1)
                v.tensor_tensor(kvb[:, b, :], work(b, 0)[:, 0:H * DV], blockmask[:, :, :].rearrange("p h e -> p (h e)"),
                                ALU.mult).then_inc(s["kv_sb"], 1)
            dve.wait_ge(s["av_done"], BH * TPB + 2)
            dve.wait_ge(s["z_saved"], BH)
            for b in range(B):
                dve.wait_ge(s["ol_ps"], b + 1)
                for u in range(2):
                    osum = work(b, 2 + u)[:, 0:2 * H * DV].rearrange("p (j h e) -> p j h e", h=H, e=DV)
                    lin = work(b, u)[:, 0:2 * H * DV].rearrange("p (j h e) -> p j h e", h=H, e=DV)
                    z = zall[:, b * H:(b + 1) * H, 2 * u:2 * u + 2].rearrange("p h j -> p j h")
                    v.scalar_tensor_tensor(out=den[:, b, 0, 2 * u:2 * u + 2, :], in0=z, scalar=ATT_EPS, in1=osum[:, :, :, D],
                                           op0=ALU.mult, op1=ALU.add)
                    ins = v.tensor_scalar(den[:, b, 1, 2 * u:2 * u + 2, :], lin[:, :, :, D], LIN_EPS, None, ALU.add)
                link(ins)
                link(v.reciprocal(rden[:, b].rearrange("p a j h -> p (a j h)"), den[:, b].rearrange("p a j h -> p (a j h)")))
                for a in range(2):
                    ins = v.tensor_tensor(wden[:, b, a], rden[:, b, a],
                                          mix[:, a, :].rearrange("p (o h) -> p o h", o=1).to_broadcast([P, TPB, H]), ALU.mult)
                link(ins)
                for u in range(2):
                    for a, dst in ((0, o_s), (1, o_l)):
                        src = work(b, 2 + u if a == 0 else u)[:, 0:2 * H * DV].rearrange("p (n e) -> p n e", e=DV)
                        ins = v.tensor_tensor(
                            dst[:, b, 2 * u:2 * u + 2, :].rearrange("p j (h d) -> p (j h) d", d=D), src[:, :, 0:D],
                            wden[:, b, a, 2 * u:2 * u + 2, :].rearrange("p j (h o) -> p (j h) o", o=1)
                            .to_broadcast([P, 2 * H, D]), ALU.mult)
                link(ins)
                v.tensor_tensor(o_tok[:, b], o_s[:, b], o_l[:, b], ALU.add).then_inc(s["o_ready"], 1)
            for b in range(B):
                dve.wait_ge(s["pr_ps"], b + 1)
                v.scalar_tensor_tensor(out=x1T[:, b, :], in0=work(b, 1), scalar=cols[:, 0:1], in1=xT[:, b * N:(b + 1) * N],
                                       op0=ALU.add, op1=ALU.add).then_inc(s["x1_s"], 1)

            def layer_norm(k, src, dst):
                for b in range(B):
                    dve.wait_ge(s["ln_m"], 2 * k + b + 1)
                    v.tensor_tensor(dT[:, b, :], src[:, b, :], work(b, 0), ALU.subtract).then_inc(s["ln_d"], 1)
                for b in range(B):
                    dve.wait_ge(s["ln_r"], 2 * k + b + 1)
                    dve.wait_ge(s["ln_d"], 2 * k + b + 1)
                    v.tensor_tensor(dst[:, b, :], dT[:, b, :], rT[:, b, :], ALU.mult).then_inc(s["ln_h"], 1)

            dve.wait_ge(s["x1_s"], 2)
            layer_norm(0, x1T, slots)
            for it in range(ITERS):
                for b in range(B):
                    dve.wait_ge(s["rn_s"], 2 * it + b + 1)
                    dve.wait_ge(s["ms_ps"], 2 * it + b + 1)
                    link(v.tensor_tensor(sc[:, b, :], work(b, 1)[0:M, :], rn[:, b, :], ALU.mult))
                    link(v.reduce_max(smax[:, b:b + 1], sc[:, b, :], AX.X))
                    v.tensor_scalar(snm[:, b:b + 1], smax[:, b:b + 1], -SCALE, None, ALU.mult).then_inc(s["snm_s"], 1)
                for b in range(B):
                    dve.wait_ge(s["ex_s"], 2 * it + b + 1)
                    link(v.reciprocal(srec[:, b:b + 1], ssum[:, b:b + 1]))
                    v.tensor_scalar(at[:, b, :], ex[:, b, :], srec[:, b:b + 1], None, ALU.mult).then_inc(s["at_s"], 1)
                for b in range(B):
                    dve.wait_ge(s["du_ps"], 2 * it + b + 1)
                    link(v.tensor_scalar(dde[:, b, :], work(b, 0), RMS_EPS, None, ALU.add))
                    link(v.reciprocal(drc[:, b, :], dde[:, b, :]))
                    v.tensor_tensor(upd[:, b, :], work(b, 1), drc[:, b, :], ALU.mult).then_inc(s["u_s"], 1)
                for b in range(B):
                    dve.wait_ge(s["gate_s"], 6 * it + 3 * b + 2)
                    link(v.scalar_tensor_tensor(out=t1[:, b, :], in0=rt[:, b, :], scalar=1.0, in1=hw[:, b, :],
                                                op0=ALU.add, op1=ALU.mult))
                    v.tensor_tensor(t2[:, b, :], t1[:, b, :], work(b, 1), ALU.add).then_inc(s["t2_s"], 1)
                for b in range(B):
                    dve.wait_ge(s["n_s"], 2 * it + b + 1)
                    dve.wait_ge(s["gate_s"], 6 * it + 3 * b + 3)
                    link(v.tensor_tensor(dd[:, b, :], slots[:, b, :], nn[:, b, :], ALU.subtract))
                    link(v.scalar_tensor_tensor(out=ee[:, b, :], in0=zt[:, b, :], scalar=1.0, in1=dd[:, b, :],
                                                op0=ALU.add, op1=ALU.mult))
                    v.scalar_tensor_tensor(out=slots[:, b, :], in0=ee[:, b, :], scalar=0.5, in1=nn[:, b, :],
                                           op0=ALU.mult, op1=ALU.add).then_inc(s["slot_s"], 1)
            for b in range(B):
                dve.wait_ge(s["slot_s"], 2 * (ITERS - 1) + b + 1)
                v.tensor_tensor(x2T[:, b, :], x1T[:, b, :], slots[:, b, :], ALU.add).then_inc(s["slot_s"], 1)
            dve.wait_ge(s["slot_s"], 2 * ITERS + 2)
            layer_norm(1, x2T, hT)

            for b in range(B):
                def add_expert(e):
                    dve.wait_ge(s["y_ps"], b * EXPERTS + e + 1)
                    if e == 0:
                        dve.wait_ge(s["x2_tok"], b + 1)
                    else:
                        dve.wait_ge(s["acc_s"], b * EXPERTS + e)
                    for j in range(TPB):
                        ins = v.scalar_tensor_tensor(out=acc[:, b, j, :], in0=bank[2][:, j * P:(j + 1) * P],
                                                     scalar=wfull[:, b, j, e:e + 1], in1=acc[:, b, j, :],
                                                     op0=ALU.mult, op1=ALU.add)
                    ins.then_inc(s["acc_s"], 1)

                for e in range(EXPERTS):
                    if e == 0:
                        dve.wait_ge(s["sc_ps"], b + 1)
                        v.tensor_copy(s2[:, b].rearrange("p j e -> p (j e)"),
                                      bank[2][:, b * TPB * EXPERTS:(b + 1) * TPB * EXPERTS]).then_inc(s["s2_s"], 1)
                        dve.wait_ge(s["sr_s"], b + 1)
                        for j in range(TPB):
                            ins = v.max(m8[:, b, j, :], sr[:, b, j, :])
                        link(ins)
                        for j in range(TPB):
                            v.max_index(ix[:, b, j, :], m8[:, b, j, :], sr[:, b, j, :])
                        link(v.tensor_tensor(sdif[:, b, :], m8[:, b, :, 1], m8[:, b, :, 0], ALU.subtract))
                        dve.sem_inc(s["sd_s"], 1)
                        link(v.tensor_copy(ixf[:, b, :, :], ix[:, b, :, 0:2]))
                    for f in range(2):
                        k = 2 * (b * EXPERTS + e) + f
                        dve.wait_ge(s["th_s"], k + 1)
                        if e >= 2:
                            dve.wait_ge(s["y_ps"], b * EXPERTS + e - 1)
                        elif b:
                            dve.wait_ge(s["y_ps"], b * EXPERTS + e - 1 if e else b * EXPERTS - 1)
                        link(v.scalar_tensor_tensor(out=a1[f][:, :], in0=th[f][:, :], scalar=1.0, in1=ob(f),
                                                    op0=ALU.add, op1=ALU.mult))
                        v.tensor_tensor(a2[2 * (e % 2) + f], a1[f][:, :], ob(2 + f), ALU.mult).then_inc(s["a2_s"], 1)
                    if e == 0:
                        dve.wait_ge(s["se_s"], b + 1)
                        link(v.tensor_scalar(spl[:, b, :], sexp[:, b, :], 1.0, None, ALU.add))
                        link(v.reciprocal(srecp[:, b, :], spl[:, b, :]))
                        link(v.tensor_scalar(w12[:, b, 0, :], srecp[:, b, :], 0.5, None, ALU.mult))
                        link(v.tensor_tensor(w12[:, b, 1, :], w12[:, b, 0, :], sexp[:, b, :], ALU.mult))
                        for i in range(2):
                            ins = v.tensor_tensor(eq[:, b, i], iota8[:, :].rearrange("p (o e) -> p o e", o=1).to_broadcast([P, TPB, EXPERTS]),
                                                  ixf[:, b, :, i:i + 1].to_broadcast([P, TPB, EXPERTS]), ALU.is_equal)
                        link(ins)
                        for i in range(2):
                            ins = v.tensor_tensor(ew[:, b, i], eq[:, b, i],
                                                  w12[:, b, i, :].rearrange("p (j o) -> p j o", o=1).to_broadcast([P, TPB, EXPERTS]), ALU.mult)
                        link(ins)
                        link(v.tensor_tensor(wfull[:, b], ew[:, b, 0], ew[:, b, 1], ALU.add))
                    else:
                        add_expert(e - 1)
                add_expert(EXPERTS - 1)


_INS = ["x", "ctx_1024", "L0_attn_Wqkv", "L0_attn_bqkv", "L0_attn_q_gamma", "L0_attn_q_beta", "L0_attn_k_gamma",
        "L0_attn_k_beta", "L0_attn_alpha", "L0_attn_Wproj", "L0_attn_bproj", "L0_xattn_Wq", "L0_xattn_Wk",
        "L0_xattn_Wv", "L0_xattn_gru_wih", "L0_xattn_gru_whh", "L0_xattn_gru_bih", "L0_xattn_gru_bhh",
        "L0_xattn_slot_norm_w", "L0_xattn_input_norm_w", "L0_ffn_W_A", "L0_ffn_W_B", "L0_ffn_W_up", "L0_ffn_W_down"]
_OUTS = [((2, 512, 128), "float32")]


def kernel(**inputs):
    import numpy as _np
    import concourse.bacc as _bacc
    from concourse import mybir as _mybir
    from concourse.bass_utils import run_bass_kernel_spmd as _run

    nc = _bacc.Bacc("TRN2", target_bir_lowering=False, num_devices=1)
    arrays, args = {}, []
    for name in _INS:
        a = _np.ascontiguousarray(inputs[name])
        arrays[f"in_{name}_dram"] = a
        args.append(nc.dram_tensor(f"in_{name}_dram", a.shape, _mybir.dt.from_np(a.dtype), kind="ExternalInput").ap())
    for i, (shape, dtype) in enumerate(_OUTS):
        dt = _mybir.dt.from_np(_np.dtype(dtype))
        args.append(nc.dram_tensor(f"out_{i}_dram", shape, dt, kind="ExternalOutput").ap())
    build(nc, *args)
    r = _run(nc, [arrays], core_ids=[0])
    got = tuple(r.results[0][f"out_{i}_dram"] for i in range(len(_OUTS)))
    return got[0]
```

```python
import concourse.bass as bass
from concourse import mybir
from contextlib import ExitStack

F32 = mybir.dt.float32
U32 = mybir.dt.uint32
ALU = mybir.AluOpType
ACT = mybir.ActivationFunctionType
AX = mybir.AxisListType

B, N, C = 2, 512, 128
H = 16
D = C // H
DV = D + 1
M = 32
EXPERTS, RANK, FF = 8, 64, 256
ITERS = 3
P = 128
TPB = N // P
T = B * TPB
TOPK = max(1, int(N * 0.05))
BH = B * H
LN_EPS, RMS_EPS, ATT_EPS, LIN_EPS = 1e-5, 1e-6, 1e-8, 1e-6
SCALE = C ** -0.5
REMOVED = -3.0e38
CHUNKS = 16
CHUNK = N // CHUNKS

GROUPS = (["wqkv", "rows", "cols", "xn0", "xn1", "x0", "x1", "proj", "wk_wv", "ctx", "kproj", "qk_fold", "vproj", "wih", "whh", "wa"]
          + [f"wb{i}" for i in range(2)] + ["qT0", "kT0"] + [f"wup{i}" for i in range(4)] + ["qT1", "kT1"]
          + [f"wdn{i}" for i in range(4)] + ["qf0", "qf1"])


def upto(name):
    return GROUPS.index(name) + 1


def build(nc, x, ctx_in, Wqkv, bqkv, q_gamma, q_beta, k_gamma, k_beta, alpha, Wproj, bproj, Wq, Wk, Wv,
          wih, whh, bih, bhh, slot_w, input_w, W_A, W_B, W_up, W_down, out):
    ctx = ExitStack()
    with ctx:
        def sb(name, shape, dt=F32):
            return ctx.enter_context(nc.sbuf_tensor(name, shape, dt))

        def sem(name):
            return ctx.enter_context(nc.semaphore(name))

        x_sb = sb("x_sb", [P, T, C])
        ctx_sb = sb("ctx_sb", [B * M, C])
        wqkv = sb("wqkv", [P, 3, C])
        wproj, wq, wk, wv = (sb(n, [C, C]) for n in ("wproj", "wq", "wk", "wv"))
        wih_sb, whh_sb = sb("wih_sb", [P, 3, C]), sb("whh_sb", [P, 3, C])
        wa_sb = sb("wa_sb", [P, 4, C])
        wb_sb = sb("wb_sb", [P, 4, 2, P])
        wup_sb = sb("wup_sb", [P, 16, C])
        wdn_sb = sb("wdn_sb", [P, EXPERTS, FF])
        ROW = 3 * C + 4 * D + H
        row = sb("row", [1, ROW])
        cols_in = sb("cols_in", [9, C])

        ident = sb("ident", [P, P])
        headmask = sb("headmask", [P, H])
        blockmask = sb("blockmask", [P, H, DV])
        halves = sb("halves", [P, 2])
        blk = sb("blk", [P, 4, EXPERTS])
        ones_row = sb("ones_row", [1, P])
        mean_mat = sb("mean_mat", [P, P])
        ones_m = sb("ones_m", [M, P])
        minus_half = sb("minus_half", [P, 1])
        plus_half = sb("plus_half", [P, 1])
        iota8 = sb("iota8", [P, EXPERTS])

        wqkvT = sb("wqkvT", [C, 3 * C])
        rowb = sb("rowb", [P, ROW])
        cols = sb("cols", [C, 9])
        wprojT = sb("wprojT", [C, C])
        wkvT = sb("wkvT", [C, 2, C])
        wihT, whhT = sb("wihT", [C, 3, C]), sb("whhT", [C, 3, C])
        waT = sb("waT", [C, 4, P])
        wbT = sb("wbT", [P, 4, 2, P])
        wupT = sb("wupT", [C, 16, P])
        wdnT = sb("wdnT", [P, EXPERTS, 2, C])
        half_rz = sb("half_rz", [C, 2])
        half_hn = sb("half_hn", [C, 1])
        brz = sb("brz", [C, 2])
        gammab, betab = sb("gammab", [P, 2, H, D]), sb("betab", [P, 2, H, D])
        alpha_t = sb("alpha_t", [P, H])
        mix = sb("mix", [P, 2, H])

        stats = sb("stats", [P, T, 6])
        mv = sb("mv", [P, T, 2])
        veps1 = sb("veps1", [P, T])
        rstd1 = sb("rstd1", [P, T])
        xn = sb("xn", [P, T, C])
        xnT, xT = sb("xnT", [C, B * N]), sb("xT", [C, B * N])
        qk = sb("qk", [P, T, 2 * C])
        vaug = sb("vaug", [P, T, H, DV])
        GR = TPB * 2 * H
        gsum, gmean, gvar, gveps, grstd = (sb(n, [P, B, GR]) for n in ("gsum", "gmean", "gvar", "gveps", "grstd"))
        gmax, gden, grec = (sb(n, [P, B, GR]) for n in ("gmax", "gden", "grec"))
        gstd, grough, gprod, gfix = gmax, gden, grec, gmean
        diff = sb("diff", [P, B, TPB * 2 * C])
        sqd = sb("sqd", [P, B, TPB * 2 * C])
        feat = sb("feat", [P, T, 2 * C])
        qT, kT, qfT = sb("qT", [C, B * N]), sb("kT", [C, B * N]), sb("qfT", [C, B * N])

        qm = [sb(f"qm{i}", [C, 2 * P]) for i in range(2)]
        S_all, E_all = sb("S_all", [P, TPB, N]), sb("E_all", [P, TPB, N])
        S = [S_all[:, i, :] for i in range(TPB)] + [diff[:, i // 2, (i % 2) * N:(i % 2 + 1) * N] for i in range(TPB)]
        W_all, PT_all = sb("W_all", [P, 2, N]), sb("PT_all", [P, 2, N])
        W = [W_all[:, i, :] for i in range(2)]
        E = [E_all[:, i, :] for i in range(TPB)]
        PT = [PT_all[:, i, :] for i in range(2)]
        lead = [sb(f"lead{i}", [P, 2, CHUNKS, 8]) for i in range(2)]
        upper = [sb(f"upper{i}", [P, 2, 32]) for i in range(2)]
        lower = [sb(f"lower{i}", [P, 2, 9]) for i in range(2)]
        rest = sb("rest", [P, 2, CHUNKS * 3])
        cand = sb("cand", [P, 2, 9])
        thr = [sb(f"thr{i}", [P, 2]) for i in range(4)]
        above = sb("above", [P, 2])
        eighth = sb("eighth", [P, 2])
        bound = sb("bound", [P, 2])
        missed = [sb(f"missed{i}", [P, 1]) for i in range(2)]
        flags = sb("flags", [1, 1], mybir.dt.int32)
        top = sb("top", [P, 32])
        negmax = [sb(f"negmax{i}", [P, 2]) for i in range(4)]
        keep = [sb(f"keep{i}", [P, N], mybir.dt.bfloat16) for i in range(2)]
        zb = sb("zb", [P, 8])
        zall = sb("zall", [P, BH // 2, 8])
        ones_col = sb("ones_col", [P, 1])

        kvb = sb("kvb", [P, B, H * DV])
        den = sb("den", [P, B, 2, TPB, H])
        rden = sb("rden", [P, B, 2, TPB, H])
        wden = sb("wden", [P, B, 2, TPB, H])
        o_tok = sb("o_tok", [P, B, TPB, C])
        o_s, o_l = (a[:, :, :].rearrange("p (b j) c -> p b j c", b=B) for a in (x_sb, xn))
        oT = sb("oT", [C, B, N])
        x1T, x2T = sb("x1T", [C, B, N]), sb("x2T", [C, B, N])
        dT, sqT = sqd[:, :, N:2 * N], sqd[:, :, 0:N]
        veps_t, rstd_t, mse, rn = (sb(n, [P, B, TPB]) for n in ("veps_t", "rstd_t", "mse", "rn"))
        sct = sb("sct", [P, B, TPB, M])
        slots = sb("slots", [C, B, N])
        hT = S_all[:, 0:2, :]
        csq, css, cms, crs = sb("csq", [B * M, C]), sb("css", [B * M, 1]), sb("cms", [B * M, 1]), sb("crs", [B * M, 1])
        pn = sb("pn", [B * M, C])
        pnT = sb("pnT", [C, B * M])
        pnTw = sb("pnTw", [C, B * M])
        kpT = sb("kpT", [C, B * M])
        fold = sb("fold", [C, B * M])
        foldw = sb("foldw", [C, B * M])
        vp = sb("vp", [M, B, C])
        ex, at = (wup_sb[0:M, 8 * i:8 * i + 8, :].rearrange("p (b j) c -> p b (j c)", b=B) for i in range(2))
        smax, snm, ssum, srec = (sb(n, [M, B]) for n in ("smax", "snm", "ssum", "srec"))
        dde, drc = (a[:, :, :].rearrange("p (b j) c -> p b (j c)", b=B) for a in (x_sb, xn))
        upd = xnT[:, :].rearrange("p (b n) -> p b n", b=B)
        zt, ee = (a[:, :].rearrange("p (b n) -> p b n", b=B) for a in (qT, kT))
        rt, dd = (wdn_sb[:, 4 * i:4 * i + 4, :].rearrange("p (b j) c -> p b (j c)", b=B) for i in range(2))
        hw, t1, t2, nn = S_all[:, 0:2, :], S_all[:, 2:4, :], E_all[:, 0:2, :], E_all[:, 2:4, :]
        gh = [a[:, :, :].rearrange("p (k i) c -> p k (i c)", i=2) for a in (qk, feat)]
        sqg = [wup_sb[:, :, :].rearrange("p (k i) c -> p k (i c)", i=4), wdn_sb[:, :, :].rearrange("p (k i) c -> p k (i c)", i=2)]
        s2, sr = sb("s2", [P, B, TPB, EXPERTS]), sb("sr", [P, B, TPB, EXPERTS])
        m8 = sb("m8", [P, B, TPB, EXPERTS])
        ix = sb("ix", [P, B, TPB, EXPERTS], U32)
        ixf = sb("ixf", [P, B, TPB, 2])
        sdif, sexp, spl, srecp = (sb(n, [P, B, TPB]) for n in ("sdif", "sexp", "spl", "srecp"))
        w12 = sb("w12", [P, B, 2, TPB])
        eq = sb("eq", [P, B, 2, TPB, EXPERTS])
        ew = sb("ew", [P, B, 2, TPB, EXPERTS])
        wfull = sb("wfull", [P, B, TPB, EXPERTS])
        th, a1, a2 = PT, W, E
        acc = o_tok

        bank = [ctx.enter_context(nc.psum_tensor(f"bank{i}", [P, 512], F32)) for i in range(4)]
        obank = ctx.enter_context(nc.psum_tensor("obank", [P, 3 * 512], F32))
        flagbank = ctx.enter_context(nc.psum_tensor("flagbank", [P, 512], F32))

        def ob(i):
            return obank[:, i * 512:(i + 1) * 512] if i < 3 else flagbank[:, :]

        def o_at(t):
            return (t // 3) * 512 + (t % 3) * H * DV

        def work(b, i):
            return bank[2 * b + i][:, :] if i < 2 else ob((0, 3, 1, 2)[2 * b + i - 2])

        PAIRS = BH * TPB // 2

        def pair(m, q):
            m, q = m + q // 4, q % 4
            if isinstance(m, int) and not 0 <= 4 * m + q < PAIRS:
                return None
            return m, q

        def g_of(pr):
            return 4 * pr[0] + pr[1]

        def head_of(pr):
            h = 2 * pr[0] + pr[1] // 2
            return (h // H, h % H) if isinstance(h, int) else ((h >> 4) & 1, h & (H - 1))

        names = """x0_in x1_in wqkv_in rows_in cols_in_s ctx_in_s att_in xw_in ffa_in ffb_in ffu_in ffd_in consts small
            fence stat_s mv_s veps_s rstd_s xn_s group_ps moved qkv_ps qk_sb v_sb
            lnq dsub dsq dvar gstd_s qk_ready fmax_s fexp fready scal_c act_c csum_s cpow_s pn_s pnw_s kp_w
            qm_ready scores_ps scores_sb negmax_s exp_done masked pt_ps pt_sb av_done z_saved topk_step lead_s keep_s missed_s flags_s flag_ps cut_s redo
            kv_ps kv_sb ol_ps o_ready ot_ps ot_sb pr_ps x1_s ln_m ln_d ln_q ln_v ln_e ln_r ln_b ln_h
            sl_sq ms_ps ms_sb rn_s sct_s sc_t snm_s ex_s at_s du_ps u_s g_ps gate_s hw_s t2_s n_s slot_s
            ga_ps gh_s sc_ps s2_s sr_s sd_s se_s wf_s gu_ps th_s a2_s y_ps acc_s x2_ps x2_tok out_s
            dchain pchain achain""".split()
        s = {n: sem(n) for n in names}

        block = ctx.enter_context(nc.Block())

        @block.sync
        def _(sp):
            for b in range(B):
                sp.dma_start(x_sb[:, TPB * b:TPB * (b + 1), :],
                             x[b].rearrange("(j p) c -> p j c", p=P)).then_inc(s[f"x{b}_in"], 16)
            for r, src in enumerate((bproj, slot_w, input_w)):
                sp.dma_start(cols_in[r:r + 1, :], src.rearrange("(o n) -> o n", o=1)).then_inc(s["cols_in_s"], 16)
            for r, src in ((3, bih), (6, bhh)):
                sp.dma_start(cols_in[r:r + 3, :], src.rearrange("(o n) -> o n", o=3)).then_inc(s["cols_in_s"], 16)
            sp.dma_start(ctx_sb[:, :], ctx_in.rearrange("b m c -> (b m) c")).then_inc(s["ctx_in_s"], 16)
            for dst, src in ((wproj, Wproj), (wq, Wq), (wk, Wk), (wv, Wv)):
                sp.dma_start(dst[:, :], src).then_inc(s["xw_in"], 16)
            for dst, src in ((wih_sb, wih), (whh_sb, whh)):
                sp.dma_start(dst[:, :, :], src.rearrange("(g p) c -> p g c", p=P)).then_inc(s["xw_in"], 16)
            sp.dma_start(wa_sb[:, :, :], W_A.rearrange("(k e) r c -> (e r) k c", e=2)).then_inc(s["ffa_in"], 16)
            for e in range(2):
                for f in range(2):
                    sp.dma_start(wb_sb[:, :, f, e * RANK:(e + 1) * RANK],
                                 W_B.rearrange("(k e) f r -> e f k r", e=2)[e, f * P:(f + 1) * P]).then_inc(s["ffb_in"], 16)
            sp.dma_start(wup_sb[:, :, :], W_up.rearrange("e (f p) c -> p (e f) c", p=P)).then_inc(s["ffu_in"], 16)
            sp.dma_start(wdn_sb[:, :, :], W_down.rearrange("e h f -> h e f")).then_inc(s["ffd_in"], 16)
            for b in range(B):
                sp.wait_ge(s["acc_s"], (b + 1) * EXPERTS)
                sp.dma_start(out[b].rearrange("(j p) c -> p j c", p=P), acc[:, b]).then_inc(s["out_s"], 16)
            sp.wait_ge(s["out_s"], 16 * B)

        @block.gpsimd
        def _(pool):
            n = [0]

            def link(ins):
                n[0] += 1
                ins.then_inc(s["pchain"], 1)
                pool.wait_ge(s["pchain"], n[0])

            link(nc.gpsimd.memset(ident[:, :], 0.0))
            link(nc.gpsimd.affine_select(out=ident[:, :], in_=ident[:, :], compare_op=ALU.not_equal, fill=1.0,
                                         base=0, pattern=[[-1, P]], channel_multiplier=1))
            link(nc.gpsimd.memset(headmask[:, :], 1.0))
            link(nc.gpsimd.affine_select(out=headmask[:, :], in_=headmask[:, :], compare_op=ALU.is_ge, fill=0.0,
                                         base=0, pattern=[[-D, H]], channel_multiplier=1))
            link(nc.gpsimd.affine_select(out=headmask[:, :], in_=headmask[:, :], compare_op=ALU.is_ge, fill=0.0,
                                         base=D - 1, pattern=[[D, H]], channel_multiplier=-1))
            link(nc.gpsimd.memset(halves[:, :], 1.0))
            link(nc.gpsimd.affine_select(out=halves[:, 0:1], in_=halves[:, 0:1], compare_op=ALU.is_ge, fill=0.0,
                                         base=RANK - 1, pattern=[[0, 1]], channel_multiplier=-1))
            link(nc.gpsimd.affine_select(out=halves[:, 1:2], in_=halves[:, 1:2], compare_op=ALU.is_ge, fill=0.0,
                                         base=-RANK, pattern=[[0, 1]], channel_multiplier=1))
            pool.sem_inc(s["consts"], 1)

            def power(dst, src, width, what):
                const = (minus_half if what < 0 else plus_half)[0:src.shape[0], 0:1]
                return nc.gpsimd.tensor_tensor(dst, src, const.to_broadcast([src.shape[0], width]), ALU.pow)

            pool.wait_ge(s["small"], 1)
            for b in range(B):
                pool.wait_ge(s["veps_s"], b + 1)
                t0 = b * TPB
                power(rstd1[:, t0:t0 + TPB], veps1[:, t0:t0 + TPB], TPB, -1).then_inc(s["rstd_s"], 1)
            pool.wait_ge(s["csum_s"], 1)
            power(crs[:, :], cms[:, :], 1, -1).then_inc(s["cpow_s"], 1)

            def mask(pr):
                g, q = g_of(pr), pr[1]
                pool.wait_ge(s["cut_s"], g + 1)
                pool.sem_inc(s["fence"], 1)
                for w in range(2):
                    if pair(pr[0], pr[1] - 1) is not None:
                        pool.wait_ge(s["masked"], 2 * g + w - 1)
                        pool.sem_inc(s["fence"], 1)
                    nc.gpsimd.tensor_scalar(keep[w][:, :], S[2 * q + w], thr[q][:, w:w + 1], None,
                                            ALU.is_ge).then_inc(s["keep_s"], 1)
                for w in range(2):
                    e = E[(2 * q + w) % 4]
                    pool.wait_ge(s["exp_done"], 2 * g + w + 1)
                    pool.sem_inc(s["fence"], 1)
                    pool.wait_ge(s["keep_s"], 2 * g + w + 1)
                    nc.gpsimd.tensor_tensor(e, e, keep[w][:, :], ALU.mult).then_inc(s["masked"], 1)

            for q in range(4):
                mask((0, q))
            with pool.Fori(1, PAIRS // 4) as m:
                for q in range(4):
                    mask((m, q))

            def lns(k):
                for b in range(B):
                    pool.wait_ge(s["ln_e"], 2 * k + b + 1)
                    power(rstd_t[:, b], veps_t[:, b], TPB, -1).then_inc(s["ln_r"], 1)

            lns(0)
            for it in range(ITERS):
                for b in range(B):
                    pool.wait_ge(s["ms_sb"], 2 * it + b + 1)
                    power(rn[:, b], mse[:, b], TPB, -1).then_inc(s["rn_s"], 1)
            lns(1)
            for b in range(B):
                pool.wait_ge(s["s2_s"], b + 1)
                power(sr[:, b].rearrange("p j e -> p (j e)"), s2[:, b].rearrange("p j e -> p (j e)"),
                      TPB * EXPERTS, 1).then_inc(s["sr_s"], 1)

        @block.tensor
        def _(pe):
            g = [0]

            def group():
                if g[0] >= 2:
                    pe.wait_ge(s["moved"], g[0] - 1)
                g[0] += 1
                return bank[2 + (g[0] - 1) % 2]

            def transposes(srcs, rows=P):
                bk = group()
                for i, src in enumerate(srcs):
                    last = nc.tensor.transpose(bk[0:src.shape[1], i * rows:(i + 1) * rows], src, ident[0:rows, 0:rows])
                last.then_inc(s["group_ps"], 1)

            pe.wait_ge(s["consts"], 1)
            pe.wait_ge(s["wqkv_in"], 16)
            transposes([wqkv[:, i, :] for i in range(3)])
            pe.wait_ge(s["rows_in"], 16 * 6)
            pe.wait_ge(s["small"], 1)
            nc.tensor.matmul(group()[:, 0:ROW], ones_row[:, :], row[:, :], start=True, stop=True).then_inc(s["group_ps"], 1)
            pe.wait_ge(s["cols_in_s"], 16 * 5)
            bk = group()
            nc.tensor.transpose(bk[:, 0:9], cols_in[:, :], ident[0:9, 0:9]).then_inc(s["group_ps"], 1)
            for b in range(B):
                pe.wait_ge(s["xn_s"], TPB * (b + 1))
                transposes([xn[:, TPB * b + j, :] for j in range(TPB)])

            def qkv(b):
                pe.wait_ge(s["moved"], upto(f"xn{b}"))
                for j in range(TPB):
                    t = b * TPB + j
                    if t >= 2:
                        pe.wait_ge(s["qk_sb"], t - 1)
                        pe.wait_ge(s["v_sb"], t - 1)
                    nc.tensor.matmul(bank[t % 2][:, 0:3 * C], xnT[:, t * P:(t + 1) * P], wqkvT[:, :],
                                     start=True, stop=True).then_inc(s["qkv_ps"], 1)

            def turned_qk(b):
                pe.wait_ge(s["qk_ready"], b + 1)
                for i in range(2):
                    transposes([qk[:, TPB * b + j, i * C:(i + 1) * C] for j in range(TPB)])

            qkv(0)
            qkv(1)
            for b in range(B):
                transposes([x_sb[:, TPB * b + j, :] for j in range(TPB)])
            pe.wait_ge(s["xw_in"], 16 * 6)
            transposes([wproj[:, :]])
            transposes([wk[:, :], wv[:, :]])
            pe.wait_ge(s["pn_s"], 1)
            transposes([pn[:, :]], rows=B * M)
            pe.wait_ge(s["pnw_s"], 1)
            nc.tensor.matmul(group()[:, 0:B * M], wkvT[:, 0, :], pnTw[:, :], start=True, stop=True).then_inc(s["group_ps"], 1)
            pe.wait_ge(s["moved"], upto("kproj"))
            nc.tensor.matmul(group()[:, 0:B * M], wq[:, :], kpT[:, :], start=True, stop=True).then_inc(s["group_ps"], 1)
            bk = group()
            for b in range(B):
                last = nc.tensor.matmul(bk[0:M, b * C:(b + 1) * C], pnTw[:, b * M:(b + 1) * M], wkvT[:, 1, :],
                                        start=True, stop=True)
            last.then_inc(s["group_ps"], 1)
            transposes([wih_sb[:, i, :] for i in range(3)])
            transposes([whh_sb[:, i, :] for i in range(3)])
            pe.wait_ge(s["ffa_in"], 16)
            transposes([wa_sb[:, i, :] for i in range(4)])
            pe.wait_ge(s["ffb_in"], 16 * 4)
            for k in range(2):
                transposes([wb_sb[:, 2 * k + i // 2, i % 2, :] for i in range(4)])
            turned_qk(0)
            pe.wait_ge(s["ffu_in"], 16)
            for k in range(4):
                transposes([wup_sb[:, 4 * k + i, :] for i in range(4)])
            turned_qk(1)
            pe.wait_ge(s["ffd_in"], 16)
            for k in range(4):
                transposes([wdn_sb[:, 2 * k + i // 2, (i % 2) * P:(i % 2 + 1) * P] for i in range(4)])

            def scores(pr):
                (b, _), g = head_of(pr), g_of(pr)
                pe.wait_ge(s["qm_ready"], g + 1)
                for w in range(2):
                    if pair(pr[0], pr[1] - 1) is not None:
                        pe.wait_ge(s["scores_sb"], 2 * g + w - 1)
                    nc.tensor.matmul(bank[w][:, :], qm[pr[1] % 2][:, w * P:(w + 1) * P], kT[:, bass.ds(b * N, N)],
                                     start=True, stop=True).then_inc(s["scores_ps"], 1)

            def count_missed(pr):
                g = g_of(pr)
                pe.wait_ge(s["missed_s"], g + 1)
                if pair(pr[0], pr[1] - 1) is not None:
                    pe.wait_ge(s["flags_s"], g)
                nc.tensor.matmul(flagbank[0:1, 0:1], ones_col[:, :], missed[pr[1] % 2][:, :], start=True, stop=True
                                 ).then_inc(s["flag_ps"], 1)

            def turn(pr):
                g, q = g_of(pr), pr[1]
                for w in range(2):
                    pe.wait_ge(s["masked"], 2 * g + w + 1)
                    pe.wait_ge(s["pt_sb"], 2 * g + w + 1)
                    for c in range(TPB):
                        last = nc.tensor.transpose(bank[2 + w][:, c * P:(c + 1) * P],
                                                   E[(2 * q + w) % 4][:, c * P:(c + 1) * P], ident[:, :])
                    last.then_inc(s["pt_ps"], 1)

            def weigh(pr):
                (b, h), g, q = head_of(pr), g_of(pr), pr[1]
                for w in range(2):
                    j = 2 * (q % 2) + w
                    pe.wait_ge(s["pt_sb"], 2 * g + w + 3)
                    o = b * (o_at(TPB + j) - o_at(j)) + h * DV + o_at(j)
                    values = vaug[:, :, :, :].rearrange("p t h e -> p (t h e)")
                    for c in range(TPB):
                        last = nc.tensor.matmul(obank[:, bass.ds(o, DV)], PT[w][:, c * P:(c + 1) * P],
                                                values[:, bass.ds(b * (TPB * H * DV) + h * DV + c * H * DV, DV)],
                                                start=(c == 0), stop=(c == TPB - 1))
                    last.then_inc(s["av_done"], 1)

            def slot(m, q):
                for step, ahead in ((count_missed, -1), (turn, -3), (scores, 1), (weigh, -3)):
                    pr = pair(m, q + ahead)
                    if pr is not None:
                        step(pr)

            pe.wait_ge(s["moved"], upto("kT1"))
            pe.wait_ge(s["qk_sb"], T)
            pe.wait_ge(s["v_sb"], T)
            slot(0, -1)
            for b in range(B):
                pe.wait_ge(s["fready"], b + 1)
                transposes([feat[:, TPB * b + j, 0:C] for j in range(TPB)])
            assert g[0] == len(GROUPS)
            pe.wait_ge(s["moved"], len(GROUPS))
            for q in range(4):
                slot(0, q)
            with pe.Fori(1, PAIRS // 4 - 1) as m:
                for q in range(4):
                    slot(m, q)
            for q in range(7):
                slot(PAIRS // 4 - 1, q)

            for b in range(B):
                if b == 0:
                    pe.wait_ge(s["scores_sb"], BH * TPB)
                    pe.wait_ge(s["pt_sb"], BH * TPB + 2)
                for j in range(TPB):
                    last = nc.tensor.matmul(work(b, 0)[:, 0:H * DV], feat[:, TPB * b + j, C:2 * C],
                                            vaug[:, TPB * b + j].rearrange("p h e -> p (h e)"),
                                            start=(j == 0), stop=(j == TPB - 1))
                last.then_inc(s["kv_ps"], 1)
            for b in range(B):
                pe.wait_ge(s["kv_sb"], b + 1)
                for j in range(TPB):
                    last = nc.tensor.matmul(work(b, j // 2)[:, (j % 2) * H * DV:(j % 2 + 1) * H * DV],
                                            qfT[:, (TPB * b + j) * P:(TPB * b + j + 1) * P], kvb[:, b, :],
                                            start=True, stop=True)
                last.then_inc(s["ol_ps"], 1)
            for b in range(B):
                pe.wait_ge(s["o_ready"], b + 1)
                for j in range(TPB):
                    last = nc.tensor.transpose(work(b, 0)[:, j * P:(j + 1) * P], o_tok[:, b, j, :], ident[:, :])
                last.then_inc(s["ot_ps"], 1)
            for b in range(B):
                pe.wait_ge(s["ot_sb"], b + 1)
                nc.tensor.matmul(work(b, 1), wprojT[:, :], oT[:, b, :], start=True, stop=True).then_inc(s["pr_ps"], 1)

            def means(b, i):
                for j in range(TPB):
                    last = nc.tensor.matmul(work(b, i)[:, j:j + 1], sqT[:, b, j * P:(j + 1) * P], mean_mat[:, 0:1],
                                            start=True, stop=True)
                return last

            def layer_norm(k, src, ready, value):
                for b in range(B):
                    pe.wait_ge(s[ready], value + b)
                    nc.tensor.matmul(work(b, 0), mean_mat[:, :], src[:, b, :], start=True, stop=True).then_inc(s["ln_m"], 1)
                for b in range(B):
                    pe.wait_ge(s["ln_q"], 2 * k + b + 1)
                    means(b, 2).then_inc(s["ln_v"], 1)
                for b in range(B):
                    pe.wait_ge(s["ln_r"], 2 * k + b + 1)
                    for j in range(TPB):
                        last = nc.tensor.matmul(work(b, 3)[:, j * P:(j + 1) * P], rstd_t[:, b, j:j + 1].to_broadcast([P, P]),
                                                ident[:, :], start=True, stop=True)
                    last.then_inc(s["ln_b"], 1)

            layer_norm(0, x1T, "x1_s", 1)
            for it in range(ITERS):
                for b in range(B):
                    if it == 0:
                        pe.wait_ge(s["ln_h"], b + 1)
                    else:
                        pe.wait_ge(s["slot_s"], 2 * (it - 1) + b + 1)
                    for j in range(TPB):
                        nc.tensor.matmul(work(b, 1)[:, j * M:(j + 1) * M], slots[:, b, j * P:(j + 1) * P],
                                         foldw[:, b * M:(b + 1) * M], start=True, stop=True)
                    for i in range(2):
                        nc.tensor.matmul(work(b, 2 + i), whhT[:, i, :], slots[:, b, :], start=True, stop=False)
                    pe.wait_ge(s["sl_sq"], 2 * it + b + 1)
                    means(b, 0).then_inc(s["ms_ps"], 1)
                for b in range(B):
                    pe.wait_ge(s["sct_s"], 2 * it + b + 1)
                    for j in range(TPB):
                        last = nc.tensor.transpose(work(b, 0)[0:M, j * P:(j + 1) * P], sct[:, b, j, :], ident[:, :])
                    last.then_inc(s["sc_t"], 1)
                for b in range(B):
                    pe.wait_ge(s["at_s"], 2 * it + b + 1)
                    nc.tensor.matmul(work(b, 0), ones_m[:, :], at[:, b, :], start=True, stop=True)
                    nc.tensor.matmul(work(b, 1), vp[:, b, :], at[:, b, :], start=True, stop=True).then_inc(s["du_ps"], 1)
                for b in range(B):
                    pe.wait_ge(s["u_s"], 2 * it + b + 1)
                    for i in range(2):
                        nc.tensor.matmul(work(b, 2 + i), wihT[:, i, :], upd[:, b, :], start=False, stop=True)
                    nc.tensor.matmul(work(b, 0), whhT[:, 2, :], slots[:, b, :], start=True, stop=True)
                    nc.tensor.matmul(work(b, 1), wihT[:, 2, :], upd[:, b, :], start=True, stop=True).then_inc(s["g_ps"], 1)
            layer_norm(1, x2T, "slot_s", 2 * ITERS + 1)

            for b in range(B):
                pe.wait_ge(s["ln_h"], 2 + b + 1)
                for c in range(4):
                    if c >= 2 or b:
                        pe.wait_ge(s["gh_s"], 2 * (4 * b + c - 1))
                    nc.tensor.matmul(bank[c % 2][:, :], waT[:, c, :], hT[:, b, :], start=True, stop=True).then_inc(s["ga_ps"], 1)
                if b:
                    pe.wait_ge(s["acc_s"], b * EXPERTS)
                for j in range(TPB):
                    for c in range(4):
                        pe.wait_ge(s["gh_s"], 2 * (4 * b + c) + 2)
                        last = nc.tensor.matmul(bank[2][:, (b * TPB + j) * EXPERTS:(b * TPB + j + 1) * EXPERTS],
                                                sqg[b][:, c, j * P:(j + 1) * P], blk[:, c, :], start=(c == 0), stop=(c == 3))
                last.then_inc(s["sc_ps"], 1)
                for j in range(TPB):
                    last = nc.tensor.transpose(bank[3][:, j * P:(j + 1) * P], x2T[:, b, j * P:(j + 1) * P], ident[:, :])
                last.then_inc(s["x2_ps"], 1)

                def down(e):
                    pe.wait_ge(s["a2_s"], 2 * (b * EXPERTS + e) + 2)
                    if b * EXPERTS + e:
                        pe.wait_ge(s["acc_s"], b * EXPERTS + e)
                    for j in range(TPB):
                        for f in range(2):
                            last = nc.tensor.matmul(bank[2][:, j * P:(j + 1) * P], a2[2 * (e % 2) + f][:, j * P:(j + 1) * P],
                                                    wdnT[:, e, f, :], start=(f == 0), stop=(f == 1))
                    last.then_inc(s["y_ps"], 1)

                pe.wait_ge(s["s2_s"], b + 1)
                for e in range(EXPERTS):
                    for f in range(2):
                        k = 2 * (b * EXPERTS + e) + f
                        if k >= 2:
                            pe.wait_ge(s["a2_s"], k - 1)
                        o = (e % 2) * RANK
                        nc.tensor.matmul(ob(f), wbT[o:o + RANK, e // 2, f, :], gh[b][o:o + RANK, e // 2, :], start=True, stop=True)
                        nc.tensor.matmul(ob(2 + f), wupT[:, 2 * e + f, :], hT[:, b, :], start=True, stop=True
                                         ).then_inc(s["gu_ps"], 1)
                    if e:
                        down(e - 1)
                down(EXPERTS - 1)

        @block.scalar
        def _(act):
            act.dma_start(wqkv[:, :, :], Wqkv.rearrange("(g p) c -> p g c", p=P)).then_inc(s["wqkv_in"], 16)
            at_ = 0
            for src, k in ((bqkv, 3 * C), (q_gamma, D), (k_gamma, D), (q_beta, D), (k_beta, D), (alpha, H)):
                act.dma_start(row[:, at_:at_ + k], src.rearrange("(o n) -> o n", o=1)).then_inc(s["rows_in"], 16)
                at_ += k

            g = [0]

            def copy(dst, src):
                return nc.scalar.activation(dst, src, ACT.Copy)

            def move(name, dst, rows, width):
                assert GROUPS[g[0]] == name
                act.wait_ge(s["group_ps"], g[0] + 1)
                copy(dst, bank[2 + g[0] % 2][0:rows, 0:width]).then_inc(s["moved"], 1)
                g[0] += 1

            def flat(ap, pattern):
                return ap.rearrange(pattern)

            act.wait_ge(s["ctx_in_s"], 16)
            nc.scalar.activation(csq[:, :], ctx_sb[:, :], ACT.Square, accum_out=css[:, :]).then_inc(s["achain"], 1)
            move("wqkv", wqkvT[:, :], P, 3 * C)
            move("rows", rowb[:, :], P, ROW)
            move("cols", cols[:, :], P, 9)
            act.wait_ge(s["moved"], upto("rows"))
            nc.scalar.activation(alpha_t[:, :], rowb[:, ROW - H:ROW], ACT.Tanh, scale=0.5).then_inc(s["act_c"], 1)
            for b in range(B):
                move(f"xn{b}", xnT[:, b * N:(b + 1) * N], P, N)
            for b in range(B):
                move(f"x{b}", xT[:, b * N:(b + 1) * N], P, N)

            def squares(b):
                act.wait_ge(s["dsub"], b + 1)
                nc.scalar.activation(sqd[:, b], diff[:, b], ACT.Square).then_inc(s["dsq"], 1)

            def exps(b):
                act.wait_ge(s["fmax_s"], b + 1)
                nc.scalar.activation(sqd[:, b], diff[:, b], ACT.Exp).then_inc(s["fexp"], 1)

            squares(0)
            squares(1)
            for b in range(B):
                act.wait_ge(s["dvar"], b + 1)
                nc.scalar.activation(gstd[:, b], gveps[:, b], ACT.Sqrt).then_inc(s["gstd_s"], 1)
            move("proj", wprojT[:, :], P, C)
            move("wk_wv", wkvT[:, :, :].rearrange("p a b -> p (a b)"), P, 2 * C)
            move("ctx", pnT[:, :], P, B * M)
            move("kproj", kpT[:, :], P, B * M)
            move("qk_fold", fold[:, :], P, B * M)
            move("vproj", vp[:, :, :].rearrange("p a b -> p (a b)"), M, B * C)
            move("wih", wihT[:, :, :].rearrange("p a b -> p (a b)"), P, 3 * C)
            move("whh", whhT[:, :, :].rearrange("p a b -> p (a b)"), P, 3 * C)
            move("wa", waT[:, :, :].rearrange("p a b -> p (a b)"), P, N)
            for k in range(2):
                move(f"wb{k}", wbT[:, 2 * k:2 * k + 2].rearrange("p a f b -> p (a f b)"), P, N)

            def moved_qk(b):
                move(f"qT{b}", qT[:, b * N:(b + 1) * N], P, N)
                move(f"kT{b}", kT[:, b * N:(b + 1) * N], P, N)

            moved_qk(0)
            for k in range(4):
                move(f"wup{k}", wupT[:, 4 * k:4 * k + 4, :].rearrange("p a b -> p (a b)"), P, N)
            moved_qk(1)
            exps(0)
            for k in range(4):
                move(f"wdn{k}", wdnT[:, 2 * k:2 * k + 2].rearrange("p a f b -> p (a f b)"), P, N)
            exps(1)

            def q_mask(pr):
                (b, h), g, p = head_of(pr), g_of(pr), pr[1] % 2
                if pair(pr[0], pr[1] - 2) is not None:
                    act.wait_ge(s["scores_ps"], 2 * g - 2)
                act.sem_inc(s["fence"], 1)
                nc.scalar.activation(qm[p][:, :], qT[:, bass.ds(b * N + p * 2 * P, 2 * P)], ACT.Copy,
                                     scale=headmask[:, bass.ds(h, 1)]).then_inc(s["qm_ready"], 1)

            def scores_out(pr):
                g, q = g_of(pr), pr[1]
                for w in range(2):
                    act.wait_ge(s["scores_ps"], 2 * g + w + 1)
                    if pair(pr[0], q - 4) is not None:
                        act.wait_ge(s["masked"], 2 * g + w - 7)
                    nc.scalar.activation(S[2 * q + w], bank[w][:, :], ACT.Copy, scale=float(D) ** -0.5
                                         ).then_inc(s["scores_sb"], 1)

            def exponentials(pr):
                g, q = g_of(pr), pr[1]
                act.wait_ge(s["negmax_s"], g + 1)
                if pair(pr[0], q - 2) is not None:
                    act.wait_ge(s["pt_ps"], 2 * g - 2)
                if q == 0 and pair(pr[0], q - 1) is not None:
                    act.wait_ge(s["z_saved"], pr[0])
                for w in range(2):
                    nc.scalar.activation(E[(2 * q + w) % 4], S[2 * q + w], ACT.Exp, bias=negmax[q][:, w:w + 1],
                                         accum_out=zb[:, 2 * q + w:2 * q + w + 1]).then_inc(s["exp_done"], 1)
                if q == 3:
                    act.wait_ge(s["exp_done"], 2 * g + 2)
                    act.sem_inc(s["fence"], 1)
                    copy(zall[:, bass.ds(pr[0], 1), :], zb[:, :].rearrange("p (o j) -> p o j", o=1)).then_inc(s["z_saved"], 1)

            def turned_out(pr):
                g = g_of(pr)
                for w in range(2):
                    act.wait_ge(s["pt_ps"], 2 * g + w + 1)
                    act.wait_ge(s["av_done"], 2 * g + w + 1)
                    copy(PT[w], bank[2 + w][:, :]).then_inc(s["pt_sb"], 1)

            def slot(m, q):
                for step, ahead in ((turned_out, -3), (scores_out, 1), (exponentials, -1), (q_mask, 3)):
                    pr = pair(m, q + ahead)
                    if pr is not None:
                        step(pr)

            act.sem_inc(s["pt_sb"], 2)
            act.sem_inc(s["av_done"], 2)
            for q in range(-3, 0):
                slot(0, q)
            move("qf0", qfT[:, 0:N], P, N)
            move("qf1", qfT[:, N:2 * N], P, N)
            for q in range(4):
                slot(0, q)
            with act.Fori(1, PAIRS // 4 - 1) as m:
                for q in range(4):
                    slot(m, q)
            for q in range(7):
                slot(PAIRS // 4 - 1, q)

            for b in range(B):
                act.wait_ge(s["ot_ps"], b + 1)
                copy(oT[:, b, :], work(b, 0)).then_inc(s["ot_sb"], 1)

            def layer_norm(k):
                for b in range(B):
                    act.wait_ge(s["ln_d"], 2 * k + b + 1)
                    nc.scalar.activation(sqT[:, b, :], dT[:, b, :], ACT.Square).then_inc(s["ln_q"], 1)
                for b in range(B):
                    act.wait_ge(s["ln_v"], 2 * k + b + 1)
                    nc.scalar.activation(veps_t[:, b, :], work(b, 2)[:, 0:TPB], ACT.Copy, bias=LN_EPS).then_inc(s["ln_e"], 1)

            layer_norm(0)
            for it in range(ITERS):
                for b in range(B):
                    if it == 0:
                        act.wait_ge(s["ln_h"], b + 1)
                        act.wait_ge(s["ln_v"], b + 1)
                    else:
                        act.wait_ge(s["slot_s"], 2 * (it - 1) + b + 1)
                        act.wait_ge(s["ms_ps"], 2 * (it - 1) + b + 1)
                    nc.scalar.activation(sqT[:, b, :], slots[:, b, :], ACT.Square).then_inc(s["sl_sq"], 1)
                for b in range(B):
                    act.wait_ge(s["ms_ps"], 2 * it + b + 1)
                    if it:
                        act.wait_ge(s["rn_s"], 2 * (it - 1) + b + 1)
                    nc.scalar.activation(mse[:, b, :], work(b, 0)[:, 0:TPB], ACT.Copy, bias=RMS_EPS).then_inc(s["ms_sb"], 1)
                for b in range(B):
                    act.wait_ge(s["snm_s"], 2 * it + b + 1)
                    if it:
                        act.wait_ge(s["at_s"], 2 * (it - 1) + b + 1)
                    nc.scalar.activation(ex[:, b, :], work(b, 0)[0:M, :], ACT.Exp, bias=snm[:, b:b + 1], scale=SCALE,
                                         accum_out=ssum[:, b:b + 1]).then_inc(s["ex_s"], 1)
                for b in range(B):
                    act.wait_ge(s["g_ps"], 2 * it + b + 1)
                    if it:
                        act.wait_ge(s["slot_s"], 2 * (it - 1) + b + 1)
                    nc.scalar.activation(rt[:, b, :], work(b, 2), ACT.Tanh, bias=half_rz[:, 0:1], scale=0.5).then_inc(s["gate_s"], 1)
                    nc.scalar.activation(hw[:, b, :], work(b, 0), ACT.Identity, bias=half_hn[:, :], scale=0.5).then_inc(s["gate_s"], 1)
                    nc.scalar.activation(zt[:, b, :], work(b, 3), ACT.Tanh, bias=half_rz[:, 1:2], scale=0.5).then_inc(s["gate_s"], 1)
                for b in range(B):
                    act.wait_ge(s["t2_s"], 2 * it + b + 1)
                    nc.scalar.activation(nn[:, b, :], t2[:, b, :], ACT.Tanh, bias=cols[:, 5:6]).then_inc(s["n_s"], 1)
            layer_norm(1)

            for b in range(B):
                for c in range(4):
                    act.wait_ge(s["ga_ps"], 4 * b + c + 1)
                    copy(gh[b][:, c, :], bank[c % 2][:, :]).then_inc(s["gh_s"], 1)
                    nc.scalar.activation(sqg[b][:, c, :], bank[c % 2][:, :], ACT.Square).then_inc(s["gh_s"], 1)
                act.wait_ge(s["x2_ps"], b + 1)
                copy(acc[:, b].rearrange("p j c -> p (j c)"), bank[3][:, :]).then_inc(s["x2_tok"], 1)
                for k in range(2 * EXPERTS):
                    kk = 2 * EXPERTS * b + k
                    act.wait_ge(s["gu_ps"], kk + 1)
                    if kk >= 2:
                        act.wait_ge(s["a2_s"], kk - 1)
                    nc.scalar.activation(th[k % 2][:, :], ob(k % 2), ACT.Tanh, scale=0.5).then_inc(s["th_s"], 1)
                    if k == 0:
                        act.wait_ge(s["sd_s"], b + 1)
                        nc.scalar.activation(sexp[:, b, :], sdif[:, b, :], ACT.Exp).then_inc(s["se_s"], 1)

        @block.vector
        def _(dve):
            v = nc.vector
            n = [0]

            def link(ins):
                n[0] += 1
                ins.then_inc(s["dchain"], 1)
                dve.wait_ge(s["dchain"], n[0])

            v.memset(minus_half[:, :], -0.5)
            v.memset(plus_half[:, :], 0.5)
            v.memset(mean_mat[:, :], 1.0 / C)
            v.memset(ones_m[:, :], 1.0)
            v.memset(ones_col[:, :], 1.0)
            for lo in lower:
                v.memset(lo[:, :, 0:1], -REMOVED)
            v.memset(vaug[:, :, :, D:DV], 1.0)
            for e in range(EXPERTS):
                v.memset(iota8[:, e:e + 1], float(e))
            v.memset(blk[:, :, :], 0.0)
            link(v.memset(ones_row[:, :], 1.0))
            dve.sem_inc(s["small"], 1)

            for b in range(B):
                dve.wait_ge(s[f"x{b}_in"], 16)
                for j in range(TPB):
                    t = b * TPB + j
                    v.bn_stats(stats[:, t, :], x_sb[:, t, :]).then_inc(s["stat_s"], 1)
                for j in range(TPB):
                    t = b * TPB + j
                    dve.wait_ge(s["stat_s"], t + 1)
                    v.bn_aggr(mv[:, t, :], stats[:, t, :]).then_inc(s["mv_s"], 1)
                dve.wait_ge(s["mv_s"], TPB * (b + 1))
                v.tensor_scalar(veps1[:, b * TPB:(b + 1) * TPB], mv[:, b * TPB:(b + 1) * TPB, 1], LN_EPS, None,
                                ALU.add).then_inc(s["veps_s"], 1)
            for b in range(B):
                dve.wait_ge(s["rstd_s"], b + 1)
                for j in range(TPB):
                    t = b * TPB + j
                    v.tensor_scalar(xn[:, t, :], x_sb[:, t, :], mv[:, t, 0:1], rstd1[:, t:t + 1],
                                    ALU.subtract, ALU.mult).then_inc(s["xn_s"], 1)
            dve.wait_ge(s["consts"], 1)
            for c in range(4):
                v.tensor_copy(blk[:, c, 2 * c:2 * c + 2], halves[:, :])
            v.tensor_copy(blockmask[:, :, :], headmask[:, :].rearrange("p (h o) -> p h o", o=1).to_broadcast([P, H, DV]))
            dve.wait_ge(s["moved"], upto("cols"))
            for i in range(2):
                for dst, o in ((gammab, 3 * C), (betab, 3 * C + 2 * D)):
                    v.tensor_copy(dst[:, i], rowb[:, o + i * D:o + (i + 1) * D].rearrange("p (o d) -> p o d", o=1)
                                  .to_broadcast([P, H, D]))
            link(v.tensor_tensor(brz[:, :], cols[:, 3:5], cols[:, 6:8], ALU.add))
            v.tensor_scalar(half_rz[:, :], brz[:, :], 0.5, None, ALU.mult)
            v.tensor_scalar(half_hn[:, :], cols[:, 8:9], 0.5, None, ALU.mult)
            dve.wait_ge(s["act_c"], 1)
            v.tensor_scalar(mix[:, 0, :], alpha_t[:, :], 0.5, 0.5, ALU.mult, ALU.add)
            link(v.tensor_scalar(mix[:, 1, :], alpha_t[:, :], -0.5, 0.5, ALU.mult, ALU.add))
            dve.wait_ge(s["achain"], 1)
            v.tensor_scalar(cms[:, :], css[:, :], 1.0 / C, RMS_EPS, ALU.mult, ALU.add).then_inc(s["csum_s"], 1)
            dve.wait_ge(s["cpow_s"], 1)
            v.tensor_scalar(pn[:, :], ctx_sb[:, :], crs[:, :], None, ALU.mult).then_inc(s["pn_s"], 1)

            def groups(ap):
                return ap.rearrange("p (g d) -> p g d", d=D)

            def each(ap):
                return ap.rearrange("p (g o) -> p g o", o=1).to_broadcast([P, GR, D])

            def qk_flat(b):
                return qk[:, TPB * b:TPB * (b + 1), :].rearrange("p t c -> p (t c)")

            for b in range(B):
                for j in range(TPB):
                    t = b * TPB + j
                    dve.wait_ge(s["qkv_ps"], t + 1)
                    v.tensor_tensor(qk[:, t, :], bank[t % 2][:, 0:2 * C], rowb[:, 0:2 * C], ALU.add).then_inc(s["qk_sb"], 1)
                    v.tensor_tensor(vaug[:, t, :, 0:D], bank[t % 2][:, 2 * C:3 * C].rearrange("p (h d) -> p h d", d=D),
                                    rowb[:, 2 * C:3 * C].rearrange("p (h d) -> p h d", d=D), ALU.add).then_inc(s["v_sb"], 1)
                dve.wait_ge(s["qk_sb"], TPB * (b + 1))
                link(v.tensor_reduce(gsum[:, b], groups(qk_flat(b)), op=ALU.add, axis=AX.X))
                link(v.tensor_scalar(gmean[:, b], gsum[:, b], 1.0 / D, None, ALU.mult))
                v.tensor_tensor(groups(diff[:, b]), groups(qk_flat(b)), each(gmean[:, b]), ALU.subtract).then_inc(s["dsub"], 1)
            for b in range(B):
                dve.wait_ge(s["dsq"], b + 1)
                link(v.tensor_reduce(gvar[:, b], groups(sqd[:, b]), op=ALU.add, axis=AX.X))
                v.tensor_scalar(gveps[:, b], gvar[:, b], 1.0 / D, LN_EPS, ALU.mult, ALU.add).then_inc(s["dvar"], 1)
            both = lambda a: a[:, :, :].rearrange("p b g -> p (b g)")
            dve.wait_ge(s["gstd_s"], 2)
            link(v.reciprocal(both(grough), both(gstd)))
            link(v.tensor_tensor(both(gprod), both(grough), both(gveps), ALU.mult))
            link(v.scalar_tensor_tensor(out=both(gfix), in0=both(grough), scalar=-0.5, in1=both(gprod), op0=ALU.mult, op1=ALU.mult))
            link(v.scalar_tensor_tensor(out=both(grstd), in0=both(gfix), scalar=1.5, in1=both(grough), op0=ALU.add, op1=ALU.mult))
            dve.wait_ge(s["moved"], upto("ctx"))
            v.tensor_scalar(pnTw[:, :], pnT[:, :], cols[:, 2:3], None, ALU.mult).then_inc(s["pnw_s"], 1)
            for b in range(B):
                dve.wait_ge(s["dsub"], b + 1)
                link(v.tensor_tensor(groups(qk_flat(b)), groups(diff[:, b]), each(grstd[:, b]), ALU.mult))
                x3 = qk[:, TPB * b:TPB * (b + 1), :]
                for last, table, op in ((False, gammab, ALU.mult), (True, betab, ALU.add)):
                    tb = table[:, :, :, :].rearrange("p (o a) h d -> p o (a h d)", o=1).to_broadcast([P, TPB, 2 * C])
                    ins = v.tensor_tensor(x3, x3, tb, op)
                    if last:
                        ins.then_inc(s["qk_ready"], 1)
                    else:
                        link(ins)
            for b in range(B):
                dve.wait_ge(s["qk_ready"], b + 1)
                link(v.tensor_reduce(gmax[:, b], groups(qk_flat(b)), op=ALU.max, axis=AX.X))
                v.tensor_tensor(groups(diff[:, b]), groups(qk_flat(b)), each(gmax[:, b]), ALU.subtract).then_inc(s["fmax_s"], 1)
            for b in range(B):
                dve.wait_ge(s["fexp"], b + 1)
                link(v.tensor_reduce(gden[:, b], groups(sqd[:, b]), op=ALU.add, axis=AX.X))
                link(v.reciprocal(grec[:, b], gden[:, b]))
                v.tensor_tensor(groups(feat[:, TPB * b:TPB * (b + 1), :].rearrange("p t c -> p (t c)")), groups(sqd[:, b]),
                                each(grec[:, b]), ALU.mult).then_inc(s["fready"], 1)
            dve.wait_ge(s["moved"], upto("qk_fold"))
            link(v.tensor_scalar(foldw[:, :], fold[:, :], cols[:, 1:2], None, ALU.mult))

            steps = [0]

            def step(ins):
                ins.then_inc(s["topk_step"], 1)
                steps[0] += 1
                return steps[0]

            def after(k):
                if k:
                    dve.wait_ge(s["topk_step"], k)

            def leader(pr, w, c):
                g, q = g_of(pr), pr[1]
                if c == 0:
                    dve.wait_ge(s["scores_sb"], 2 * g + w + 1)
                    dve.sem_inc(s["fence"], 1)
                ins = v.max(lead[q % 2][:, w, c, :], S[2 * q + w][:, c * CHUNK:(c + 1) * CHUNK])
                if c == CHUNKS - 1:
                    ins.then_inc(s["lead_s"], 1)

            def threshold(pr):
                g, q, z = g_of(pr), pr[1], pr[1] % 2
                up, lo, ld = upper[z], lower[z], lead[z]
                dve.wait_ge(s["lead_s"], 2 * g + 2)
                dve.sem_inc(s["fence"], 1)
                done = [0, 0]
                for r in range(4):
                    for w in range(2):
                        if r:
                            after(done[w])
                        done[w] = step(v.max(up[:, w, 8 * r:8 * r + 8], ld[:, w, :, 0:3] if r == 0 else rest[:, w, :]))
                    if r == 0:
                        for w in range(2):
                            step(v.max(lo[:, w, 1:9], ld[:, w, :, 3:8]))
                        top1 = done[1]
                    if r < 3:
                        for w in range(2):
                            src = ld[:, w, :, 0:3] if r == 0 else rest[:, w, :]
                            dst = rest[:, w, :].rearrange("p (c k) -> p c k", k=3) if r == 0 else rest[:, w, :]
                            after(done[w])
                            done[w] = step(v.match_replace(dst, up[:, w, 8 * r:8 * r + 8], src, REMOVED))
                    if r == 0:
                        after(top1)
                        v.tensor_scalar(negmax[q][:, :], up[:, :, 0], -1.0, None, ALU.mult).then_inc(s["negmax_s"], 1)
                    if r == 1:
                        e8 = step(v.tensor_reduce(eighth[:, :], ld[:, :, :, 7], op=ALU.max, axis=AX.X))
                    if r == 2:
                        after(e8)
                        step(v.tensor_tensor(bound[:, :], eighth[:, :], lo[:, :, 8], ALU.max))
                return done[1]

            def merge(pr, part, k):
                q, z = pr[1], pr[1] % 2
                after(k)
                if part == 0:
                    return step(v.tensor_tensor(cand[:, :, :], upper[z][:, :, TOPK - 1:TOPK - 10:-1], lower[z][:, :, :], ALU.min))
                if part == 1:
                    return step(v.tensor_reduce(thr[q][:, :], cand[:, :, :], op=ALU.max, axis=AX.X))
                if part == 2:
                    return step(v.tensor_tensor(above[:, :], bound[:, :], thr[q][:, :], ALU.is_gt))
                v.scalar_tensor_tensor(out=missed[z][:, :], in0=above[:, 1:2], scalar=float(2 * P), in1=above[:, 0:1],
                                       op0=ALU.mult, op1=ALU.add).then_inc(s["missed_s"], 1)
                return 0

            def whole_row(pr, w):
                row_ = S[2 * pr[1] + w]
                k = 0
                for r in range(4):
                    if k:
                        dve.wait_ge(s["redo"], k)
                    v.max(top[:, 8 * r:8 * r + 8], row_ if r == 0 else W[0]).then_inc(s["redo"], 1)
                    k += 1
                    if r < 3:
                        dve.wait_ge(s["redo"], k)
                        v.match_replace(W[0], top[:, 8 * r:8 * r + 8], row_ if r == 0 else W[0], REMOVED).then_inc(s["redo"], 1)
                        k += 1
                dve.wait_ge(s["redo"], k)
                v.tensor_copy(thr[pr[1]][:, w:w + 1], top[:, TOPK - 1:TOPK]).then_inc(s["redo"], 1)
                dve.wait_ge(s["redo"], k + 1)
                dve.sem_clear(s["redo"])

            def settle(pr):
                dve.wait_ge(s["flags_s"], g_of(pr) + 1)
                dve.sem_inc(s["fence"], 1)
                counts = dve.value_load(flags[0:1, 0:1], min_val=0, max_val=P + 2 * P * P)
                with dve.If(counts):
                    with dve.If(counts & (2 * P - 1)):
                        whole_row(pr, 0)
                    with dve.If(counts >> 8):
                        whole_row(pr, 1)
                dve.sem_inc(s["cut_s"], 1)

            FIRST = 2

            def half(pr, w, before, found):
                for c in range(CHUNKS):
                    if pr is not None:
                        leader(pr, w, c)
                    if before is not None and w == 0 and c % FIRST == FIRST - 1 and c // FIRST < 4:
                        found = merge(before, c // FIRST, found)
                    if before is not None and w == 1 and c == 3:
                        dve.wait_ge(s["flag_ps"], g_of(before) + 1)
                        v.tensor_copy(flags[:, :], flagbank[0:1, 0:1]).then_inc(s["flags_s"], 1)

            def turn(m):
                for q in range(4):
                    half(pair(m, q), 1, pair(m, q - 1), 0)
                    if pair(m, q - 1) is not None:
                        settle(pair(m, q - 1))
                    found = threshold((m, q))
                    half(pair(m, q + 1), 0, (m, q), found)
                dve.wait_ge(s["topk_step"], steps[0])
                dve.sem_clear(s["topk_step"])
                steps[0] = 0

            half((0, 0), 0, None, 0)
            turn(0)
            with dve.Fori(1, PAIRS // 4 - 1) as m:
                turn(m)
            turn(PAIRS // 4 - 1)
            half(None, 1, (PAIRS // 4 - 1, 3), 0)
            settle((PAIRS // 4 - 1, 3))

            for b in range(B):
                dve.wait_ge(s["kv_ps"], b + 1)
                v.tensor_tensor(kvb[:, b, :], work(b, 0)[:, 0:H * DV], blockmask[:, :, :].rearrange("p h e -> p (h e)"),
                                ALU.mult).then_inc(s["kv_sb"], 1)
            dve.wait_ge(s["av_done"], BH * TPB + 2)
            dve.wait_ge(s["z_saved"], BH // 2)
            for b in range(B):
                dve.wait_ge(s["ol_ps"], b + 1)
                for j in range(TPB):
                    osum = obank[:, o_at(TPB * b + j):o_at(TPB * b + j) + H * DV].rearrange("p (h e) -> p h e", e=DV)
                    lin = work(b, j // 2)[:, (j % 2) * H * DV:(j % 2 + 1) * H * DV].rearrange("p (h e) -> p h e", e=DV)
                    z = zall[:, b * H // 2:(b + 1) * H // 2, :].rearrange("p m (i j) -> p (m i) j", j=TPB)[:, :, j]
                    v.scalar_tensor_tensor(out=den[:, b, 0, j, :], in0=z, scalar=ATT_EPS, in1=osum[:, :, D],
                                           op0=ALU.mult, op1=ALU.add)
                    ins = v.tensor_scalar(den[:, b, 1, j, :], lin[:, :, D], LIN_EPS, None, ALU.add)
                link(ins)
                link(v.reciprocal(rden[:, b].rearrange("p a j h -> p (a j h)"), den[:, b].rearrange("p a j h -> p (a j h)")))
                for a in range(2):
                    ins = v.tensor_tensor(wden[:, b, a], rden[:, b, a],
                                          mix[:, a, :].rearrange("p (o h) -> p o h", o=1).to_broadcast([P, TPB, H]), ALU.mult)
                link(ins)
                for j in range(TPB):
                    osum = obank[:, o_at(TPB * b + j):o_at(TPB * b + j) + H * DV]
                    lin = work(b, j // 2)[:, (j % 2) * H * DV:(j % 2 + 1) * H * DV]
                    for a, dst, src in ((0, o_s, osum), (1, o_l, lin)):
                        ins = v.tensor_tensor(
                            dst[:, b, j, :].rearrange("p (h d) -> p h d", d=D), src.rearrange("p (h e) -> p h e", e=DV)[:, :, 0:D],
                            wden[:, b, a, j, :].rearrange("p (h o) -> p h o", o=1).to_broadcast([P, H, D]), ALU.mult)
                link(ins)
                v.tensor_tensor(o_tok[:, b], o_s[:, b], o_l[:, b], ALU.add).then_inc(s["o_ready"], 1)
            for b in range(B):
                dve.wait_ge(s["pr_ps"], b + 1)
                v.scalar_tensor_tensor(out=x1T[:, b, :], in0=work(b, 1), scalar=cols[:, 0:1], in1=xT[:, b * N:(b + 1) * N],
                                       op0=ALU.add, op1=ALU.add).then_inc(s["x1_s"], 1)

            def layer_norm(k, src, dst):
                for b in range(B):
                    dve.wait_ge(s["ln_m"], 2 * k + b + 1)
                    v.tensor_tensor(dT[:, b, :], src[:, b, :], work(b, 0), ALU.subtract).then_inc(s["ln_d"], 1)
                for b in range(B):
                    dve.wait_ge(s["ln_b"], 2 * k + b + 1)
                    dve.wait_ge(s["ln_d"], 2 * k + b + 1)
                    v.tensor_tensor(dst[:, b, :], dT[:, b, :], work(b, 3), ALU.mult).then_inc(s["ln_h"], 1)

            dve.wait_ge(s["x1_s"], 2)
            layer_norm(0, x1T, slots)
            for it in range(ITERS):
                for b in range(B):
                    dve.wait_ge(s["rn_s"], 2 * it + b + 1)
                    dve.wait_ge(s["ms_ps"], 2 * it + b + 1)
                    v.tensor_tensor(sct[:, b], work(b, 1)[:, 0:TPB * M].rearrange("p (j m) -> p j m", m=M),
                                    rn[:, b, :].rearrange("p (j o) -> p j o", o=1).to_broadcast([P, TPB, M]),
                                    ALU.mult).then_inc(s["sct_s"], 1)
                for b in range(B):
                    dve.wait_ge(s["sc_t"], 2 * it + b + 1)
                    link(v.reduce_max(smax[:, b:b + 1], work(b, 0)[0:M, :], AX.X))
                    v.tensor_scalar(snm[:, b:b + 1], smax[:, b:b + 1], -SCALE, None, ALU.mult).then_inc(s["snm_s"], 1)
                for b in range(B):
                    dve.wait_ge(s["ex_s"], 2 * it + b + 1)
                    link(v.reciprocal(srec[:, b:b + 1], ssum[:, b:b + 1]))
                    v.tensor_scalar(at[:, b, :], ex[:, b, :], srec[:, b:b + 1], None, ALU.mult).then_inc(s["at_s"], 1)
                for b in range(B):
                    dve.wait_ge(s["du_ps"], 2 * it + b + 1)
                    link(v.tensor_scalar(dde[:, b, :], work(b, 0), RMS_EPS, None, ALU.add))
                    link(v.reciprocal(drc[:, b, :], dde[:, b, :]))
                    v.tensor_tensor(upd[:, b, :], work(b, 1), drc[:, b, :], ALU.mult).then_inc(s["u_s"], 1)
                for b in range(B):
                    dve.wait_ge(s["gate_s"], 6 * it + 3 * b + 2)
                    link(v.scalar_tensor_tensor(out=t1[:, b, :], in0=rt[:, b, :], scalar=1.0, in1=hw[:, b, :],
                                                op0=ALU.add, op1=ALU.mult))
                    v.tensor_tensor(t2[:, b, :], t1[:, b, :], work(b, 1), ALU.add).then_inc(s["t2_s"], 1)
                for b in range(B):
                    dve.wait_ge(s["n_s"], 2 * it + b + 1)
                    dve.wait_ge(s["gate_s"], 6 * it + 3 * b + 3)
                    link(v.tensor_tensor(dd[:, b, :], slots[:, b, :], nn[:, b, :], ALU.subtract))
                    link(v.scalar_tensor_tensor(out=ee[:, b, :], in0=zt[:, b, :], scalar=1.0, in1=dd[:, b, :],
                                                op0=ALU.add, op1=ALU.mult))
                    v.scalar_tensor_tensor(out=slots[:, b, :], in0=ee[:, b, :], scalar=0.5, in1=nn[:, b, :],
                                           op0=ALU.mult, op1=ALU.add).then_inc(s["slot_s"], 1)
            for b in range(B):
                dve.wait_ge(s["slot_s"], 2 * (ITERS - 1) + b + 1)
                v.tensor_tensor(x2T[:, b, :], x1T[:, b, :], slots[:, b, :], ALU.add).then_inc(s["slot_s"], 1)
            dve.wait_ge(s["slot_s"], 2 * ITERS + 2)
            layer_norm(1, x2T, hT)

            for b in range(B):
                def add_expert(e):
                    dve.wait_ge(s["y_ps"], b * EXPERTS + e + 1)
                    if e == 0:
                        dve.wait_ge(s["x2_tok"], b + 1)
                    else:
                        dve.wait_ge(s["acc_s"], b * EXPERTS + e)
                    for j in range(TPB):
                        ins = v.scalar_tensor_tensor(out=acc[:, b, j, :], in0=bank[2][:, j * P:(j + 1) * P],
                                                     scalar=wfull[:, b, j, e:e + 1], in1=acc[:, b, j, :],
                                                     op0=ALU.mult, op1=ALU.add)
                    ins.then_inc(s["acc_s"], 1)

                for e in range(EXPERTS):
                    if e == 0:
                        dve.wait_ge(s["sc_ps"], b + 1)
                        v.tensor_copy(s2[:, b].rearrange("p j e -> p (j e)"),
                                      bank[2][:, b * TPB * EXPERTS:(b + 1) * TPB * EXPERTS]).then_inc(s["s2_s"], 1)
                        dve.wait_ge(s["sr_s"], b + 1)
                        for j in range(TPB):
                            ins = v.max(m8[:, b, j, :], sr[:, b, j, :])
                        link(ins)
                        for j in range(TPB):
                            v.max_index(ix[:, b, j, :], m8[:, b, j, :], sr[:, b, j, :])
                        link(v.tensor_tensor(sdif[:, b, :], m8[:, b, :, 1], m8[:, b, :, 0], ALU.subtract))
                        dve.sem_inc(s["sd_s"], 1)
                        link(v.tensor_copy(ixf[:, b, :, :], ix[:, b, :, 0:2]))
                    for f in range(2):
                        k = 2 * (b * EXPERTS + e) + f
                        dve.wait_ge(s["th_s"], k + 1)
                        if e >= 2:
                            dve.wait_ge(s["y_ps"], b * EXPERTS + e - 1)
                        elif b:
                            dve.wait_ge(s["y_ps"], b * EXPERTS + e - 1 if e else b * EXPERTS - 1)
                        link(v.scalar_tensor_tensor(out=a1[f][:, :], in0=th[f][:, :], scalar=1.0, in1=ob(f),
                                                    op0=ALU.add, op1=ALU.mult))
                        v.tensor_tensor(a2[2 * (e % 2) + f], a1[f][:, :], ob(2 + f), ALU.mult).then_inc(s["a2_s"], 1)
                    if e == 0:
                        dve.wait_ge(s["se_s"], b + 1)
                        link(v.tensor_scalar(spl[:, b, :], sexp[:, b, :], 1.0, None, ALU.add))
                        link(v.reciprocal(srecp[:, b, :], spl[:, b, :]))
                        link(v.tensor_scalar(w12[:, b, 0, :], srecp[:, b, :], 0.5, None, ALU.mult))
                        link(v.tensor_tensor(w12[:, b, 1, :], w12[:, b, 0, :], sexp[:, b, :], ALU.mult))
                        for i in range(2):
                            ins = v.tensor_tensor(eq[:, b, i], iota8[:, :].rearrange("p (o e) -> p o e", o=1).to_broadcast([P, TPB, EXPERTS]),
                                                  ixf[:, b, :, i:i + 1].to_broadcast([P, TPB, EXPERTS]), ALU.is_equal)
                        link(ins)
                        for i in range(2):
                            ins = v.tensor_tensor(ew[:, b, i], eq[:, b, i],
                                                  w12[:, b, i, :].rearrange("p (j o) -> p j o", o=1).to_broadcast([P, TPB, EXPERTS]), ALU.mult)
                        link(ins)
                        link(v.tensor_tensor(wfull[:, b], ew[:, b, 0], ew[:, b, 1], ALU.add))
                    else:
                        add_expert(e - 1)
                add_expert(EXPERTS - 1)


_INS = ["x", "ctx_1024", "L0_attn_Wqkv", "L0_attn_bqkv", "L0_attn_q_gamma", "L0_attn_q_beta", "L0_attn_k_gamma",
        "L0_attn_k_beta", "L0_attn_alpha", "L0_attn_Wproj", "L0_attn_bproj", "L0_xattn_Wq", "L0_xattn_Wk",
        "L0_xattn_Wv", "L0_xattn_gru_wih", "L0_xattn_gru_whh", "L0_xattn_gru_bih", "L0_xattn_gru_bhh",
        "L0_xattn_slot_norm_w", "L0_xattn_input_norm_w", "L0_ffn_W_A", "L0_ffn_W_B", "L0_ffn_W_up", "L0_ffn_W_down"]
_OUTS = [((2, 512, 128), "float32")]


def kernel(**inputs):
    import numpy as _np
    import concourse.bacc as _bacc
    from concourse import mybir as _mybir
    from concourse.bass_utils import run_bass_kernel_spmd as _run

    nc = _bacc.Bacc("TRN2", target_bir_lowering=False, num_devices=1)
    arrays, args = {}, []
    for name in _INS:
        a = _np.ascontiguousarray(inputs[name])
        arrays[f"in_{name}_dram"] = a
        args.append(nc.dram_tensor(f"in_{name}_dram", a.shape, _mybir.dt.from_np(a.dtype), kind="ExternalInput").ap())
    for i, (shape, dtype) in enumerate(_OUTS):
        dt = _mybir.dt.from_np(_np.dtype(dtype))
        args.append(nc.dram_tensor(f"out_{i}_dram", shape, dt, kind="ExternalOutput").ap())
    build(nc, *args)
    r = _run(nc, [arrays], core_ids=[0])
    got = tuple(r.results[0][f"out_{i}_dram"] for i in range(len(_OUTS)))
    return got[0]
```

```python
import concourse.bass as bass
from concourse import mybir
from contextlib import ExitStack

F32 = mybir.dt.float32
U32 = mybir.dt.uint32
ALU = mybir.AluOpType
ACT = mybir.ActivationFunctionType
AX = mybir.AxisListType

B, N, C = 2, 512, 128
H = 16
D = C // H
DV = D + 1
M = 32
EXPERTS, RANK, FF = 8, 64, 256
ITERS = 3
P = 128
TPB = N // P
T = B * TPB
TOPK = max(1, int(N * 0.05))
BH = B * H
LN_EPS, RMS_EPS, ATT_EPS, LIN_EPS = 1e-5, 1e-6, 1e-8, 1e-6
SCALE = C ** -0.5
WIDE = P
REMOVED = -3.0e38
CHUNKS = 16
CHUNK = N // CHUNKS

GROUPS = (["wqkv", "xn0", "xn1", "rows", "bproj", "cols", "proj", "wk_wv", "ctx", "kproj", "qk_fold", "vproj", "wih",
           "values0", "values1", "whh", "wa"]
          + [f"wb{i}" for i in range(2)] + ["qT0", "kT0"] + [f"wup{i}" for i in range(4)] + ["qT1", "kT1"]
          + [f"wdn{i}" for i in range(4)] + ["qf0", "qf1"])


def upto(name):
    return GROUPS.index(name) + 1


def build(nc, x, ctx_in, Wqkv, bqkv, q_gamma, q_beta, k_gamma, k_beta, alpha, Wproj, bproj, Wq, Wk, Wv,
          wih, whh, bih, bhh, slot_w, input_w, W_A, W_B, W_up, W_down, out):
    ctx = ExitStack()
    with ctx:
        def sb(name, shape, dt=F32):
            return ctx.enter_context(nc.sbuf_tensor(name, shape, dt))

        def sem(name):
            return ctx.enter_context(nc.semaphore(name))

        x_sb = sb("x_sb", [P, T, C])
        ctx_sb = sb("ctx_sb", [B * M, C])
        wqkv = sb("wqkv", [P, 3, C])
        wproj, wq, wk, wv = (sb(n, [C, C]) for n in ("wproj", "wq", "wk", "wv"))
        wih_sb, whh_sb = sb("wih_sb", [P, 3, C]), sb("whh_sb", [P, 3, C])
        wa_sb = sb("wa_sb", [P, 4, C])
        wb_sb = sb("wb_sb", [P, 4, 2, P])
        wup_sb = sb("wup_sb", [P, 16, C])
        wdn_sb = sb("wdn_sb", [P, EXPERTS, FF])
        ROW = 3 * C + 4 * D + H
        row = sb("row", [1, ROW + C])
        cols_in = sb("cols_in", [8, C])

        ident = sb("ident", [P, P])
        headmask = sb("headmask", [P, H])
        blockmask = sb("blockmask", [P, H, DV])
        halves = sb("halves", [P, 2])
        blk = sb("blk", [P, 4, WIDE])
        ones_row = sb("ones_row", [1, P])
        mean_mat = sb("mean_mat", [P, P])
        minus_half = sb("minus_half", [P, 1])
        plus_half = sb("plus_half", [P, 1])
        iota8 = sb("iota8", [P, EXPERTS])

        wqkvT = sb("wqkvT", [C, 3 * C])
        rowb = sb("rowb", [P, ROW + C])
        cols = sb("cols", [C, 8])
        wprojT = sb("wprojT", [C, C])
        wkvT = sb("wkvT", [C, 2, C])
        wihT, whhT = sb("wihT", [C, 3, C]), sb("whhT", [C, 3, C])
        waT = sb("waT", [C, 4, P])
        wbT = sb("wbT", [P, 4, 2, P])
        wupT = sb("wupT", [C, 16, P])
        wdnT = sb("wdnT", [P, EXPERTS, 2, C])
        half_rz = sb("half_rz", [C, 2])
        half_hn = sb("half_hn", [C, 1])
        brz = sb("brz", [C, 2])
        gammab, betab = sb("gammab", [P, 2, H, D]), sb("betab", [P, 2, H, D])
        alpha_t = sb("alpha_t", [P, H])
        mix = sb("mix", [P, 2, H])

        stats = sb("stats", [P, T, 6])
        mv = sb("mv", [P, T, 2])
        veps1 = sb("veps1", [P, T])
        rstd1 = sb("rstd1", [P, T])
        xn = sb("xn", [P, T, C])
        xnT = sb("xnT", [C, B * N])
        xb = sb("xb", [P, T, C])
        qk = sb("qk", [P, T, 2 * C])
        vaug = sb("vaug", [P, T, H, DV])
        GR = TPB * 2 * H
        gsum, gmean, gvar, gveps, grstd = (sb(n, [P, B, GR]) for n in ("gsum", "gmean", "gvar", "gveps", "grstd"))
        gmax, gden, grec = (sb(n, [P, B, GR]) for n in ("gmax", "gden", "grec"))
        gstd, grough, gprod, gfix = gmax, gden, grec, gmean
        diff = sb("diff", [P, B, TPB * 2 * C])
        sqd = sb("sqd", [P, B, TPB * 2 * C])
        feat = sb("feat", [P, T, 2 * C])
        qT, kT, qfT = sb("qT", [C, B * N]), sb("kT", [C, B * N]), sb("qfT", [C, B * N])

        qm = [sb(f"qm{i}", [C, 2 * P]) for i in range(2)]
        S_all, E_all = sb("S_all", [P, TPB, N]), sb("E_all", [P, TPB, N])
        S = [S_all[:, i, :] for i in range(TPB)] + [diff[:, i // 2, (i % 2) * N:(i % 2 + 1) * N] for i in range(TPB)]
        W_all, PT_all = sb("W_all", [P, 2, N]), sb("PT_all", [P, 2, N])
        W = [W_all[:, i, :] for i in range(2)]
        E = [E_all[:, i, :] for i in range(TPB)]
        PT = [PT_all[:, i, :] for i in range(2)]
        lead = [sb(f"lead{i}", [P, 2, CHUNKS, 8]) for i in range(2)]
        upper = [sb(f"upper{i}", [P, 2, 32]) for i in range(2)]
        lower = [sb(f"lower{i}", [P, 2, 9]) for i in range(2)]
        rest = sb("rest", [P, 2, CHUNKS * 3])
        cand = sb("cand", [P, 2, 9])
        thr = [sb(f"thr{i}", [P, 2]) for i in range(4)]
        signs = sb("signs", [P, N], mybir.dt.bfloat16)
        balance = sb("balance", [P, 4])
        missed = sb("missed", [P, 4])
        flags = sb("flags", [1, 5], mybir.dt.int32)
        top = sb("top", [P, 32])
        negmax = [sb(f"negmax{i}", [P, 2]) for i in range(4)]
        keep = [sb(f"keep{i}", [P, N], mybir.dt.bfloat16) for i in range(2)]
        zb = sb("zb", [P, 8])
        zall = sb("zall", [P, BH // 2, 8])
        ones_col = sb("ones_col", [P, 1])

        kvb = sb("kvb", [P, B, H * DV])
        den = sb("den", [P, B, 2, TPB, H])
        rden = sb("rden", [P, B, 2, TPB, H])
        wden = sb("wden", [P, B, 2, TPB, H])
        o_tok = sb("o_tok", [P, B, TPB, C])
        o_s, o_l = (a[:, :, :].rearrange("p (b j) c -> p b j c", b=B) for a in (x_sb, xn))
        oT = sb("oT", [C, B, N])
        x1 = sb("x1", [P, B, TPB, C])
        sqT = sqd[:, :, 0:N]
        mse, rn = (sb(n, [P, B, TPB]) for n in ("mse", "rn"))
        sct = sb("sct", [P, B, TPB, M])
        slots = sb("slots", [C, B, N])
        hT = S_all[:, 0:2, :]
        csq, css, cms, crs = sb("csq", [B * M, C]), sb("css", [B * M, 1]), sb("cms", [B * M, 1]), sb("crs", [B * M, 1])
        pn = sb("pn", [B * M, C])
        pnT = sb("pnT", [C, B * M])
        pnTw = sb("pnTw", [C, B * M])
        kpT = sb("kpT", [C, B * M])
        fold = sb("fold", [C, B * M])
        foldw = sb("foldw", [C, P // (B * M), B * M])
        vT = sb("vT", [C, B * M])
        gv = sb("gv", [M, B, 3 * C])
        ex, at = (wup_sb[0:M, 8 * i:8 * i + 8, :].rearrange("p (b j) c -> p b (j c)", b=B) for i in range(2))
        smax, snm, ssum, srec = (sb(n, [M, B]) for n in ("smax", "snm", "ssum", "srec"))
        dde, drc = (sb(n, [P, B, TPB]) for n in ("dde", "drc"))
        gvs = xnT[0:M, 0:B * 3 * C].rearrange("p (b g) -> p b g", b=B)
        zt, zh = (a[:, :].rearrange("p (b n) -> p b n", b=B) for a in (qT, kT))
        rt, nz = (wdn_sb[:, 4 * i:4 * i + 4, :].rearrange("p (b j) c -> p b (j c)", b=B) for i in range(2))
        hw, t1, t2, nn = S_all[:, 0:2, :], S_all[:, 2:4, :], E_all[:, 0:2, :], E_all[:, 2:4, :]
        omz = x_sb[:, :, :].rearrange("p (b j) c -> p b (j c)", b=B)
        gh = [a[:, :, :].rearrange("p (k i) c -> p k (i c)", i=2) for a in (qk, feat)]
        sqg = [wup_sb[:, :, :].rearrange("p (k i) c -> p k (i c)", i=4), wdn_sb[:, :, :].rearrange("p (k i) c -> p k (i c)", i=2)]
        s2, sr = sb("s2", [P, B, TPB, EXPERTS]), sb("sr", [P, B, TPB, EXPERTS])
        m8 = sb("m8", [P, B, TPB, EXPERTS])
        ix = sb("ix", [P, B, TPB, EXPERTS], U32)
        ixf = sb("ixf", [P, B, TPB, 2])
        sdif, sexp, spl, srecp = (sb(n, [P, B, TPB]) for n in ("sdif", "sexp", "spl", "srecp"))
        w12 = sb("w12", [P, B, 2, TPB])
        eq = sb("eq", [P, B, 2, TPB, EXPERTS])
        ew = sb("ew", [P, B, 2, TPB, EXPERTS])
        wfull = sb("wfull", [P, B, TPB, EXPERTS])
        th, a1, a2 = PT, W, E
        acc = o_tok

        bank = [ctx.enter_context(nc.psum_tensor(f"bank{i}", [P, 512], F32)) for i in range(4)]
        obank = ctx.enter_context(nc.psum_tensor("obank", [P, 3 * 512], F32))
        flagbank = ctx.enter_context(nc.psum_tensor("flagbank", [P, 512], F32))

        def ob(i):
            return obank[:, i * 512:(i + 1) * 512] if i < 3 else flagbank[:, :]

        def o_at(t):
            return (t // 3) * 512 + (t % 3) * H * DV

        def work(b, i):
            return bank[2 * b + i][:, :] if i < 2 else ob((0, 3, 1, 2)[2 * b + i - 2])

        def gate_bank(b, c):
            return (ob(1), ob(3), bank[0][:, :], bank[1][:, :])[c] if b == 0 else bank[c][:, :]

        RANKED = (2, 5)

        PAIRS = BH * TPB // 2

        def pair(m, q):
            m, q = m + q // 4, q % 4
            if isinstance(m, int) and not 0 <= 4 * m + q < PAIRS:
                return None
            return m, q

        def g_of(pr):
            return 4 * pr[0] + pr[1]

        def head_of(pr):
            h = 2 * pr[0] + pr[1] // 2
            return (h // H, h % H) if isinstance(h, int) else ((h >> 4) & 1, h & (H - 1))

        names = """
            x0_in x1_in wqkv_in rows_in cols_in_s ctx_in_s xw_in ffa_in ffb_in ffu_in ffd_in out_s
            consts small act_c fence dchain pchain achain
            stat_s mv_s veps_s rstd_s xn_s xb_s
            group_ps moved
            qkv_ps qk_sb v_sb dsub dsq dvar gstd_s qk_ready fmax_s fexp fready
            csum_s cpow_s pn_s pnw_s
            qm_ready scores_ps scores_sb lead_s topk_step negmax_s thr_s balance_s missed_s flag_ps flags_s redo cut_s
            exp_done z_saved keep_s masked pt_ps pt_sb av_done
            kv_ps kv_sb kv_own ol_ps o_ready ot_ps ot_sb pr_ps
            ln_e ln_r ln_n ln_t ln_h
            sl_sq ms_ps ms_sb rn_s sct_s sc_t snm_s ex_s srec_s gvs_s den_ps drc_s rb_ps at_s
            hn_ps g_ps rt_s zt_s hw_s t2_s n_s slot_s so_ps
            ga_ps gh_s sqg_s sc_ps s2_s sr_s sd_s se_s gu_ps th_s a2_s y_ps acc_s""".split()
        s = {n: sem(n) for n in names}

        block = ctx.enter_context(nc.Block())

        @block.sync
        def _(sp):
            for b in range(B):
                sp.dma_start(x_sb[:, TPB * b:TPB * (b + 1), :],
                             x[b].rearrange("(j p) c -> p j c", p=P)).then_inc(s[f"x{b}_in"], 16)
            first = 0
            for src, k in ((bqkv, 3 * C), (q_gamma, D), (k_gamma, D), (q_beta, D), (k_beta, D), (alpha, H), (bproj, C)):
                sp.dma_start(row[:, first:first + k], src.rearrange("(o n) -> o n", o=1)).then_inc(s["rows_in"], 16)
                first += k
            for r, src in enumerate((slot_w, input_w)):
                sp.dma_start(cols_in[r:r + 1, :], src.rearrange("(o n) -> o n", o=1)).then_inc(s["cols_in_s"], 16)
            for r, src in ((2, bih), (5, bhh)):
                sp.dma_start(cols_in[r:r + 3, :], src.rearrange("(o n) -> o n", o=3)).then_inc(s["cols_in_s"], 16)
            sp.dma_start(ctx_sb[:, :], ctx_in.rearrange("b m c -> (b m) c")).then_inc(s["ctx_in_s"], 16)
            for dst, src in ((wproj, Wproj), (wq, Wq), (wk, Wk), (wv, Wv)):
                sp.dma_start(dst[:, :], src).then_inc(s["xw_in"], 16)
            for dst, src in ((wih_sb, wih), (whh_sb, whh)):
                sp.dma_start(dst[:, :, :], src.rearrange("(g p) c -> p g c", p=P)).then_inc(s["xw_in"], 16)
            sp.dma_start(wa_sb[:, :, :], W_A.rearrange("(k e) r c -> (e r) k c", e=2)).then_inc(s["ffa_in"], 16)
            for e in range(2):
                for f in range(2):
                    sp.dma_start(wb_sb[:, :, f, e * RANK:(e + 1) * RANK],
                                 W_B.rearrange("(k e) f r -> e f k r", e=2)[e, f * P:(f + 1) * P]).then_inc(s["ffb_in"], 16)
            sp.dma_start(wup_sb[:, :, :], W_up.rearrange("e (f p) c -> p (e f) c", p=P)).then_inc(s["ffu_in"], 16)
            sp.dma_start(wdn_sb[:, :, :], W_down.rearrange("e h f -> h e f")).then_inc(s["ffd_in"], 16)
            for b in range(B):
                sp.wait_ge(s["acc_s"], (b + 1) * EXPERTS)
                sp.dma_start(out[b].rearrange("(j p) c -> p j c", p=P), acc[:, b]).then_inc(s["out_s"], 16)
            sp.wait_ge(s["out_s"], 16 * B)

        @block.gpsimd
        def _(pool):
            n = [0]

            def link(ins):
                n[0] += 1
                ins.then_inc(s["pchain"], 1)
                pool.wait_ge(s["pchain"], n[0])

            link(nc.gpsimd.memset(ident[:, :], 0.0))
            link(nc.gpsimd.affine_select(out=ident[:, :], in_=ident[:, :], compare_op=ALU.not_equal, fill=1.0,
                                         base=0, pattern=[[-1, P]], channel_multiplier=1))
            link(nc.gpsimd.memset(headmask[:, :], 1.0))
            link(nc.gpsimd.affine_select(out=headmask[:, :], in_=headmask[:, :], compare_op=ALU.is_ge, fill=0.0,
                                         base=0, pattern=[[-D, H]], channel_multiplier=1))
            link(nc.gpsimd.affine_select(out=headmask[:, :], in_=headmask[:, :], compare_op=ALU.is_ge, fill=0.0,
                                         base=D - 1, pattern=[[D, H]], channel_multiplier=-1))
            link(nc.gpsimd.memset(halves[:, :], 1.0))
            link(nc.gpsimd.affine_select(out=halves[:, 0:1], in_=halves[:, 0:1], compare_op=ALU.is_ge, fill=0.0,
                                         base=RANK - 1, pattern=[[0, 1]], channel_multiplier=-1))
            link(nc.gpsimd.affine_select(out=halves[:, 1:2], in_=halves[:, 1:2], compare_op=ALU.is_ge, fill=0.0,
                                         base=-RANK, pattern=[[0, 1]], channel_multiplier=1))
            pool.sem_inc(s["consts"], 1)

            def power(dst, src, width, what):
                const = (minus_half if what < 0 else plus_half)[0:src.shape[0], 0:1]
                return nc.gpsimd.tensor_tensor(dst, src, const.to_broadcast([src.shape[0], width]), ALU.pow)

            pool.wait_ge(s["small"], 1)
            for b in range(B):
                pool.wait_ge(s["veps_s"], b + 1)
                t0 = b * TPB
                power(rstd1[:, t0:t0 + TPB], veps1[:, t0:t0 + TPB], TPB, -1).then_inc(s["rstd_s"], 1)
            pool.wait_ge(s["csum_s"], 1)
            power(crs[:, :], cms[:, :], 1, -1).then_inc(s["cpow_s"], 1)

            pool.wait_ge(s["moved"], upto("bproj"))
            for b in range(B):
                pool.wait_ge(s[f"x{b}_in"], 16)
                nc.gpsimd.tensor_tensor(xb[:, TPB * b:TPB * (b + 1), :], x_sb[:, TPB * b:TPB * (b + 1), :],
                                        rowb[:, ROW:ROW + C].rearrange("p (o c) -> p o c", o=1).to_broadcast([P, TPB, C]),
                                        ALU.add).then_inc(s["xb_s"], 1)

            def mask(pr):
                g, q = g_of(pr), pr[1]
                pool.wait_ge(s["cut_s"], g + 1)
                pool.sem_inc(s["fence"], 1)
                for w in range(2):
                    if pair(pr[0], pr[1] - 1) is not None:
                        pool.wait_ge(s["masked"], 2 * g + w - 1)
                        pool.sem_inc(s["fence"], 1)
                    nc.gpsimd.tensor_scalar(keep[w][:, :], S[2 * q + w], thr[q][:, w:w + 1], None,
                                            ALU.is_ge).then_inc(s["keep_s"], 1)
                for w in range(2):
                    e = E[(2 * q + w) % 4]
                    pool.wait_ge(s["exp_done"], 2 * g + w + 1)
                    pool.sem_inc(s["fence"], 1)
                    pool.wait_ge(s["keep_s"], 2 * g + w + 1)
                    nc.gpsimd.tensor_tensor(e, e, keep[w][:, :], ALU.mult).then_inc(s["masked"], 1)

            for b in range(B):
                pool.wait_ge(s["kv_sb"], b + 1)
                nc.gpsimd.tensor_tensor(kvb[:, b, :], kvb[:, b, :], blockmask[:, :, :].rearrange("p h e -> p (h e)"),
                                        ALU.mult).then_inc(s["kv_own"], 1)
            for q in range(4):
                mask((0, q))
            with pool.Fori(1, PAIRS // 4 - 1) as m:
                for q in range(4):
                    mask((m, q))
            for q in range(2):
                mask((PAIRS // 4 - 1, q))

            def lns(k):
                for b in range(B):
                    pool.wait_ge(s["ln_e"], 2 * k + b + 1)
                    power(rstd1[:, b * TPB:(b + 1) * TPB], veps1[:, b * TPB:(b + 1) * TPB], TPB, -1).then_inc(s["ln_r"], 1)

            lns(0)
            for it in range(ITERS):
                for b in range(B):
                    pool.wait_ge(s["ms_sb"], 2 * it + b + 1)
                    power(rn[:, b], mse[:, b], TPB, -1).then_inc(s["rn_s"], 1)
            lns(1)
            for b in range(B):
                pool.wait_ge(s["s2_s"], b + 1)
                power(sr[:, b].rearrange("p j e -> p (j e)"), s2[:, b].rearrange("p j e -> p (j e)"),
                      TPB * EXPERTS, 1).then_inc(s["sr_s"], 1)

        @block.tensor
        def _(pe):
            g = [0]

            def group():
                if g[0] >= 2:
                    pe.wait_ge(s["moved"], g[0] - 1)
                g[0] += 1
                return bank[2 + (g[0] - 1) % 2]

            def transposes(srcs, rows=P):
                bk = group()
                for i, src in enumerate(srcs):
                    last = nc.tensor.transpose(bk[0:src.shape[1], i * rows:(i + 1) * rows], src, ident[0:rows, 0:rows])
                last.then_inc(s["group_ps"], 1)

            pe.wait_ge(s["consts"], 1)
            pe.wait_ge(s["wqkv_in"], 16)
            transposes([wqkv[:, i, :] for i in range(3)])
            for b in range(B):
                pe.wait_ge(s["xn_s"], TPB * (b + 1))
                transposes([xn[:, TPB * b + j, :] for j in range(TPB)])
            pe.wait_ge(s["rows_in"], 16 * 7)
            pe.wait_ge(s["small"], 1)
            nc.tensor.matmul(group()[:, 0:ROW], ones_row[:, :], row[:, 0:ROW], start=True, stop=True).then_inc(s["group_ps"], 1)
            nc.tensor.matmul(group()[:, 0:C], ones_row[:, :], row[:, ROW:ROW + C], start=True, stop=True).then_inc(s["group_ps"], 1)
            pe.wait_ge(s["cols_in_s"], 16 * 4)
            bk = group()
            nc.tensor.transpose(bk[:, 0:8], cols_in[:, :], ident[0:8, 0:8]).then_inc(s["group_ps"], 1)

            def qkv(b):
                pe.wait_ge(s["moved"], upto(f"xn{b}"))
                for j in range(TPB):
                    t = b * TPB + j
                    if t >= 2:
                        pe.wait_ge(s["qk_sb"], t - 1)
                        pe.wait_ge(s["v_sb"], t - 1)
                    nc.tensor.matmul(bank[t % 2][:, 0:3 * C], xnT[:, t * P:(t + 1) * P], wqkvT[:, :],
                                     start=True, stop=True).then_inc(s["qkv_ps"], 1)

            def turned_qk(b):
                pe.wait_ge(s["qk_ready"], b + 1)
                for i in range(2):
                    transposes([qk[:, TPB * b + j, i * C:(i + 1) * C] for j in range(TPB)])

            qkv(0)
            qkv(1)
            pe.wait_ge(s["xw_in"], 16 * 6)
            transposes([wproj[:, :]])
            transposes([wk[:, :], wv[:, :]])
            pe.wait_ge(s["pn_s"], 1)
            transposes([pn[:, :]], rows=B * M)
            pe.wait_ge(s["pnw_s"], 1)
            nc.tensor.matmul(group()[:, 0:B * M], wkvT[:, 0, :], pnTw[:, :], start=True, stop=True).then_inc(s["group_ps"], 1)
            pe.wait_ge(s["moved"], upto("kproj"))
            nc.tensor.matmul(group()[:, 0:B * M], wq[:, :], kpT[:, :], start=True, stop=True).then_inc(s["group_ps"], 1)
            nc.tensor.matmul(group()[:, 0:B * M], wkvT[:, 1, :], pnTw[:, :], start=True, stop=True).then_inc(s["group_ps"], 1)
            transposes([wih_sb[:, i, :] for i in range(3)])
            pe.wait_ge(s["moved"], upto("wih"))
            for b in range(B):
                nc.tensor.matmul(group()[0:M, 0:3 * C], vT[:, b * M:(b + 1) * M], wihT[:, :, :].rearrange("p a b -> p (a b)"),
                                 start=True, stop=True).then_inc(s["group_ps"], 1)
            transposes([whh_sb[:, i, :] for i in range(3)])
            pe.wait_ge(s["ffa_in"], 16)
            transposes([wa_sb[:, i, :] for i in range(4)])
            pe.wait_ge(s["ffb_in"], 16 * 4)
            for k in range(2):
                transposes([wb_sb[:, 2 * k + i // 2, i % 2, :] for i in range(4)])
            turned_qk(0)
            pe.wait_ge(s["ffu_in"], 16)
            for k in range(4):
                transposes([wup_sb[:, 4 * k + i, :] for i in range(4)])
            turned_qk(1)

            def scores(pr):
                (b, _), g = head_of(pr), g_of(pr)
                pe.wait_ge(s["qm_ready"], g + 1)
                for w in range(2):
                    if pair(pr[0], pr[1] - 1) is not None:
                        pe.wait_ge(s["scores_sb"], 2 * g + w - 1)
                    nc.tensor.matmul(bank[w][:, :], qm[pr[1] % 2][:, w * P:(w + 1) * P], kT[:, bass.ds(b * N, N)],
                                     start=True, stop=True).then_inc(s["scores_ps"], 1)

            def count_missed(pr):
                q = pr[1]
                if q % 2 == 0:
                    return
                pe.wait_ge(s["missed_s"], 2 * pr[0] + q // 2 + 1)
                if pair(pr[0], q - 2) is not None:
                    pe.wait_ge(s["flags_s"], 2 * pr[0] + q // 2)
                nc.tensor.matmul(flagbank[0:1, 0:4], ones_col[:, :], missed[:, :], start=True, stop=True)
                for i in range(4):
                    last = nc.tensor.matmul(flagbank[0:1, 4:5], ones_col[:, :], missed[:, i:i + 1], start=(i == 0), stop=(i == 3))
                last.then_inc(s["flag_ps"], 1)

            def turn(pr):
                g, q = g_of(pr), pr[1]
                for w in range(2):
                    pe.wait_ge(s["masked"], 2 * g + w + 1)
                    pe.wait_ge(s["pt_sb"], 2 * g + w + 1)
                    for c in range(TPB):
                        last = nc.tensor.transpose(bank[2 + w][:, c * P:(c + 1) * P],
                                                   E[(2 * q + w) % 4][:, c * P:(c + 1) * P], ident[:, :])
                    last.then_inc(s["pt_ps"], 1)

            def weigh(pr):
                (b, h), g, q = head_of(pr), g_of(pr), pr[1]
                for w in range(2):
                    j = 2 * (q % 2) + w
                    pe.wait_ge(s["pt_sb"], 2 * g + w + 3)
                    o = b * (o_at(TPB + j) - o_at(j)) + h * DV + o_at(j)
                    values = vaug[:, :, :, :].rearrange("p t h e -> p (t h e)")
                    for c in range(TPB):
                        last = nc.tensor.matmul(obank[:, bass.ds(o, DV)], PT[w][:, c * P:(c + 1) * P],
                                                values[:, bass.ds(b * (TPB * H * DV) + h * DV + c * H * DV, DV)],
                                                start=(c == 0), stop=(c == TPB - 1))
                    last.then_inc(s["av_done"], 1)

            def slot(m, q):
                for step, ahead in ((turn, -4), (scores, 1), (count_missed, -1), (weigh, -4)):
                    pr = pair(m, q + ahead)
                    if pr is not None:
                        step(pr)

            def down_weights(k):
                transposes([wdn_sb[:, 2 * k + i // 2, (i % 2) * P:(i % 2 + 1) * P] for i in range(4)])

            pe.wait_ge(s["moved"], upto("kT1"))
            pe.wait_ge(s["qk_sb"], T)
            pe.wait_ge(s["v_sb"], T)
            slot(0, -1)
            pe.wait_ge(s["ffd_in"], 16)
            down_weights(0)
            down_weights(1)
            slot(0, 0)
            down_weights(2)
            down_weights(3)
            for b in range(B):
                pe.wait_ge(s["fready"], b + 1)
                transposes([feat[:, TPB * b + j, 0:C] for j in range(TPB)])
            assert g[0] == len(GROUPS)
            slot(0, 1)
            pe.wait_ge(s["moved"], len(GROUPS))
            for b in range(B):
                for j in range(TPB):
                    last = nc.tensor.matmul(bank[2 + b][:, 0:H * DV], feat[:, TPB * b + j, C:2 * C],
                                            vaug[:, TPB * b + j].rearrange("p h e -> p (h e)"),
                                            start=(j == 0), stop=(j == TPB - 1))
                last.then_inc(s["kv_ps"], 1)
            for q in range(2, 4):
                slot(0, q)
            pe.wait_ge(s["kv_sb"], B)
            with pe.Fori(1, PAIRS // 4 - 1) as m:
                for q in range(4):
                    slot(m, q)

            def linear(b):
                for j in range(TPB):
                    last = nc.tensor.matmul(work(b, j // 2)[:, (j % 2) * H * DV:(j % 2 + 1) * H * DV],
                                            qfT[:, (TPB * b + j) * P:(TPB * b + j + 1) * P], kvb[:, b, :],
                                            start=True, stop=True)
                last.then_inc(s["ol_ps"], 1)

            end = PAIRS // 4 - 1
            for q in range(4):
                slot(end, q)
            turn((end, 0))
            pe.wait_ge(s["scores_sb"], BH * TPB)
            pe.wait_ge(s["kv_own"], B)
            linear(0)
            count_missed((end, 3))
            weigh((end, 0))
            for q in range(1, 4):
                turn((end, q))
                weigh((end, q))
            pe.wait_ge(s["pt_sb"], BH * TPB + 2)
            linear(1)

            for b in range(B):
                pe.wait_ge(s["o_ready"], b + 1)
                for j in range(TPB):
                    last = nc.tensor.transpose(work(b, 0)[:, j * P:(j + 1) * P], o_tok[:, b, j, :], ident[:, :])
                last.then_inc(s["ot_ps"], 1)
            for b in range(B):
                pe.wait_ge(s["ot_sb"], b + 1)
                for j in range(TPB):
                    last = nc.tensor.matmul(work(b, 1)[:, j * P:(j + 1) * P], oT[:, b, j * P:(j + 1) * P], wprojT[:, :],
                                            start=True, stop=True)
                last.then_inc(s["pr_ps"], 1)

            def layer_norm(k):
                for b in range(B):
                    pe.wait_ge(s["ln_n"], TPB * (2 * k + b + 1))
                    for j in range(TPB):
                        last = nc.tensor.transpose(work(b, 0)[:, j * P:(j + 1) * P], xn[:, b * TPB + j, :], ident[:, :])
                    last.then_inc(s["ln_t"], 1)

            layer_norm(0)
            for it in range(ITERS):
                for b in range(B):
                    if it == 0:
                        pe.wait_ge(s["ln_h"], b + 1)
                    else:
                        pe.wait_ge(s["slot_s"], 2 * (it - 1) + b + 1)
                    for j in range(TPB):
                        nc.tensor.matmul(work(b, 1)[:, j * WIDE:(j + 1) * WIDE], slots[:, b, j * P:(j + 1) * P],
                                         foldw[:, :, :].rearrange("p i m -> p (i m)"), start=True, stop=True)
                    pe.wait_ge(s["sl_sq"], 2 * it + b + 1)
                    for j in range(TPB):
                        last = nc.tensor.matmul(work(b, 0)[:, j * WIDE:(j + 1) * WIDE], sqT[:, b, j * P:(j + 1) * P],
                                                mean_mat[:, 0:WIDE], start=True, stop=True)
                    last.then_inc(s["ms_ps"], 1)

                def slots_part(b, bk, i):
                    return nc.tensor.matmul(work(b, bk), whhT[:, i, :], slots[:, b, :], start=True, stop=(bk == 0))

                def turned_scores(b):
                    pe.wait_ge(s["sct_s"], 2 * it + b + 1)
                    for j in range(TPB):
                        last = nc.tensor.transpose(work(b, 0)[0:M, j * P:(j + 1) * P], sct[:, b, j, :], ident[:, :])
                    last.then_inc(s["sc_t"], 1)

                def token_sums(b):
                    pe.wait_ge(s["srec_s"], 2 * it + b + 1)
                    pe.wait_ge(s["ex_s"], 2 * it + b + 1)
                    for j in range(TPB):
                        last = nc.tensor.matmul(work(b, 1)[:, j * WIDE:(j + 1) * WIDE], ex[:, b, j * P:(j + 1) * P],
                                                srec[:, b:b + 1].to_broadcast([M, WIDE]), start=True, stop=True)
                    last.then_inc(s["den_ps"], 1)

                def spread_inverse(b):
                    pe.wait_ge(s["drc_s"], 2 * it + b + 1)
                    for j in range(TPB):
                        last = nc.tensor.matmul(work(b, 1)[0:M, j * P:(j + 1) * P], drc[:, b, j:j + 1].to_broadcast([P, M]),
                                                ident[:, :], start=True, stop=True)
                    last.then_inc(s["rb_ps"], 1)

                turned_scores(0)
                slots_part(0, 2, 0)
                turned_scores(1)
                slots_part(1, 2, 0)
                token_sums(0)
                slots_part(0, 0, 2).then_inc(s["hn_ps"], 1)
                token_sums(1)
                slots_part(1, 0, 2).then_inc(s["hn_ps"], 1)
                spread_inverse(0)
                slots_part(0, 3, 1)
                spread_inverse(1)
                slots_part(1, 3, 1)
                for b in range(B):
                    pe.wait_ge(s["at_s"], 2 * it + b + 1)
                    for bk, i in ((2, 0), (1, 2), (3, 1)):
                        nc.tensor.matmul(work(b, bk), gvs[:, b, i * C:(i + 1) * C], at[:, b, :], start=(bk == 1), stop=True
                                         ).then_inc(s["g_ps"], 1)
            for b in range(B):
                pe.wait_ge(s["slot_s"], 2 * (ITERS - 1) + b + 1)
                for j in range(TPB):
                    last = nc.tensor.transpose(work(b, 1)[:, j * P:(j + 1) * P], slots[:, b, j * P:(j + 1) * P], ident[:, :])
                last.then_inc(s["so_ps"], 1)
            layer_norm(1)

            def gates(b):
                pe.wait_ge(s["ln_h"], 2 + (b + 1))
                for c in range(4):
                    if b == 1 and c < 2:
                        pe.wait_ge(s["gh_s"], c + 3)
                    if b == 1 and c == 2:
                        pe.wait_ge(s["ln_h"], 4)
                    nc.tensor.matmul(gate_bank(b, c), waT[:, c, :], hT[:, b, :], start=True, stop=True).then_inc(s["ga_ps"], 1)

            def squared_scores(b):
                pe.wait_ge(s["gh_s"], 7 + b)
                for j in range(TPB):
                    for c in range(4):
                        pe.wait_ge(s["sqg_s"], 4 * b + c + 1)
                        last = nc.tensor.matmul(bank[2 + b][:, j * WIDE:(j + 1) * WIDE],
                                                sqg[b][:, c, j * P:(j + 1) * P], blk[:, c, :], start=(c == 0), stop=(c == 3))
                last.then_inc(s["sc_ps"], 1)

            def gate_and_up(k):
                b, e = k // EXPERTS, k % EXPERTS
                pe.wait_ge(s["gh_s"], 4 * b + e // 2 + 1)
                for f in range(2):
                    if k:
                        pe.wait_ge(s["a2_s"], 2 * k + f - 1)
                    elif f:
                        pe.wait_ge(s["gh_s"], 2)
                    o = (e % 2) * RANK
                    nc.tensor.matmul(ob(f), wbT[o:o + RANK, e // 2, f, :], gh[b][o:o + RANK, e // 2, :], start=True, stop=True)
                    nc.tensor.matmul(ob(2 + f), wupT[:, 2 * e + f, :], hT[:, b, :], start=True, stop=True
                                     ).then_inc(s["gu_ps"], 1)

            def down(k):
                pe.wait_ge(s["a2_s"], 2 * k + 2)
                if k >= 2:
                    pe.wait_ge(s["acc_s"], k - 1)
                else:
                    pe.wait_ge(s["s2_s"], k + 1)
                for j in range(TPB):
                    for f in range(2):
                        last = nc.tensor.matmul(bank[2 + k % 2][:, j * P:(j + 1) * P], a2[2 * (k % 2) + f][:, j * P:(j + 1) * P],
                                                wdnT[:, k % EXPERTS, f, :], start=(f == 0), stop=(f == 1))
                last.then_inc(s["y_ps"], 1)

            gates(0)
            gate_and_up(0)
            gates(1)
            squared_scores(0)
            gate_and_up(1)
            squared_scores(1)
            down(0)
            for k in range(2, B * EXPERTS):
                gate_and_up(k)
                down(k - 1)
            down(B * EXPERTS - 1)

        @block.scalar
        def _(act):
            act.dma_start(wqkv[:, :, :], Wqkv.rearrange("(g p) c -> p g c", p=P)).then_inc(s["wqkv_in"], 16)

            g = [0]

            def copy(dst, src):
                return nc.scalar.activation(dst, src, ACT.Copy)

            def move(name, dst, rows, width):
                assert GROUPS[g[0]] == name
                act.wait_ge(s["group_ps"], g[0] + 1)
                copy(dst, bank[2 + g[0] % 2][0:rows, 0:width]).then_inc(s["moved"], 1)
                g[0] += 1

            act.wait_ge(s["ctx_in_s"], 16)
            nc.scalar.activation(csq[:, :], ctx_sb[:, :], ACT.Square, accum_out=css[:, :]).then_inc(s["achain"], 1)
            move("wqkv", wqkvT[:, :], P, 3 * C)
            for b in range(B):
                move(f"xn{b}", xnT[:, b * N:(b + 1) * N], P, N)
            move("rows", rowb[:, 0:ROW], P, ROW)
            move("bproj", rowb[:, ROW:ROW + C], P, C)
            move("cols", cols[:, :], P, 8)
            act.wait_ge(s["moved"], upto("rows"))
            nc.scalar.activation(alpha_t[:, :], rowb[:, ROW - H:ROW], ACT.Tanh, scale=0.5).then_inc(s["act_c"], 1)

            def squares(b):
                act.wait_ge(s["dsub"], b + 1)
                nc.scalar.activation(sqd[:, b], diff[:, b], ACT.Square).then_inc(s["dsq"], 1)

            def exps(b):
                act.wait_ge(s["fmax_s"], b + 1)
                nc.scalar.activation(sqd[:, b], diff[:, b], ACT.Exp).then_inc(s["fexp"], 1)

            squares(0)
            squares(1)
            for b in range(B):
                act.wait_ge(s["dvar"], b + 1)
                nc.scalar.activation(gstd[:, b], gveps[:, b], ACT.Sqrt).then_inc(s["gstd_s"], 1)
            move("proj", wprojT[:, :], P, C)
            move("wk_wv", wkvT[:, :, :].rearrange("p a b -> p (a b)"), P, 2 * C)
            move("ctx", pnT[:, :], P, B * M)
            move("kproj", kpT[:, :], P, B * M)
            move("qk_fold", fold[:, :], P, B * M)
            move("vproj", vT[:, :], P, B * M)
            move("wih", wihT[:, :, :].rearrange("p a b -> p (a b)"), P, 3 * C)
            for b in range(B):
                move(f"values{b}", gv[:, b, :], M, 3 * C)
            move("whh", whhT[:, :, :].rearrange("p a b -> p (a b)"), P, 3 * C)
            move("wa", waT[:, :, :].rearrange("p a b -> p (a b)"), P, N)
            for k in range(2):
                move(f"wb{k}", wbT[:, 2 * k:2 * k + 2].rearrange("p a f b -> p (a f b)"), P, N)

            def moved_qk(b):
                move(f"qT{b}", qT[:, b * N:(b + 1) * N], P, N)
                move(f"kT{b}", kT[:, b * N:(b + 1) * N], P, N)

            moved_qk(0)
            exps(0)
            for k in range(4):
                if k == 2:
                    exps(1)
                move(f"wup{k}", wupT[:, 4 * k:4 * k + 4, :].rearrange("p a b -> p (a b)"), P, N)
            moved_qk(1)

            def down_weights(k):
                move(f"wdn{k}", wdnT[:, 2 * k:2 * k + 2].rearrange("p a f b -> p (a f b)"), P, N)

            def q_mask(pr):
                (b, h), g, p = head_of(pr), g_of(pr), pr[1] % 2
                if pair(pr[0], pr[1] - 2) is not None:
                    act.wait_ge(s["scores_ps"], 2 * g - 2)
                act.sem_inc(s["fence"], 1)
                nc.scalar.activation(qm[p][:, :], qT[:, bass.ds(b * N + p * 2 * P, 2 * P)], ACT.Copy,
                                     scale=headmask[:, bass.ds(h, 1)]).then_inc(s["qm_ready"], 1)

            def scores_out(pr):
                g, q = g_of(pr), pr[1]
                for w in range(2):
                    act.wait_ge(s["scores_ps"], 2 * g + w + 1)
                    if pair(pr[0], q - 4) is not None:
                        act.wait_ge(s["masked"], 2 * g + w - 7)
                    nc.scalar.activation(S[2 * q + w], bank[w][:, :], ACT.Copy, scale=float(D) ** -0.5
                                         ).then_inc(s["scores_sb"], 1)

            def compare(pr):
                g, q = g_of(pr), pr[1]
                act.wait_ge(s["thr_s"], g + 1)
                act.sem_inc(s["fence"], 1)
                for w in range(2):
                    if w or pair(pr[0], q - 1) is not None:
                        act.wait_ge(s["balance_s"], 2 * g + w)
                    nc.scalar.activation(signs[:, :], S[2 * q + w], ACT.Sign, bias=thr[q][:, w:w + 1], scale=-1.0,
                                         accum_out=balance[:, 2 * (q % 2) + w:2 * (q % 2) + w + 1]).then_inc(s["balance_s"], 1)

            def exponentials(pr):
                g, q = g_of(pr), pr[1]
                act.wait_ge(s["negmax_s"], g + 1)
                if pair(pr[0], q - 2) is not None:
                    act.wait_ge(s["pt_ps"], 2 * g - 2)
                if q == 0 and pair(pr[0], q - 1) is not None:
                    act.wait_ge(s["z_saved"], pr[0])
                for w in range(2):
                    nc.scalar.activation(E[(2 * q + w) % 4], S[2 * q + w], ACT.Exp, bias=negmax[q][:, w:w + 1],
                                         accum_out=zb[:, 2 * q + w:2 * q + w + 1]).then_inc(s["exp_done"], 1)
                if q == 3:
                    act.wait_ge(s["exp_done"], 2 * g + 2)
                    act.sem_inc(s["fence"], 1)
                    copy(zall[:, bass.ds(pr[0], 1), :], zb[:, :].rearrange("p (o j) -> p o j", o=1)).then_inc(s["z_saved"], 1)

            def turned_out(pr):
                g = g_of(pr)
                for w in range(2):
                    act.wait_ge(s["pt_ps"], 2 * g + w + 1)
                    act.wait_ge(s["av_done"], 2 * g + w + 1)
                    copy(PT[w], bank[2 + w][:, :]).then_inc(s["pt_sb"], 1)

            def slot(m, q):
                first = [(compare, -1), (turned_out, -4)]
                if q % 2:
                    first.reverse()
                for step, ahead in (*first, (scores_out, 1), (q_mask, 2), (exponentials, -2)):
                    pr = pair(m, q + ahead)
                    if pr is not None:
                        step(pr)

            act.sem_inc(s["pt_sb"], 2)
            act.sem_inc(s["av_done"], 2)
            for q in range(-3, 0):
                slot(0, q)
            down_weights(0)
            down_weights(1)
            slot(0, 0)
            down_weights(2)
            down_weights(3)
            move("qf0", qfT[:, 0:N], P, N)
            move("qf1", qfT[:, N:2 * N], P, N)
            slot(0, 1)
            for b in range(B):
                act.wait_ge(s["kv_ps"], b + 1)
                copy(kvb[:, b, :], bank[2 + b][:, 0:H * DV]).then_inc(s["kv_sb"], 1)
            for q in range(2, 4):
                slot(0, q)
            with act.Fori(1, PAIRS // 4 - 1) as m:
                for q in range(4):
                    slot(m, q)
            for q in range(8):
                slot(PAIRS // 4 - 1, q)

            for b in range(B):
                act.wait_ge(s["ot_ps"], b + 1)
                copy(oT[:, b, :], work(b, 0)).then_inc(s["ot_sb"], 1)

            def layer_norm(k, dst):
                for b in range(B):
                    act.wait_ge(s["ln_t"], 2 * k + b + 1)
                    copy(dst[:, b, :], work(b, 0)).then_inc(s["ln_h"], 1)

            layer_norm(0, slots)

            def slot_squares(it, b):
                if it == 0:
                    act.wait_ge(s["ln_h"], b + 1)
                elif it < ITERS:
                    act.wait_ge(s["slot_s"], 2 * (it - 1) + b + 1)
                    act.wait_ge(s["ms_ps"], 2 * (it - 1) + b + 1)
                else:
                    return
                nc.scalar.activation(sqT[:, b, :], slots[:, b, :], ACT.Square).then_inc(s["sl_sq"], 1)

            slot_squares(0, 0)
            slot_squares(0, 1)
            for it in range(ITERS):
                for b in range(B):
                    act.wait_ge(s["ms_ps"], 2 * it + b + 1)
                    if it:
                        act.wait_ge(s["rn_s"], 2 * (it - 1) + b + 1)
                    nc.scalar.activation(mse[:, b, :], work(b, 0)[:, 0:TPB * WIDE:WIDE], ACT.Copy, bias=RMS_EPS).then_inc(s["ms_sb"], 1)
                for b in range(B):
                    act.wait_ge(s["snm_s"], 2 * it + b + 1)
                    if it:
                        act.wait_ge(s["at_s"], 2 * (it - 1) + b + 1)
                    nc.scalar.activation(ex[:, b, :], work(b, 0)[0:M, :], ACT.Exp, bias=snm[:, b:b + 1], scale=SCALE,
                                         accum_out=ssum[:, b:b + 1]).then_inc(s["ex_s"], 1)
                for b in range(B):
                    act.wait_ge(s["hn_ps"], 2 * it + b + 1)
                    nc.scalar.activation(hw[:, b, :], work(b, 0), ACT.Identity, bias=half_hn[:, :], scale=0.5).then_inc(s["hw_s"], 1)
                for b in range(B):
                    act.wait_ge(s["g_ps"], 3 * (2 * it + b) + 1)
                    nc.scalar.activation(rt[:, b, :], work(b, 2), ACT.Tanh, bias=half_rz[:, 0:1], scale=0.5).then_inc(s["rt_s"], 1)
                    act.wait_ge(s["g_ps"], 3 * (2 * it + b) + 3)
                    nc.scalar.activation(zt[:, b, :], work(b, 3), ACT.Tanh, bias=half_rz[:, 1:2], scale=0.5).then_inc(s["zt_s"], 1)
                    if b == 1:
                        slot_squares(it + 1, 0)
                    act.wait_ge(s["t2_s"], 2 * it + b + 1)
                    nc.scalar.activation(nn[:, b, :], t2[:, b, :], ACT.Tanh, bias=cols[:, 4:5]).then_inc(s["n_s"], 1)
                slot_squares(it + 1, 1)
            layer_norm(1, hT)

            def gates_out(b):
                for c in range(4):
                    act.wait_ge(s["ga_ps"], 4 * b + c + 1)
                    copy(gh[b][:, c, :], gate_bank(b, c)).then_inc(s["gh_s"], 1)

            def gate_tanh(k):
                for f in range(2):
                    kk = 2 * k + f
                    act.wait_ge(s["gu_ps"], kk + 1)
                    if k:
                        act.wait_ge(s["a2_s"], kk - 1)
                    nc.scalar.activation(th[f][:, :], ob(f), ACT.Tanh, scale=0.5).then_inc(s["th_s"], 1)

            gates_out(0)
            gate_tanh(0)
            gates_out(1)
            for k in range(1, B * EXPERTS):
                gate_tanh(k)
                if k in RANKED:
                    b = RANKED.index(k)
                    act.wait_ge(s["sd_s"], b + 1)
                    nc.scalar.activation(sexp[:, b, :], sdif[:, b, :], ACT.Exp).then_inc(s["se_s"], 1)

        @block.vector
        def _(dve):
            v = nc.vector
            n = [0]

            def link(ins):
                n[0] += 1
                ins.then_inc(s["dchain"], 1)
                dve.wait_ge(s["dchain"], n[0])

            v.memset(minus_half[:, :], -0.5)
            v.memset(plus_half[:, :], 0.5)
            v.memset(mean_mat[:, :], 1.0 / C)
            v.memset(ones_col[:, :], 1.0)
            for lo in lower:
                v.memset(lo[:, :, 0:1], -REMOVED)
            v.memset(vaug[:, :, :, D:DV], 1.0)
            for e in range(EXPERTS):
                v.memset(iota8[:, e:e + 1], float(e))
            v.memset(blk[:, :, :], 0.0)
            link(v.memset(ones_row[:, :], 1.0))
            dve.sem_inc(s["small"], 1)

            for b in range(B):
                dve.wait_ge(s[f"x{b}_in"], 16)
                for j in range(TPB):
                    t = b * TPB + j
                    v.bn_stats(stats[:, t, :], x_sb[:, t, :]).then_inc(s["stat_s"], 1)
                for j in range(TPB):
                    t = b * TPB + j
                    dve.wait_ge(s["stat_s"], t + 1)
                    v.bn_aggr(mv[:, t, :], stats[:, t, :]).then_inc(s["mv_s"], 1)
                dve.wait_ge(s["mv_s"], TPB * (b + 1))
                v.tensor_scalar(veps1[:, b * TPB:(b + 1) * TPB], mv[:, b * TPB:(b + 1) * TPB, 1], LN_EPS, None,
                                ALU.add).then_inc(s["veps_s"], 1)
            for b in range(B):
                dve.wait_ge(s["rstd_s"], b + 1)
                for j in range(TPB):
                    t = b * TPB + j
                    v.tensor_scalar(xn[:, t, :], x_sb[:, t, :], mv[:, t, 0:1], rstd1[:, t:t + 1],
                                    ALU.subtract, ALU.mult).then_inc(s["xn_s"], 1)
            dve.wait_ge(s["consts"], 1)
            for c in range(4):
                v.tensor_copy(blk[:, c, 2 * c:2 * c + 2], halves[:, :])
            v.tensor_copy(blockmask[:, :, :], headmask[:, :].rearrange("p (h o) -> p h o", o=1).to_broadcast([P, H, DV]))
            dve.wait_ge(s["moved"], upto("cols"))
            for i in range(2):
                for dst, o in ((gammab, 3 * C), (betab, 3 * C + 2 * D)):
                    v.tensor_copy(dst[:, i], rowb[:, o + i * D:o + (i + 1) * D].rearrange("p (o d) -> p o d", o=1)
                                  .to_broadcast([P, H, D]))
            link(v.tensor_tensor(brz[:, :], cols[:, 2:4], cols[:, 5:7], ALU.add))
            v.tensor_scalar(half_rz[:, :], brz[:, :], 0.5, None, ALU.mult)
            v.tensor_scalar(half_hn[:, :], cols[:, 7:8], 0.5, None, ALU.mult)
            dve.wait_ge(s["act_c"], 1)
            v.tensor_scalar(mix[:, 0, :], alpha_t[:, :], 0.5, 0.5, ALU.mult, ALU.add)
            link(v.tensor_scalar(mix[:, 1, :], alpha_t[:, :], -0.5, 0.5, ALU.mult, ALU.add))
            dve.wait_ge(s["achain"], 1)
            v.tensor_scalar(cms[:, :], css[:, :], 1.0 / C, RMS_EPS, ALU.mult, ALU.add).then_inc(s["csum_s"], 1)
            dve.wait_ge(s["cpow_s"], 1)
            v.tensor_scalar(pn[:, :], ctx_sb[:, :], crs[:, :], None, ALU.mult).then_inc(s["pn_s"], 1)

            def groups(ap):
                return ap.rearrange("p (g d) -> p g d", d=D)

            def each(ap):
                return ap.rearrange("p (g o) -> p g o", o=1).to_broadcast([P, GR, D])

            def qk_flat(b):
                return qk[:, TPB * b:TPB * (b + 1), :].rearrange("p t c -> p (t c)")

            for b in range(B):
                for j in range(TPB):
                    t = b * TPB + j
                    dve.wait_ge(s["qkv_ps"], t + 1)
                    v.tensor_tensor(qk[:, t, :], bank[t % 2][:, 0:2 * C], rowb[:, 0:2 * C], ALU.add).then_inc(s["qk_sb"], 1)
                    v.tensor_tensor(vaug[:, t, :, 0:D], bank[t % 2][:, 2 * C:3 * C].rearrange("p (h d) -> p h d", d=D),
                                    rowb[:, 2 * C:3 * C].rearrange("p (h d) -> p h d", d=D), ALU.add).then_inc(s["v_sb"], 1)
                dve.wait_ge(s["qk_sb"], TPB * (b + 1))
                link(v.tensor_reduce(gsum[:, b], groups(qk_flat(b)), op=ALU.add, axis=AX.X))
                link(v.tensor_scalar(gmean[:, b], gsum[:, b], 1.0 / D, None, ALU.mult))
                v.tensor_tensor(groups(diff[:, b]), groups(qk_flat(b)), each(gmean[:, b]), ALU.subtract).then_inc(s["dsub"], 1)
            for b in range(B):
                dve.wait_ge(s["dsq"], b + 1)
                link(v.tensor_reduce(gvar[:, b], groups(sqd[:, b]), op=ALU.add, axis=AX.X))
                v.tensor_scalar(gveps[:, b], gvar[:, b], 1.0 / D, LN_EPS, ALU.mult, ALU.add).then_inc(s["dvar"], 1)
            both = lambda a: a[:, :, :].rearrange("p b g -> p (b g)")
            dve.wait_ge(s["gstd_s"], 2)
            link(v.reciprocal(both(grough), both(gstd)))
            link(v.tensor_tensor(both(gprod), both(grough), both(gveps), ALU.mult))
            link(v.scalar_tensor_tensor(out=both(gfix), in0=both(grough), scalar=-0.5, in1=both(gprod), op0=ALU.mult, op1=ALU.mult))
            link(v.scalar_tensor_tensor(out=both(grstd), in0=both(gfix), scalar=1.5, in1=both(grough), op0=ALU.add, op1=ALU.mult))
            dve.wait_ge(s["moved"], upto("ctx"))
            v.tensor_scalar(pnTw[:, :], pnT[:, :], cols[:, 1:2], None, ALU.mult).then_inc(s["pnw_s"], 1)
            for b in range(B):
                dve.wait_ge(s["dsub"], b + 1)
                link(v.tensor_tensor(groups(qk_flat(b)), groups(diff[:, b]), each(grstd[:, b]), ALU.mult))
                x3 = qk[:, TPB * b:TPB * (b + 1), :]
                for last, table, op in ((False, gammab, ALU.mult), (True, betab, ALU.add)):
                    tb = table[:, :, :, :].rearrange("p (o a) h d -> p o (a h d)", o=1).to_broadcast([P, TPB, 2 * C])
                    ins = v.tensor_tensor(x3, x3, tb, op)
                    if last:
                        ins.then_inc(s["qk_ready"], 1)
                    else:
                        link(ins)
            for b in range(B):
                dve.wait_ge(s["qk_ready"], b + 1)
                link(v.tensor_reduce(gmax[:, b], groups(qk_flat(b)), op=ALU.max, axis=AX.X))
                v.tensor_tensor(groups(diff[:, b]), groups(qk_flat(b)), each(gmax[:, b]), ALU.subtract).then_inc(s["fmax_s"], 1)
            for b in range(B):
                dve.wait_ge(s["fexp"], b + 1)
                link(v.tensor_reduce(gden[:, b], groups(sqd[:, b]), op=ALU.add, axis=AX.X))
                link(v.reciprocal(grec[:, b], gden[:, b]))
                v.tensor_tensor(groups(feat[:, TPB * b:TPB * (b + 1), :].rearrange("p t c -> p (t c)")), groups(sqd[:, b]),
                                each(grec[:, b]), ALU.mult).then_inc(s["fready"], 1)
            dve.wait_ge(s["moved"], upto("qk_fold"))
            for i in range(P // (B * M)):
                ins = v.tensor_scalar(foldw[:, i, :], fold[:, :], cols[:, 0:1], None, ALU.mult)
            link(ins)

            steps = [0]

            def step(ins):
                ins.then_inc(s["topk_step"], 1)
                steps[0] += 1
                return steps[0]

            def after(k):
                if k:
                    dve.wait_ge(s["topk_step"], k)

            def leader(pr, w, c):
                g, q = g_of(pr), pr[1]
                if c == 0:
                    dve.wait_ge(s["scores_sb"], 2 * g + w + 1)
                    dve.sem_inc(s["fence"], 1)
                ins = v.max(lead[q % 2][:, w, c, :], S[2 * q + w][:, c * CHUNK:(c + 1) * CHUNK])
                if c == CHUNKS - 1:
                    ins.then_inc(s["lead_s"], 1)

            def first_round(pr, w):
                g, z = g_of(pr), pr[1] % 2
                dve.wait_ge(s["lead_s"], 2 * g + w + 1)
                dve.sem_inc(s["fence"], 1)
                k = step(v.max(upper[z][:, w, 0:8], lead[z][:, w, :, 0:3]))
                step(v.max(lower[z][:, w, 1:9], lead[z][:, w, :, 3:8]))
                return k

            def threshold(pr, first):
                q, z = pr[1], pr[1] % 2
                up = upper[z]
                done = [first, first_round(pr, 1)]
                for r in range(3):
                    for w in range(2):
                        src = lead[z][:, w, :, 0:3] if r == 0 else rest[:, w, :]
                        dst = rest[:, w, :].rearrange("p (c k) -> p c k", k=3) if r == 0 else rest[:, w, :]
                        after(done[w])
                        done[w] = step(v.match_replace(dst, up[:, w, 8 * r:8 * r + 8], src, REMOVED))
                    if r == 0:
                        v.tensor_scalar(negmax[q][:, :], up[:, :, 0], -1.0, None, ALU.mult).then_inc(s["negmax_s"], 1)
                    for w in range(2):
                        after(done[w])
                        done[w] = step(v.max(up[:, w, 8 * r + 8:8 * r + 16], rest[:, w, :]))
                return done[1]

            def merge(pr, part, k):
                q, z = pr[1], pr[1] % 2
                after(k)
                if part == 0:
                    return step(v.tensor_tensor(cand[:, :, :], upper[z][:, :, TOPK - 1:TOPK - 10:-1], lower[z][:, :, :], ALU.min))
                v.tensor_reduce(thr[q][:, :], cand[:, :, :], op=ALU.max, axis=AX.X).then_inc(s["thr_s"], 1)
                return 0

            def find_missed(pr):
                dve.wait_ge(s["balance_s"], 2 * g_of(pr) + 2)
                dve.sem_inc(s["fence"], 1)
                v.tensor_scalar(missed[:, :], balance[:, :], float(N - 1 - 2 * (TOPK - 1)), None,
                                ALU.is_lt).then_inc(s["missed_s"], 1)

            def whole_row(pr, w):
                row_ = S[2 * pr[1] + w]
                k = 0
                for r in range(4):
                    if k:
                        dve.wait_ge(s["redo"], k)
                    v.max(top[:, 8 * r:8 * r + 8], row_ if r == 0 else W[0]).then_inc(s["redo"], 1)
                    k += 1
                    if r < 3:
                        dve.wait_ge(s["redo"], k)
                        v.match_replace(W[0], top[:, 8 * r:8 * r + 8], row_ if r == 0 else W[0], REMOVED).then_inc(s["redo"], 1)
                        k += 1
                dve.wait_ge(s["redo"], k)
                v.tensor_copy(thr[pr[1]][:, w:w + 1], top[:, TOPK - 1:TOPK]).then_inc(s["redo"], 1)
                dve.wait_ge(s["redo"], k + 1)
                dve.sem_clear(s["redo"])

            def settle(first, second):
                dve.wait_ge(s["flags_s"], 2 * first[0] + first[1] // 2 + 1)
                dve.sem_inc(s["fence"], 1)
                with dve.If(dve.value_load(flags[0:1, 4:5], min_val=0, max_val=4 * P)):
                    for i in range(4):
                        with dve.If(dve.value_load(flags[0:1, i:i + 1], min_val=0, max_val=P)):
                            whole_row((first, second)[i // 2], i % 2)
                dve.sem_inc(s["cut_s"], 2)

            MERGE, FIND, READ = (0, 2), 4, 9

            def first_leaders(pr, last, found):
                for c in range(CHUNKS):
                    if pr is not None:
                        leader(pr, 0, c)
                    if last is not None and c in MERGE:
                        found = merge(last, MERGE.index(c), found)

            def second_leaders(pr, last):
                for c in range(CHUNKS):
                    if pr is not None:
                        leader(pr, 1, c)
                    if last is not None and last[1] % 2 and c == FIND:
                        find_missed(last)
                    if last is not None and last[1] % 2 and c == READ:
                        dve.wait_ge(s["flag_ps"], 2 * last[0] + last[1] // 2 + 1)
                        v.tensor_copy(flags[:, :], flagbank[0:1, 0:5]).then_inc(s["flags_s"], 1)

            def turn(m):
                for q in range(4):
                    second_leaders((m, q), pair(m, q - 1))
                    first = first_round((m, q), 0)
                    if q % 2 == 0 and pair(m, q - 2) is not None:
                        settle(pair(m, q - 2), pair(m, q - 1))
                    found = threshold((m, q), first)
                    first_leaders(pair(m, q + 1), (m, q), found)
                dve.wait_ge(s["topk_step"], steps[0])
                dve.sem_clear(s["topk_step"])
                steps[0] = 0

            last = (PAIRS // 4 - 1, 3)
            first_leaders((0, 0), None, 0)
            turn(0)
            with dve.Fori(1, PAIRS // 4 - 1) as m:
                turn(m)
            turn(PAIRS // 4 - 1)
            second_leaders(None, last)
            settle((PAIRS // 4 - 1, 2), last)

            dve.wait_ge(s["masked"], 2 * PAIRS - 4)
            for q in range(2, 4):
                for w in range(2):
                    dve.wait_ge(s["exp_done"], 2 * (PAIRS - 4 + q) + w + 1)
                    e = E[(2 * q + w) % 4]
                    v.scalar_tensor_tensor(out=e, in0=S[2 * q + w], scalar=thr[q][:, w:w + 1], in1=e,
                                           op0=ALU.is_ge, op1=ALU.mult).then_inc(s["masked"], 1)

            def share(b, a, j0, j1):
                products = []
                for j in range(j0, j1):
                    if a == 0:
                        src = obank[:, o_at(TPB * b + j):o_at(TPB * b + j) + H * DV].rearrange("p (h e) -> p h e", e=DV)
                        z = zall[:, b * H // 2:(b + 1) * H // 2, :].rearrange("p m (i j) -> p (m i) j", j=TPB)[:, :, j]
                        ins = v.scalar_tensor_tensor(out=den[:, b, a, j, :], in0=z, scalar=ATT_EPS, in1=src[:, :, D],
                                                     op0=ALU.mult, op1=ALU.add)
                    else:
                        src = work(b, j // 2)[:, (j % 2) * H * DV:(j % 2 + 1) * H * DV].rearrange("p (h e) -> p h e", e=DV)
                        ins = v.tensor_scalar(den[:, b, a, j, :], src[:, :, D], LIN_EPS, None, ALU.add)
                    products.append(src)
                link(ins)
                link(v.reciprocal(rden[:, b, a, j0:j1].rearrange("p j h -> p (j h)"), den[:, b, a, j0:j1].rearrange("p j h -> p (j h)")))
                link(v.tensor_tensor(wden[:, b, a, j0:j1], rden[:, b, a, j0:j1],
                                     mix[:, a, :].rearrange("p (o h) -> p o h", o=1).to_broadcast([P, j1 - j0, H]), ALU.mult))
                for j, src in zip(range(j0, j1), products):
                    ins = v.tensor_tensor((o_s, o_l)[a][:, b, j, :].rearrange("p (h d) -> p h d", d=D), src[:, :, 0:D],
                                          wden[:, b, a, j, :].rearrange("p (h o) -> p h o", o=1).to_broadcast([P, H, D]), ALU.mult)
                link(ins)

            def mixed(b):
                v.tensor_tensor(o_tok[:, b], o_s[:, b], o_l[:, b], ALU.add).then_inc(s["o_ready"], 1)

            dve.wait_ge(s["ol_ps"], 1)
            share(0, 1, 0, TPB)
            dve.wait_ge(s["av_done"], BH * TPB // 2 + 2)
            dve.wait_ge(s["z_saved"], BH // 4)
            share(0, 0, 0, TPB - 1)
            dve.wait_ge(s["av_done"], BH * TPB + 2)
            share(0, 0, TPB - 1, TPB)
            mixed(0)
            dve.wait_ge(s["z_saved"], BH // 2)
            share(1, 0, 0, TPB)
            dve.wait_ge(s["ol_ps"], 2)
            share(1, 1, 0, TPB)
            mixed(1)

            def layer_norm(k, added, new, old):
                for b in range(B):
                    dve.wait_ge(s[added], b + 1)
                    flat = "p j c -> p (j c)"
                    link(v.tensor_tensor(new[:, b].rearrange(flat), work(b, 1), old[:, b].rearrange(flat), ALU.add))
                    for j in range(TPB):
                        ins = v.bn_stats(stats[:, b * TPB + j, :], new[:, b, j, :])
                    link(ins)
                    for j in range(TPB):
                        ins = v.bn_aggr(mv[:, b * TPB + j, :], stats[:, b * TPB + j, :])
                    link(ins)
                    v.tensor_scalar(veps1[:, b * TPB:(b + 1) * TPB], mv[:, b * TPB:(b + 1) * TPB, 1], LN_EPS, None,
                                    ALU.add).then_inc(s["ln_e"], 1)
                for b in range(B):
                    dve.wait_ge(s["ln_r"], 2 * k + b + 1)
                    for j in range(TPB):
                        t = b * TPB + j
                        v.tensor_scalar(xn[:, t, :], new[:, b, j, :], mv[:, t, 0:1], rstd1[:, t:t + 1],
                                        ALU.subtract, ALU.mult).then_inc(s["ln_n"], 1)

            dve.wait_ge(s["xb_s"], B)
            dve.wait_ge(s["o_ready"], B)
            layer_norm(0, "pr_ps", x1, xb[:, :, :].rearrange("p (b j) c -> p b j c", b=B))
            for it in range(ITERS):
                for b in range(B):
                    dve.wait_ge(s["rn_s"], 2 * it + b + 1)
                    dve.wait_ge(s["ms_ps"], 2 * it + b + 1)
                    v.tensor_tensor(sct[:, b], work(b, 1)[:, 0:TPB * WIDE].rearrange("p (j m) -> p j m", m=WIDE)[:, :, b * M:(b + 1) * M],
                                    rn[:, b, :].rearrange("p (j o) -> p j o", o=1).to_broadcast([P, TPB, M]),
                                    ALU.mult).then_inc(s["sct_s"], 1)
                for b in range(B):
                    dve.wait_ge(s["sc_t"], 2 * it + b + 1)
                    link(v.reduce_max(smax[:, b:b + 1], work(b, 0)[0:M, :], AX.X))
                    v.tensor_scalar(snm[:, b:b + 1], smax[:, b:b + 1], -SCALE, None, ALU.mult).then_inc(s["snm_s"], 1)
                for b in range(B):
                    dve.wait_ge(s["ex_s"], 2 * it + b + 1)
                    v.reciprocal(srec[:, b:b + 1], ssum[:, b:b + 1]).then_inc(s["srec_s"], 1)
                    dve.wait_ge(s["srec_s"], 2 * it + b + 1)
                    v.tensor_scalar(gvs[:, b, :], gv[:, b, :], srec[:, b:b + 1], None, ALU.mult).then_inc(s["gvs_s"], 1)
                for b in range(B):
                    dve.wait_ge(s["den_ps"], 2 * it + b + 1)
                    link(v.tensor_scalar(dde[:, b, :], work(b, 1)[:, 0:TPB * WIDE:WIDE], RMS_EPS, None, ALU.add))
                    v.reciprocal(drc[:, b, :], dde[:, b, :]).then_inc(s["drc_s"], 1)
                for b in range(B):
                    dve.wait_ge(s["rb_ps"], 2 * it + b + 1)
                    dve.wait_ge(s["gvs_s"], 2 * it + b + 1)
                    v.tensor_tensor(at[:, b, :], ex[:, b, :], work(b, 1)[0:M, :], ALU.mult).then_inc(s["at_s"], 1)
                for b in range(B):
                    dve.wait_ge(s["rt_s"], 2 * it + b + 1)
                    dve.wait_ge(s["hw_s"], 2 * it + b + 1)
                    link(v.scalar_tensor_tensor(out=t1[:, b, :], in0=rt[:, b, :], scalar=1.0, in1=hw[:, b, :],
                                                op0=ALU.add, op1=ALU.mult))
                    dve.wait_ge(s["g_ps"], 3 * (2 * it + b) + 2)
                    v.tensor_tensor(t2[:, b, :], t1[:, b, :], work(b, 1), ALU.add).then_inc(s["t2_s"], 1)
                    dve.wait_ge(s["zt_s"], 2 * it + b + 1)
                    v.scalar_tensor_tensor(out=zh[:, b, :], in0=zt[:, b, :], scalar=1.0, in1=slots[:, b, :],
                                           op0=ALU.add, op1=ALU.mult)
                    link(v.tensor_scalar(omz[:, b, :], zt[:, b, :], -0.5, 0.5, ALU.mult, ALU.add))
                    dve.wait_ge(s["n_s"], 2 * it + b + 1)
                    link(v.tensor_tensor(nz[:, b, :], omz[:, b, :], nn[:, b, :], ALU.mult))
                    v.scalar_tensor_tensor(out=slots[:, b, :], in0=zh[:, b, :], scalar=0.5, in1=nz[:, b, :],
                                           op0=ALU.mult, op1=ALU.add).then_inc(s["slot_s"], 1)
            layer_norm(1, "so_ps", acc, x1)

            def squares(b):
                for c in range(4):
                    dve.wait_ge(s["gh_s"], 4 * b + c + 1)
                    v.tensor_tensor(sqg[b][:, c, :], gh[b][:, c, :], gh[b][:, c, :], ALU.mult).then_inc(s["sqg_s"], 1)

            def scores_read(b):
                dve.wait_ge(s["sc_ps"], b + 1)
                v.tensor_copy(s2[:, b], bank[2 + b][:, 0:TPB * WIDE].rearrange("p (j e) -> p j e", e=WIDE)[:, :, 0:EXPERTS]
                              ).then_inc(s["s2_s"], 1)

            def ranks(b):
                dve.wait_ge(s["sr_s"], b + 1)
                for j in range(TPB):
                    ins = v.max(m8[:, b, j, :], sr[:, b, j, :])
                link(ins)
                for j in range(TPB):
                    v.max_index(ix[:, b, j, :], m8[:, b, j, :], sr[:, b, j, :])
                link(v.tensor_tensor(sdif[:, b, :], m8[:, b, :, 1], m8[:, b, :, 0], ALU.subtract))
                dve.sem_inc(s["sd_s"], 1)
                link(v.tensor_copy(ixf[:, b, :, :], ix[:, b, :, 0:2]))

            def weights(b):
                dve.wait_ge(s["se_s"], b + 1)
                link(v.tensor_scalar(spl[:, b, :], sexp[:, b, :], 1.0, None, ALU.add))
                link(v.reciprocal(srecp[:, b, :], spl[:, b, :]))
                link(v.tensor_scalar(w12[:, b, 0, :], srecp[:, b, :], 0.5, None, ALU.mult))
                link(v.tensor_tensor(w12[:, b, 1, :], w12[:, b, 0, :], sexp[:, b, :], ALU.mult))
                for i in range(2):
                    ins = v.tensor_tensor(eq[:, b, i], iota8[:, :].rearrange("p (o e) -> p o e", o=1).to_broadcast([P, TPB, EXPERTS]),
                                          ixf[:, b, :, i:i + 1].to_broadcast([P, TPB, EXPERTS]), ALU.is_equal)
                link(ins)
                for i in range(2):
                    ins = v.tensor_tensor(ew[:, b, i], eq[:, b, i],
                                          w12[:, b, i, :].rearrange("p (j o) -> p j o", o=1).to_broadcast([P, TPB, EXPERTS]), ALU.mult)
                link(ins)
                link(v.tensor_tensor(wfull[:, b], ew[:, b, 0], ew[:, b, 1], ALU.add))

            def add_expert(k):
                b, e = k // EXPERTS, k % EXPERTS
                dve.wait_ge(s["y_ps"], k + 1)
                if e:
                    dve.wait_ge(s["acc_s"], k)
                for j in range(TPB):
                    ins = v.scalar_tensor_tensor(out=acc[:, b, j, :], in0=bank[2 + k % 2][:, j * P:(j + 1) * P],
                                                 scalar=wfull[:, b, j, e:e + 1], in1=acc[:, b, j, :],
                                                 op0=ALU.mult, op1=ALU.add)
                ins.then_inc(s["acc_s"], 1)

            def silu_times_up(k):
                for f in range(2):
                    dve.wait_ge(s["th_s"], 2 * k + f + 1)
                    if k >= 2:
                        dve.wait_ge(s["y_ps"], k - 1)
                    link(v.scalar_tensor_tensor(out=a1[f][:, :], in0=th[f][:, :], scalar=1.0, in1=ob(f),
                                                op0=ALU.add, op1=ALU.mult))
                    v.tensor_tensor(a2[2 * (k % 2) + f], a1[f][:, :], ob(2 + f), ALU.mult).then_inc(s["a2_s"], 1)

            squares(0)
            silu_times_up(0)
            squares(1)
            scores_read(0)
            silu_times_up(1)
            scores_read(1)
            for k in range(2, B * EXPERTS):
                silu_times_up(k)
                if k in RANKED:
                    b = RANKED.index(k)
                    ranks(b)
                    weights(b)
                if k == RANKED[0]:
                    for e in range(k - 1):
                        add_expert(e)
                if k >= RANKED[0]:
                    add_expert(k - 1)
            add_expert(B * EXPERTS - 1)


_INS = ["x", "ctx_1024", "L0_attn_Wqkv", "L0_attn_bqkv", "L0_attn_q_gamma", "L0_attn_q_beta", "L0_attn_k_gamma",
        "L0_attn_k_beta", "L0_attn_alpha", "L0_attn_Wproj", "L0_attn_bproj", "L0_xattn_Wq", "L0_xattn_Wk",
        "L0_xattn_Wv", "L0_xattn_gru_wih", "L0_xattn_gru_whh", "L0_xattn_gru_bih", "L0_xattn_gru_bhh",
        "L0_xattn_slot_norm_w", "L0_xattn_input_norm_w", "L0_ffn_W_A", "L0_ffn_W_B", "L0_ffn_W_up", "L0_ffn_W_down"]
_OUTS = [((2, 512, 128), "float32")]


def kernel(**inputs):
    import numpy as _np
    import concourse.bacc as _bacc
    from concourse import mybir as _mybir
    from concourse.bass_utils import run_bass_kernel_spmd as _run

    nc = _bacc.Bacc("TRN2", target_bir_lowering=False, num_devices=1)
    arrays, args = {}, []
    for name in _INS:
        a = _np.ascontiguousarray(inputs[name])
        arrays[f"in_{name}_dram"] = a
        args.append(nc.dram_tensor(f"in_{name}_dram", a.shape, _mybir.dt.from_np(a.dtype), kind="ExternalInput").ap())
    for i, (shape, dtype) in enumerate(_OUTS):
        dt = _mybir.dt.from_np(_np.dtype(dtype))
        args.append(nc.dram_tensor(f"out_{i}_dram", shape, dt, kind="ExternalOutput").ap())
    build(nc, *args)
    r = _run(nc, [arrays], core_ids=[0])
    got = tuple(r.results[0][f"out_{i}_dram"] for i in range(len(_OUTS)))
    return got[0]
```
